# Optimizing a Trainium2 kernel written in Bass

```python
import numpy as np
import jax
import jax.numpy as jnp

def _softmax(x, axis=-1):
    return jax.nn.softmax(x, axis=axis)

def _gelu(x):
    return jax.nn.gelu(x, approximate=True)

def _silu(x):
    return jax.nn.silu(x)

def _sigmoid(x):
    return jax.nn.sigmoid(x)

def _layernorm(x, axis=-1, eps=1e-05):
    m = jnp.mean(x, axis=axis, keepdims=True)
    v = jnp.var(x, axis=axis, keepdims=True)
    return (x - m) / jnp.sqrt(v + eps)

def _scatter_add(tgt, idx, src, axis=0):
    return tgt.at[idx].add(src)

def _segment_sum(src, seg, n):
    return jax.ops.segment_sum(src, seg, n)
kernel_name = 'mk_prb_d2_jaxref_r4_862a79'

def setup_inputs(seed: int=0):
    np.random.seed(seed)
    _w = jnp.asarray

    def _L0_attn_setup():
        import jax, jax.numpy as jnp
        import numpy as np
        B, S, E = (4, 512, 256)
        H, KVH = (16, 4)
        D = E // H
        QL, KVL = (64, 32)
        ROPE_BASE = 10000.0

        def _rope(x):
            d = x.shape[-1]
            inv_freq = 1.0 / ROPE_BASE ** (jnp.arange(0, d, 2, dtype=jnp.float32) / d)
            t = jnp.arange(x.shape[1], dtype=jnp.float32)
            freqs = jnp.outer(t, inv_freq)
            cos = jnp.cos(freqs)[None, :, None, :].astype(x.dtype)
            sin = jnp.sin(freqs)[None, :, None, :].astype(x.dtype)
            x1, x2 = (x[..., ::2], x[..., 1::2])
            r1 = x1 * cos - x2 * sin
            r2 = x1 * sin + x2 * cos
            return jnp.stack([r1, r2], axis=-1).reshape(x.shape)
        key = jax.random.key(seed)
        ks = jax.random.split(key, 7)
        s = 0.02
        return {'x': jax.random.normal(ks[0], (B, S, E), dtype=jnp.float32), 'Wqa': jax.random.normal(ks[1], (E, QL), dtype=jnp.float32) * s, 'Wqb': jax.random.normal(ks[2], (QL, E), dtype=jnp.float32) * s, 'Wkva': jax.random.normal(ks[3], (E, KVL), dtype=jnp.float32) * s, 'Wkvb': jax.random.normal(ks[4], (KVL, KVH * D * 2), dtype=jnp.float32) * s, 'Wout': jax.random.normal(ks[5], (E, E), dtype=jnp.float32) * s, 'bout': jax.random.normal(ks[6], (E,), dtype=jnp.float32) * s}
    _L0_attn_in = _L0_attn_setup()

    def _L0_ffn_setup():
        import math
        import jax, jax.numpy as jnp
        import numpy as np
        B, T, H = (4, 512, 256)
        E, K, F = (8, 2, 512)
        CAP_FACTOR = 1.25

        def _moe_forward(x, Wg, W_in, W_out):
            b, t, h = x.shape
            xf = x.reshape(-1, h)
            S = xf.shape[0]
            C = int(math.ceil(K * S / E * CAP_FACTOR))
            logits = xf @ Wg
            probs = jax.nn.softmax(logits, axis=-1)
            top_vals, top_idx = jax.lax.top_k(probs, K)
            flat_idx = top_idx.T.reshape(-1)
            onehot = jax.nn.one_hot(flat_idx, E, dtype=jnp.int32)
            cum = jnp.cumsum(onehot, axis=0) - 1
            loc = jnp.take_along_axis(cum, flat_idx[:, None], axis=1)[:, 0]
            loc = loc.reshape(K, S).T
            keep = loc < C
            gates = top_vals * keep.astype(top_vals.dtype)
            denom = jnp.maximum(gates.sum(-1, keepdims=True), 1e-09)
            gates = gates / denom
            loc_c = jnp.where(keep, loc, C)
            e_flat = top_idx.reshape(-1)
            l_flat = loc_c.reshape(-1)
            xk = jnp.broadcast_to(xf[:, None, :], (S, K, h)).reshape(-1, h)
            xk = jnp.where(keep.reshape(-1, 1), xk, 0.0)
            buf = jnp.zeros((E, C + 1, h), x.dtype).at[e_flat, l_flat].set(xk)
            inp = buf[:, :C]
            hid = jnp.einsum('ech,ehf->ecf', inp, W_in)
            a, g = jnp.split(hid, 2, axis=-1)
            hid = jax.nn.gelu(a, approximate=False) * g
            out_e = jnp.einsum('ecf,efh->ech', hid, W_out)
            out_pad = jnp.concatenate([out_e, jnp.zeros((E, 1, h), out_e.dtype)], axis=1)
            gathered = out_pad[e_flat, l_flat].reshape(S, K, h)
            y = (gathered * gates[..., None]).sum(axis=1)
            return y.reshape(b, t, h)
        key = jax.random.key(seed)
        k1, k2, k3, k4 = jax.random.split(key, 4)
        x = jax.random.normal(k1, (B, T, H), dtype=jnp.float32)
        Wg = jax.random.normal(k2, (H, E), dtype=jnp.float32) * 0.02
        W_in = jax.random.normal(k3, (E, H, 2 * F), dtype=jnp.float32) * (1.0 / math.sqrt(H))
        W_out = jax.random.normal(k4, (E, F, H), dtype=jnp.float32) * (1.0 / math.sqrt(F))
        return {'x': x, 'Wg': Wg, 'W_in': W_in, 'W_out': W_out}
    _L0_ffn_in = _L0_ffn_setup()

    def _L1_attn_setup():
        import jax, jax.numpy as jnp
        import numpy as np
        D_MODEL = 256
        N_HEADS = 16
        NUM_PATTERN = 32
        HEAD_DIM = D_MODEL // N_HEADS

        def sparsemax(z):
            S = z.shape[-1]
            z_sorted = -jnp.sort(-z, axis=-1)
            cum = jnp.cumsum(z_sorted, axis=-1)
            k = jnp.arange(1, S + 1, dtype=z.dtype)
            support = 1.0 + k * z_sorted > cum
            k_sup = jnp.sum(support, axis=-1, keepdims=True)
            cum_sel = jnp.take_along_axis(cum, k_sup - 1, axis=-1)
            tau = (cum_sel - 1.0) / k_sup.astype(z.dtype)
            return jnp.maximum(z - tau, 0.0)
        key = jax.random.key(seed)
        ks = jax.random.split(key, 10)
        s = 1.0 / np.sqrt(D_MODEL)
        inp = {'query': jax.random.normal(ks[0], (8, 1024, D_MODEL), dtype=jnp.float32), 'key_param': jax.random.normal(ks[1], (1, NUM_PATTERN, D_MODEL), dtype=jnp.float32), 'Wq': jax.random.normal(ks[2], (D_MODEL, N_HEADS * HEAD_DIM), dtype=jnp.float32) * s, 'bq': jnp.zeros((N_HEADS * HEAD_DIM,), dtype=jnp.float32), 'Wk': jax.random.normal(ks[3], (D_MODEL, N_HEADS * HEAD_DIM), dtype=jnp.float32) * s, 'bk': jnp.zeros((N_HEADS * HEAD_DIM,), dtype=jnp.float32), 'Wv': jax.random.normal(ks[4], (N_HEADS * HEAD_DIM, N_HEADS * HEAD_DIM), dtype=jnp.float32) * s, 'bv': jnp.zeros((N_HEADS * HEAD_DIM,), dtype=jnp.float32), 'Wo': jax.random.normal(ks[5], (N_HEADS * HEAD_DIM, D_MODEL), dtype=jnp.float32) * s, 'bo': jnp.zeros((D_MODEL,), dtype=jnp.float32)}
        return inp
    _L1_attn_in = _L1_attn_setup()

    def _L1_ffn_setup():
        import jax, jax.numpy as jnp
        import numpy as np
        H = 256
        I = 128
        E = 8
        K = 2
        SI = I * 2
        B, S = (2, 256)

        def _mlp(x, gw, uw, dw):
            return jax.nn.silu(x @ gw.T) * (x @ uw.T) @ dw.T
        key = jax.random.key(seed)
        ks = jax.random.split(key, 9)
        s = 0.02
        return {'x': jax.random.normal(ks[0], (B, S, H), jnp.float32), 'gate_w': jax.random.normal(ks[1], (E, H), jnp.float32) * s, 'lb_bias': jnp.zeros((E,), jnp.float32), 'expert_gate_w': jax.random.normal(ks[2], (E, I, H), jnp.float32) * s, 'expert_up_w': jax.random.normal(ks[3], (E, I, H), jnp.float32) * s, 'expert_down_w': jax.random.normal(ks[4], (E, H, I), jnp.float32) * s, 'shared_gate_w': jax.random.normal(ks[5], (SI, H), jnp.float32) * s, 'shared_up_w': jax.random.normal(ks[6], (SI, H), jnp.float32) * s, 'shared_down_w': jax.random.normal(ks[7], (H, SI), jnp.float32) * s}
    _L1_ffn_in = _L1_ffn_setup()
    _d = {'L0_attn_x': _L0_attn_in['x'], 'L0_attn_Wqa': _L0_attn_in['Wqa'], 'L0_attn_Wqb': _L0_attn_in['Wqb'], 'L0_attn_Wkva': _L0_attn_in['Wkva'], 'L0_attn_Wkvb': _L0_attn_in['Wkvb'], 'L0_attn_Wout': _L0_attn_in['Wout'], 'L0_attn_bout': _L0_attn_in['bout'], 'L0_ffn_Wg': _L0_ffn_in['Wg'], 'L0_ffn_W_in': _L0_ffn_in['W_in'], 'L0_ffn_W_out': _L0_ffn_in['W_out'], 'L1_attn_key_param': _L1_attn_in['key_param'], 'L1_attn_Wq': _L1_attn_in['Wq'], 'L1_attn_bq': _L1_attn_in['bq'], 'L1_attn_Wk': _L1_attn_in['Wk'], 'L1_attn_bk': _L1_attn_in['bk'], 'L1_attn_Wv': _L1_attn_in['Wv'], 'L1_attn_bv': _L1_attn_in['bv'], 'L1_attn_Wo': _L1_attn_in['Wo'], 'L1_attn_bo': _L1_attn_in['bo'], 'L1_ffn_gate_w': _L1_ffn_in['gate_w'], 'L1_ffn_lb_bias': _L1_ffn_in['lb_bias'], 'L1_ffn_expert_gate_w': _L1_ffn_in['expert_gate_w'], 'L1_ffn_expert_up_w': _L1_ffn_in['expert_up_w'], 'L1_ffn_expert_down_w': _L1_ffn_in['expert_down_w'], 'L1_ffn_shared_gate_w': _L1_ffn_in['shared_gate_w'], 'L1_ffn_shared_up_w': _L1_ffn_in['shared_up_w'], 'L1_ffn_shared_down_w': _L1_ffn_in['shared_down_w']}
    _x0 = _d['L0_attn_x']
    _d['L0_attn_x'] = jax.random.normal(jax.random.fold_in(jax.random.key(seed), 1), (2, 2048, 256), dtype=_x0.dtype)
    del _x0
    return _d

def reference(L0_attn_x, L0_attn_Wqa, L0_attn_Wqb, L0_attn_Wkva, L0_attn_Wkvb, L0_attn_Wout, L0_attn_bout, L0_ffn_Wg, L0_ffn_W_in, L0_ffn_W_out, L1_attn_key_param, L1_attn_Wq, L1_attn_bq, L1_attn_Wk, L1_attn_bk, L1_attn_Wv, L1_attn_bv, L1_attn_Wo, L1_attn_bo, L1_ffn_gate_w, L1_ffn_lb_bias, L1_ffn_expert_gate_w, L1_ffn_expert_up_w, L1_ffn_expert_down_w, L1_ffn_shared_gate_w, L1_ffn_shared_up_w, L1_ffn_shared_down_w):

    def _L0_attn_ref(x, Wqa, Wqb, Wkva, Wkvb, Wout, bout):
        import jax, jax.numpy as jnp
        import numpy as np
        B, S, E = (4, 512, 256)
        H, KVH = (16, 4)
        D = E // H
        QL, KVL = (64, 32)
        ROPE_BASE = 10000.0

        def _rope(x):
            d = x.shape[-1]
            inv_freq = 1.0 / ROPE_BASE ** (jnp.arange(0, d, 2, dtype=jnp.float32) / d)
            t = jnp.arange(x.shape[1], dtype=jnp.float32)
            freqs = jnp.outer(t, inv_freq)
            cos = jnp.cos(freqs)[None, :, None, :].astype(x.dtype)
            sin = jnp.sin(freqs)[None, :, None, :].astype(x.dtype)
            x1, x2 = (x[..., ::2], x[..., 1::2])
            r1 = x1 * cos - x2 * sin
            r2 = x1 * sin + x2 * cos
            return jnp.stack([r1, r2], axis=-1).reshape(x.shape)
        b, s, _ = x.shape
        scale = D ** (-0.5)
        q = (x @ Wqa @ Wqb).reshape(b, s, H, D)
        kv = (x @ Wkva @ Wkvb).reshape(b, s, KVH, D, 2)
        k, v = (kv[..., 0], kv[..., 1])
        q = _rope(q)
        k = _rope(k)
        g = H // KVH
        k = jnp.repeat(k, g, axis=2)
        v = jnp.repeat(v, g, axis=2)
        scores = jnp.einsum('bqhd,bkhd->bhqk', q, k) * scale
        causal = jnp.triu(jnp.ones((s, s), dtype=bool), k=1)
        scores = jnp.where(causal[None, None], -jnp.inf, scores)
        w = jax.nn.softmax(scores, axis=-1)
        out = jnp.einsum('bhqk,bkhd->bqhd', w, v).reshape(b, s, E)
        return out @ Wout + bout

    def _L0_ffn_ref(x, Wg, W_in, W_out):
        import math
        import jax, jax.numpy as jnp
        import numpy as np
        B, T, H = (4, 512, 256)
        E, K, F = (8, 2, 512)
        CAP_FACTOR = 1.25

        def _moe_forward(x, Wg, W_in, W_out):
            b, t, h = x.shape
            xf = x.reshape(-1, h)
            S = xf.shape[0]
            C = int(math.ceil(K * S / E * CAP_FACTOR))
            logits = xf @ Wg
            probs = jax.nn.softmax(logits, axis=-1)
            top_vals, top_idx = jax.lax.top_k(probs, K)
            flat_idx = top_idx.T.reshape(-1)
            onehot = jax.nn.one_hot(flat_idx, E, dtype=jnp.int32)
            cum = jnp.cumsum(onehot, axis=0) - 1
            loc = jnp.take_along_axis(cum, flat_idx[:, None], axis=1)[:, 0]
            loc = loc.reshape(K, S).T
            keep = loc < C
            gates = top_vals * keep.astype(top_vals.dtype)
            denom = jnp.maximum(gates.sum(-1, keepdims=True), 1e-09)
            gates = gates / denom
            loc_c = jnp.where(keep, loc, C)
            e_flat = top_idx.reshape(-1)
            l_flat = loc_c.reshape(-1)
            xk = jnp.broadcast_to(xf[:, None, :], (S, K, h)).reshape(-1, h)
            xk = jnp.where(keep.reshape(-1, 1), xk, 0.0)
            buf = jnp.zeros((E, C + 1, h), x.dtype).at[e_flat, l_flat].set(xk)
            inp = buf[:, :C]
            hid = jnp.einsum('ech,ehf->ecf', inp, W_in)
            a, g = jnp.split(hid, 2, axis=-1)
            hid = jax.nn.gelu(a, approximate=False) * g
            out_e = jnp.einsum('ecf,efh->ech', hid, W_out)
            out_pad = jnp.concatenate([out_e, jnp.zeros((E, 1, h), out_e.dtype)], axis=1)
            gathered = out_pad[e_flat, l_flat].reshape(S, K, h)
            y = (gathered * gates[..., None]).sum(axis=1)
            return y.reshape(b, t, h)
        return _moe_forward(x, Wg, W_in, W_out)

    def _L1_attn_ref(query, key_param, Wq, bq, Wk, bk, Wv, bv, Wo, bo):
        import jax, jax.numpy as jnp
        import numpy as np
        D_MODEL = 256
        N_HEADS = 16
        NUM_PATTERN = 32
        HEAD_DIM = D_MODEL // N_HEADS

        def sparsemax(z):
            S = z.shape[-1]
            z_sorted = -jnp.sort(-z, axis=-1)
            cum = jnp.cumsum(z_sorted, axis=-1)
            k = jnp.arange(1, S + 1, dtype=z.dtype)
            support = 1.0 + k * z_sorted > cum
            k_sup = jnp.sum(support, axis=-1, keepdims=True)
            cum_sel = jnp.take_along_axis(cum, k_sup - 1, axis=-1)
            tau = (cum_sel - 1.0) / k_sup.astype(z.dtype)
            return jnp.maximum(z - tau, 0.0)
        B, L, _ = query.shape
        S = key_param.shape[1]
        H, E = (N_HEADS, HEAD_DIM)
        D = HEAD_DIM
        k = jnp.broadcast_to(key_param, (B, S, D_MODEL))
        queries = (query @ Wq + bq).reshape(B, L, H, E)
        keys_flat = k @ Wk + bk
        values = (keys_flat @ Wv + bv).reshape(B, S, H, D)
        keys = keys_flat.reshape(B, S, H, E)
        scale = 1.0 / np.sqrt(E)
        scores = jnp.einsum('blhe,bshe->bhls', queries, keys)
        A = sparsemax(scale * scores)
        out = jnp.einsum('bhls,bshd->blhd', A, values)
        out = jnp.transpose(out, (0, 2, 1, 3)).reshape(B, L, H * D)
        return out @ Wo + bo

    def _L1_ffn_ref(x, gate_w, lb_bias, expert_gate_w, expert_up_w, expert_down_w, shared_gate_w, shared_up_w, shared_down_w):
        import jax, jax.numpy as jnp
        import numpy as np
        H = 256
        I = 128
        E = 8
        K = 2
        SI = I * 2
        B, S = (2, 256)

        def _mlp(x, gw, uw, dw):
            return jax.nn.silu(x @ gw.T) * (x @ uw.T) @ dw.T
        b, s, h = x.shape
        xf = x.reshape(-1, h)
        logits = xf @ gate_w.T + lb_bias
        scores = jax.nn.sigmoid(logits.astype(jnp.float32))
        topw, topi = jax.lax.top_k(scores, K)
        topw = (topw / (topw.sum(-1, keepdims=True) + 1e-08)).astype(x.dtype)
        out = jnp.zeros_like(xf)
        for e in range(E):
            m = topi == e
            sel = m.any(axis=-1)
            cnt = m.sum()
            wmean = (topw * m).sum() / jnp.maximum(cnt, 1).astype(topw.dtype)
            y = _mlp(xf, expert_gate_w[e], expert_up_w[e], expert_down_w[e])
            out = out + jnp.where(sel[:, None], y * wmean, jnp.zeros((), x.dtype))
        out = out.reshape(b, s, h)
        out = out + _mlp(x, shared_gate_w, shared_up_w, shared_down_w)
        return out
    x = L0_attn_x
    xn = _layernorm(x, axis=-1)
    x = x + _L0_attn_ref(xn, L0_attn_Wqa, L0_attn_Wqb, L0_attn_Wkva, L0_attn_Wkvb, L0_attn_Wout, L0_attn_bout) + _L0_ffn_ref(xn, L0_ffn_Wg, L0_ffn_W_in, L0_ffn_W_out)
    xn = _layernorm(x, axis=-1)
    x = x + _L1_attn_ref(xn, L1_attn_key_param, L1_attn_Wq, L1_attn_bq, L1_attn_Wk, L1_attn_bk, L1_attn_Wv, L1_attn_bv, L1_attn_Wo, L1_attn_bo) + _L1_ffn_ref(xn, L1_ffn_gate_w, L1_ffn_lb_bias, L1_ffn_expert_gate_w, L1_ffn_expert_up_w, L1_ffn_expert_down_w, L1_ffn_shared_gate_w, L1_ffn_shared_up_w, L1_ffn_shared_down_w)
    return x

_drawn_inputs = setup_inputs


def setup_inputs(seed=0):
    import zlib

    import numpy as np

    out = dict(_drawn_inputs(seed))
    spreads = {'L1_attn_bq': (0.0, 0.462),
     'L1_attn_bk': (0.0, 0.724),
     'L1_attn_bv': (0.0, 0.654),
     'L1_attn_bo': (0.0, 0.698),
     'L1_ffn_lb_bias': (0.0, 0.8)}
    factors = {'L0_attn_Wqa': 8.0,
     'L0_attn_Wqb': 8.0,
     'L0_attn_Wkva': 8.0,
     'L0_attn_Wkvb': 8.0,
     'L0_attn_Wout': 8.0,
     'L1_ffn_gate_w': 8.0,
     'L1_ffn_expert_gate_w': 8.0,
     'L1_ffn_expert_up_w': 8.0,
     'L1_ffn_expert_down_w': 8.0,
     'L1_ffn_shared_gate_w': 4.58,
     'L1_ffn_shared_up_w': 4.536,
     'L1_ffn_shared_down_w': 4.548}
    for name, (base, spread) in spreads.items():
        noise = np.random.default_rng([zlib.crc32(name.encode()), seed]).standard_normal(out[name].shape)
        drawn = base * np.exp(spread * noise) if base else spread * noise
        out[name] = jnp.asarray(drawn.astype(out[name].dtype))
    for name, factor in factors.items():
        out[name] = (out[name] * factor).astype(out[name].dtype)
    return out
```

```python
from contextlib import ExitStack

import concourse.bass as bass
from concourse import mybir

F32 = mybir.dt.float32
BF16 = mybir.dt.bfloat16
U32 = mybir.dt.uint32
ALU = mybir.AluOpType
ACT = mybir.ActivationFunctionType
AX = mybir.AxisListType

P = 128
B, S, E = 2, 2048, 256
NT = B * S
TILES = NT // P
EC = E // P
CH = 512
NCH = NT // CH
TPC = CH // P
H, KVH, D = 16, 4, 16
QL, KVL = 64, 32
NX, TOPK, F = 8, 2, 512
CAP = -(-TOPK * NT * 5 // (NX * 4))
SLOTS = NX * CAP
NPAT = 32
I1, SI = 128, 256
LN_EPS = 1e-5
LAT = QL + KVL
COMB = LAT + NX
NEG = -1.0e30
PARTS = 3
VW = 32
RUNS = ((0, 3), (3, 2), (5, 1))
STACK = 6 * D
NQ = S // CH
QT = S // P
HEADS = B * H



class Steps:

    def __init__(self, eng, sem):
        self.eng, self.sem, self.n = eng, sem, 0

    def did(self, ins):
        ins.then_inc(self.sem, 1)
        self.n += 1

    def all_done(self):
        self.eng.wait_ge(self.sem, self.n)


def latents(nc, d, s):
    with ExitStack() as ctx:
        def sb(name, shape, dt=F32):
            return ctx.enter_context(nc.sbuf_tensor(name, shape, dt))

        def pb(name, shape, dt=F32):
            return ctx.enter_context(nc.psum_tensor(name, shape, dt))

        def sem(name):
            return ctx.enter_context(nc.semaphore("lat_" + name))

        ident = s["ident"]
        logits = s["logits"]
        wcomb = sb("wcomb", [P, EC, COMB])
        wqb = sb("wqb", [QL, H * D])
        wqb_swap = sb("wqb_swap", [QL, H * D])
        wkvb = sb("wkvb", [LAT, KVH * D, 2])
        wk = sb("wk", [LAT, KVH * D])
        wk_swap = sb("wk_swap", [LAT, KVH * D])
        wv = sb("wv", [LAT, KVH * D])
        cos = sb("cos", [P, NT])
        sin = sb("sin", [P, NT])
        x = [sb(f"x{u}", [P, TPC, E]) for u in range(2)]
        stats = sb("stats", [P, TPC, 6])
        carrier = sb("carrier", [P, 1])
        mean_var = sb("mean_var", [P, TPC, 2])
        var_eps = sb("var_eps", [P, TPC])
        std = sb("std", [P, TPC])
        rstd = sb("rstd", [P, TPC])
        xn = [sb(f"xn{u}", [P, TPC, E]) for u in range(2)]
        xnT = [sb(f"xnT{u}", [P, EC, CH]) for u in range(2)]
        comb = [sb(f"comb{u}", [COMB, CH]) for u in range(2)]
        by_cos = [sb(f"by_cos{m}", [P, CH]) for m in range(2)]
        by_sin = [sb(f"by_sin{m}", [P, CH]) for m in range(2)]
        rot = [sb(f"rot{m}", [P, CH]) for m in range(2)]
        rest = [sb(f"rest{m}", [P, CH]) for m in range(2)]
        parts = [sb(f"parts{m}", [P, PARTS, CH], BF16) for m in range(2)]
        vtok = [sb(f"vtok{u}", [P, KVH, TPC, VW]) for u in range(2)]

        zeros = sb("zeros", [P, 8 * E])

        pT = pb("pT", [P, EC, CH])
        pC = pb("pC", [COMB, CH])
        pR = [pb(f"pR{m}", [P, 2, CH]) for m in range(2)]
        pM = pb("pM", [P, 512])
        pV = pM[:, 0:TPC * KVH * D].rearrange("p (t n) -> p t n", t=TPC)
        pL = pT[:, 0, 0:TPC * NX].rearrange("p (t n) -> p t n", t=TPC)

        weights_in = sem("weights_in")
        swapped = sem("swapped")
        x_in = [sem(f"x_in{u}") for u in range(2)]
        stats_ready = sem("stats_ready")
        var_ready = sem("var_ready")
        std_ready = sem("std_ready")
        rstd_ready = sem("rstd_ready")
        xn_ready = sem("xn_ready")
        xn_out = [sem(f"xn_out{u}") for u in range(2)]
        xnT_made = sem("xnT_made")
        xnT_ready = sem("xnT_ready")
        comb_made = sem("comb_made")
        comb_ready = sem("comb_ready")
        vl_made = sem("vl_made")
        vl_ready = sem("vl_ready")
        v_filled = sem("v_filled")
        zeros_ready = sem("zeros_ready")
        buf_blank = sem("buf_blank")
        v_out = [sem(f"v_out{u}") for u in range(2)]
        pair_made = sem("pair_made")
        pair_used = sem("pair_used")
        rot_ready = sem("rot_ready")
        high_ready = sem("high_ready")
        low_ready = sem("low_ready")
        parts_out = [sem(f"parts_out{m}") for m in range(2)]

        PAIRS = 3
        ROUNDS = NCH // 2
        x_rows = d["x"].rearrange("b (c t p) e -> (b c) p t e", t=TPC, p=P)
        xn_rows = d["xn"].rearrange("(c t p) e -> c p t e", t=TPC, p=P)

        def one(ap, c):
            return ap[bass.ds(c, 1)].rearrange("o p t e -> (o p) t e")

        block = ctx.enter_context(nc.Block())

        @block.sync
        def _(sp):
            for dst, src in (
                (wcomb[:, :, 0:QL], d["Wqa"].rearrange("(k p) n -> p k n", p=P)),
                (wcomb[:, :, QL:LAT], d["Wkva"].rearrange("(k p) n -> p k n", p=P)),
                (wcomb[:, :, LAT:COMB], d["Wg"].rearrange("(k p) n -> p k n", p=P)),
                (wqb[:], d["Wqb"]),
                (wkvb[QL:LAT], d["Wkvb"].rearrange("k (n two) -> k n two", two=2)),
                (cos[:, 0:S], d["c_cos"]), (cos[:, S:NT], d["c_cos"]),
                (sin[:, 0:S], d["c_sin"]), (sin[:, S:NT], d["c_sin"]),
                (ident[:], d["c_ident"]),
            ):
                sp.dma_start(dst, src).then_inc(weights_in, 16)
            for u in range(2):
                sp.dma_start(x[u][:], x_rows[u]).then_inc(x_in[u], 16)
                sp.sem_inc(xn_out[u], 16)
                sp.sem_inc(v_out[u], 16)
                sp.sem_inc(parts_out[u], 16)

            def stores(j, more):
                for u in range(2):
                    c = 2 * j + u
                    sp.wait_ge(xn_ready, 4 * c + 4)
                    if more:
                        sp.dma_start(x[u][:], one(x_rows, c + 2)).then_inc(x_in[u], 16)
                    sp.dma_start(one(xn_rows, c), xn[u][:]).then_inc(xn_out[u], 16)
                    sp.wait_ge(vl_ready, 2 * c + 4)
                    sp.dma_start(d["v"][bass.ds(c, 1)].rearrange("o h p n -> p (o h) n"),
                                 vtok[u][:].rearrange("p h t n -> p h (t n)")).then_inc(v_out[u], 16)
                    for k in range(PAIRS):
                        n, m = PAIRS * c + k, (PAIRS * u + k) % 2
                        sp.wait_ge(low_ready, 2 * n + 2)
                        rows = P if k < 2 else KVH * D
                        dst = d["q_parts"][:, k * P:(k + 1) * P] if k < 2 else d["k_parts"]
                        sp.dma_start(dst[:, :, bass.ds(c * CH, CH)].rearrange("a p n -> p a n"),
                                     parts[m][0:rows]).then_inc(parts_out[m], 16)

            with sp.Fori(0, ROUNDS - 1) as j:
                stores(j, True)
            stores(ROUNDS - 1, False)
            for u in range(2):
                sp.wait_ge(xn_out[u], 16 * (ROUNDS + 1))
                sp.wait_ge(v_out[u], 16 * (ROUNDS + 1))
                sp.wait_ge(parts_out[u], 16 * (PAIRS * ROUNDS + 1))

        @block.gpsimd
        def _(pool):
            pool.memset(zeros[:], 0.0).then_inc(zeros_ready, 1)
            pool.wait_ge(zeros_ready, 1)
            blank = d["buf"].rearrange("(a p r) e -> a p (r e)", p=P, r=8)
            for a in range(SLOTS // P // 8):
                pool.dma_start(blank[a], zeros[:]).then_inc(buf_blank, 16)
            pool.wait_ge(buf_blank, 16 * (SLOTS // P // 8))

        @block.scalar
        def _(act):
            act.wait_ge(weights_in, 16 * 10)
            q_pair = wqb[:].rearrange("k (n two) -> k n two", two=2)
            q_swap = wqb_swap[:].rearrange("k (n two) -> k n two", two=2)
            k_pair = wkvb[QL:LAT, :, 0].rearrange("k (n two) -> k n two", two=2)
            k_swap = wk_swap[QL:LAT].rearrange("k (n two) -> k n two", two=2)
            for dst, src in (
                (q_swap[:, :, 0], q_pair[:, :, 1]), (q_swap[:, :, 1], q_pair[:, :, 0]),
                (k_swap[:, :, 0], k_pair[:, :, 1]), (k_swap[:, :, 1], k_pair[:, :, 0]),
                (wk[QL:LAT], wkvb[QL:LAT, :, 0]), (wv[QL:LAT], wkvb[QL:LAT, :, 1]),
            ):
                act.copy(dst, src).then_inc(swapped, 1)
            with act.Fori(0, ROUNDS) as j:
                for u in range(2):
                    c = 2 * j + u
                    act.wait_ge(var_ready, 5 * c + 5)
                    act.activation(std[:], var_eps[:], ACT.Sqrt).then_inc(std_ready, 1)
                    act.wait_ge(xnT_made, c + 1)
                    act.copy(xnT[u][:, 0], pT[:, 0]).then_inc(xnT_ready, 1)
                    act.copy(xnT[u][:, 1], pT[:, 1]).then_inc(xnT_ready, 1)
                    act.wait_ge(comb_made, c + 1)
                    act.copy(comb[u][:], pC[:]).then_inc(comb_ready, 1)
                    for k in range(PAIRS):
                        n, m = PAIRS * c + k, (PAIRS * u + k) % 2
                        rows = P if k < 2 else KVH * D
                        act.wait_ge(rot_ready, n + 1)
                        act.wait_ge(parts_out[m], 16 * (3 * j + (PAIRS * u + k) // 2 + 1))
                        act.copy(parts[m][0:rows, 0], rot[m][0:rows]).then_inc(high_ready, 1)
                        act.wait_ge(low_ready, 2 * n + 1)
                        act.copy(parts[m][0:rows, 1], rest[m][0:rows]).then_inc(high_ready, 1)

        @block.tensor
        def _(pe):
            pe.sem_inc(xnT_ready, 2)
            pe.sem_inc(comb_ready, 1)
            pe.sem_inc(vl_ready, 2)
            pe.sem_inc(pair_used, 4)
            pe.wait_ge(weights_in, 16 * 10)
            pe.wait_ge(swapped, 6)
            with pe.Fori(0, ROUNDS) as j:
                for u in range(2):
                    c = 2 * j + u
                    pe.wait_ge(xn_ready, 4 * c + 4)
                    pe.wait_ge(xnT_ready, 2 * c + 2)
                    pe.wait_ge(vl_ready, 2 * c + 2)
                    for t in range(TPC):
                        for k in range(EC):
                            ins = pe.transpose(pT[:, k, t * P:(t + 1) * P], xn[u][:, t, k * P:(k + 1) * P], ident[:])
                    ins.then_inc(xnT_made, 1)
                    pe.wait_ge(xnT_ready, 2 * c + 4)
                    pe.wait_ge(comb_ready, c + 1)
                    for k in range(EC):
                        ins = pe.matmul(pC[:], wcomb[:, k, :], xnT[u][:, k, :], start=(k == 0), stop=(k == EC - 1))
                    ins.then_inc(comb_made, 1)
                    pe.wait_ge(comb_ready, c + 2)
                    for k in range(PAIRS):
                        n, m = PAIRS * c + k, (PAIRS * u + k) % 2
                        pe.wait_ge(pair_used, 2 * n + 2)
                        for a in range(2):
                            w = (wqb, wqb_swap)[a][:, k * P:(k + 1) * P] if k < 2 else (wk, wk_swap)[a][QL:LAT]
                            rows = slice(0, QL) if k < 2 else slice(QL, LAT)
                            dst = pR[m][0:P if k < 2 else KVH * D, a]
                            ins = pe.matmul(dst, w, comb[u][rows, :], start=True, stop=True)
                        ins.then_inc(pair_made, 1)
                        if k == 0:
                            for t in range(TPC):
                                cols = slice(t * P, (t + 1) * P)
                                pe.matmul(pV[:, t, :], comb[u][QL:LAT, cols], wv[QL:LAT, :], start=True, stop=True)
                                ins = pe.transpose(pL[:, t, :], comb[u][LAT:COMB, cols], ident[LAT:COMB, LAT:COMB])
                            ins.then_inc(vl_made, 1)

        @block.vector
        def _(dve):
            for u in range(2):
                dve.memset(vtok[u][:], 0.0).then_inc(v_filled, 1)
                dve.wait_ge(v_filled, 2 * u + 1)
                dve.memset(vtok[u][:, :, :, D:D + 1], 1.0).then_inc(v_filled, 1)
            dve.wait_ge(v_filled, 4)
            dve.wait_ge(weights_in, 16 * 10)
            with dve.Fori(0, ROUNDS) as j:
                for u in range(2):
                    c = 2 * j + u
                    dve.wait_ge(x_in[u], 16 * j + 16)
                    for t in range(TPC):
                        dve.bn_stats(stats[:, t], x[u][:, t]).then_inc(stats_ready, 1)
                    dve.wait_ge(stats_ready, 4 * c + 4)
                    dve.memset(carrier[:], 0.0)
                    for t in range(TPC):
                        dve.bn_aggr(mean_var[:, t], stats[:, t]).then_inc(var_ready, 1)
                    dve.wait_ge(var_ready, 5 * c + 4)
                    dve.tensor_scalar(var_eps[:], mean_var[:, :, 1], LN_EPS, None, ALU.add).then_inc(var_ready, 1)
                    dve.wait_ge(std_ready, c + 1)
                    dve.reciprocal(rstd[:], std[:]).then_inc(rstd_ready, 1)
                    dve.wait_ge(rstd_ready, c + 1)
                    dve.wait_ge(xn_out[u], 16 * j + 16)
                    for t in range(TPC):
                        dve.tensor_scalar(xn[u][:, t], x[u][:, t], mean_var[:, t, 0:1], rstd[:, t:t + 1],
                                          ALU.subtract, ALU.mult).then_inc(xn_ready, 1)
                    for k in range(PAIRS):
                        n, m = PAIRS * c + k, (PAIRS * u + k) % 2
                        rows = P if k < 2 else KVH * D
                        at = bass.ds(c * CH, CH)
                        dve.wait_ge(pair_made, n + 1)
                        dve.tensor_tensor(by_cos[m][0:rows], pR[m][0:rows, 0], cos[0:rows, at],
                                          ALU.mult).then_inc(pair_used, 1)
                        dve.tensor_tensor(by_sin[m][0:rows], pR[m][0:rows, 1], sin[0:rows, at],
                                          ALU.mult).then_inc(pair_used, 1)
                        dve.wait_ge(pair_used, 2 * n + 6)
                        dve.tensor_tensor(rot[m][0:rows], by_cos[m][0:rows], by_sin[m][0:rows],
                                          ALU.add).then_inc(rot_ready, 1)
                        if k == 0:
                            dve.wait_ge(vl_made, c + 1)
                            dve.wait_ge(v_out[u], 16 * j + 16)
                            dve.tensor_copy(vtok[u][:, :, :, 0:D],
                                            pV.rearrange("p t (h n) -> p h t n", h=KVH)).then_inc(vl_ready, 1)
                            dve.tensor_copy(logits[:, bass.ds(c * TPC, TPC), :], pL).then_inc(vl_ready, 1)
                        dve.wait_ge(high_ready, 2 * n + 1)
                        dve.tensor_tensor(rest[m][0:rows], rot[m][0:rows], parts[m][0:rows, 0],
                                          ALU.subtract).then_inc(low_ready, 1)
                        dve.wait_ge(high_ready, 2 * n + 2)
                        dve.tensor_tensor(parts[m][0:rows, 2], rest[m][0:rows], parts[m][0:rows, 1],
                                          ALU.subtract).then_inc(low_ready, 1)


def routing(nc, d, s):
    with ExitStack() as ctx:
        def sb(name, shape, dt=F32):
            return ctx.enter_context(nc.sbuf_tensor("rt_" + name, shape, dt))

        def pb(name, shape, dt=F32):
            return ctx.enter_context(nc.psum_tensor("rt_" + name, shape, dt))

        def sem(name):
            return ctx.enter_context(nc.semaphore("rt_" + name))

        logits, gates = s["logits"], s["gates"]
        top = sb("top", [P, TILES, 8])
        top_at = sb("top_at", [P, TILES, 8], U32)
        expert = sb("expert", [P, TOPK, TILES])
        iota = sb("iota", [P, NX])
        below = sb("below", [P, P])
        ones = sb("ones", [P, P])
        chosen = sb("chosen", [P, TOPK, TILES, NX])
        shifted = sb("shifted", [P, TILES, NX])
        exps = sb("exps", [P, TILES, NX])
        total = sb("total", [P, TILES])
        inv = sb("inv", [P, TILES])
        top_shift = sb("top_shift", [P, TOPK, TILES])
        top_exp = sb("top_exp", [P, TOPK, TILES])
        prob = sb("prob", [P, TOPK, TILES])
        tile_count = sb("tile_count", [P, TOPK * TILES, NX])
        run_count = sb("run_count", [P, TOPK * TILES, NX])
        before = sb("before", [P, TOPK * TILES, NX])
        ahead = sb("ahead", [P, TOPK * TILES, NX])
        loc = sb("loc", [P, TOPK * TILES])
        keep = sb("keep", [P, TOPK * TILES])
        drop = sb("drop", [P, TOPK * TILES])
        slot = sb("slot", [P, TOPK * TILES])
        slot_low = sb("slot_low", [P, TOPK * TILES])
        slot_put = sb("slot_put", [P, TOPK * TILES])
        kept = sb("kept", [P, TOPK * TILES])
        denom = sb("denom", [P, TILES])
        denom_low = sb("denom_low", [P, TILES])
        inv_denom = sb("inv_denom", [P, TILES])
        pB = pb("p_before", [P, TOPK * TILES * NX])
        pN = pb("p_count", [P, TOPK * TILES * NX])

        consts_in = sem("consts_in")
        ones_ready = sem("ones_ready")
        dve_step = sem("dve_step")
        exp_ready = sem("exp_ready")
        counted = sem("counted")
        FAR = float(1 << 20)

        block = ctx.enter_context(nc.Block())
        after = {}

        def over_experts(ap):
            return ap.unsqueeze(len(ap.shape)).to_broadcast(list(ap.shape) + [NX])

        @block.sync
        def _(sp):
            sp.dma_start(iota[:], d["c_iota"]).then_inc(consts_in, 16)
            sp.dma_start(below[:], d["c_below"]).then_inc(consts_in, 16)

        @block.gpsimd
        def _(pool):
            pool.memset(ones[:], 1.0).then_inc(ones_ready, 1)

        @block.vector
        def _(dve):
            st = Steps(dve, dve_step)
            for t in range(TILES):
                st.did(dve.max(top[:, t], logits[:, t]))
            st.all_done()
            for t in range(TILES):
                st.did(dve.max_index(top_at[:, t], top[:, t], logits[:, t]))
            st.did(dve.tensor_tensor(shifted[:], logits[:], over_experts(top[:, :, 0]), ALU.subtract))
            for k in range(TOPK):
                st.did(dve.tensor_tensor(top_shift[:, k], top[:, :, k], top[:, :, 0], ALU.subtract))
            after["shifts"] = st.n
            st.all_done()
            for k in range(TOPK):
                st.did(dve.tensor_copy(expert[:, k], top_at[:, :, k]))
            st.all_done()
            dve.wait_ge(consts_in, 32)
            for k in range(TOPK):
                st.did(dve.tensor_tensor(chosen[:, k], iota[:].unsqueeze(1).to_broadcast([P, TILES, NX]),
                                         over_experts(expert[:, k]), ALU.is_equal))
            after["chosen"] = st.n
            dve.wait_ge(exp_ready, 2)
            st.did(dve.tensor_reduce(total[:], exps[:], AX.X, ALU.add))
            st.all_done()
            st.did(dve.reciprocal(inv[:], total[:]))
            st.all_done()
            for k in range(TOPK):
                st.did(dve.tensor_tensor(prob[:, k], top_exp[:, k], inv[:], ALU.mult))
            dve.wait_ge(counted, 2)
            st.did(dve.tensor_copy(tile_count[:].rearrange("p c e -> p (c e)"), pN[:]))
            st.all_done()
            for e in range(NX):
                st.did(dve.tensor_tensor_scan(run_count[:, :, e], ones[:, 0:TOPK * TILES], tile_count[:, :, e],
                                              0.0, ALU.mult, ALU.add))
            st.all_done()
            st.did(dve.tensor_tensor(before[:], run_count[:], tile_count[:], ALU.subtract))
            st.all_done()
            st.did(dve.tensor_tensor(ahead[:], before[:], pB[:].rearrange("p (c e) -> p c e", e=NX), ALU.add))
            st.all_done()
            st.did(dve.tensor_tensor(before[:], ahead[:], chosen[:].rearrange("p k t e -> p (k t) e"), ALU.mult))
            st.all_done()
            st.did(dve.tensor_reduce(loc[:], before[:], AX.X, ALU.add))
            st.all_done()
            experts_flat = expert[:].rearrange("p k t -> p (k t)")
            st.did(dve.tensor_scalar(keep[:], loc[:], float(CAP), None, ALU.is_lt))
            st.did(dve.tensor_scalar(drop[:], loc[:], float(CAP), FAR, ALU.is_ge, ALU.mult))
            st.did(dve.scalar_tensor_tensor(slot[:], experts_flat, float(CAP), loc[:], ALU.mult, ALU.add))
            st.all_done()
            st.did(dve.tensor_scalar(slot_low[:], slot[:], float(SLOTS - 1), None, ALU.min))
            st.did(dve.tensor_tensor(slot_put[:], slot[:], drop[:], ALU.add))
            st.did(dve.tensor_tensor(kept[:], prob[:].rearrange("p k t -> p (k t)"), keep[:], ALU.mult))
            st.all_done()
            st.did(dve.tensor_copy(s["slot_get"][:], slot_low[:]))
            st.did(dve.tensor_copy(s["slot_put"][:], slot_put[:]))
            st.did(dve.tensor_tensor(denom[:], kept[:, 0:TILES], kept[:, TILES:2 * TILES], ALU.add))
            st.all_done()
            st.did(dve.tensor_scalar(denom_low[:], denom[:], 1e-9, None, ALU.max))
            st.all_done()
            st.did(dve.reciprocal(inv_denom[:], denom_low[:]))
            st.all_done()
            for k in range(TOPK):
                st.did(dve.tensor_tensor(gates[:, k], kept[:, k * TILES:(k + 1) * TILES], inv_denom[:], ALU.mult))

        @block.scalar
        def _(act):
            act.wait_ge(dve_step, after["shifts"])
            act.activation(exps[:], shifted[:], ACT.Exp).then_inc(exp_ready, 1)
            act.activation(top_exp[:], top_shift[:], ACT.Exp).then_inc(exp_ready, 1)

        @block.tensor
        def _(pe):
            pe.wait_ge(consts_in, 32)
            pe.wait_ge(ones_ready, 1)
            pe.wait_ge(dve_step, after["chosen"])
            flat = chosen[:].rearrange("p k t e -> p (k t e)")
            pe.matmul(pB[:], below[:], flat, start=True, stop=True).then_inc(counted, 1)
            pe.matmul(pN[:], ones[:], flat, start=True, stop=True).then_inc(counted, 1)


def attention(nc, d, s):
    with ExitStack() as ctx:
        def sb(name, shape, dt=F32):
            return ctx.enter_context(nc.sbuf_tensor("at_" + name, shape, dt))

        def pb(name, shape, dt=F32):
            return ctx.enter_context(nc.psum_tensor("at_" + name, shape, dt))

        def sem(name):
            return ctx.enter_context(nc.semaphore("at_" + name))

        attn, ident = s["attn"], s["ident"]
        NA, NB, NE_ = 3, 3, 8
        MR = PARTS
        qa = [sb(f"qa{u}", [STACK, S], BF16) for u in range(2)]
        ka = [sb(f"ka{u}", [STACK, S], BF16) for u in range(2)]
        qb = [sb(f"qb{u}", [STACK + MR, S], BF16) for u in range(2)]
        kb = [sb(f"kb{u}", [STACK + MR, S], BF16) for u in range(2)]
        vs = [sb(f"v{u}", [P, NQ, TPC, VW]) for u in range(2)]
        v_first = [sb(f"v_first{u}", [P, P]) for u in range(2)]
        identb = sb("identb", [P, P], BF16)
        hide_f = sb("hide_f", [P, 2, P])
        hide = sb("hide", [P, 2, P], BF16)
        piece_max = sb("piece_max", [P, QT, NQ])
        neg_max = sb("neg_max", [P, QT])
        neg_rest = sb("neg_rest", [P, QT])
        max_parts = sb("max_parts", [P, 2, PARTS, QT // 2], BF16)
        max_rows = [sb(f"max_rows{i}", [PARTS * QT // 2, P], BF16) for i in range(2)]
        wt = [sb(f"wt{i}", [P, CH]) for i in range(NE_)]
        raw = [sb(f"raw{i}", [P, CH]) for i in range(2)]
        osum = sb("osum", [P, TPC, D + 1])
        oinv = sb("oinv", [P, TPC])
        xrow = [sb(f"xrow{i}", [P, E]) for i in range(2)]

        pA = [pb(f"A{i}", [P, CH]) for i in range(NA)]
        pB = [pb(f"B{i}", [P, CH]) for i in range(NB)]
        pO = [pb(f"O{i}", [P, CH]) for i in range(2)]

        def pX_of(j):
            return pO[j % 2][:].rearrange("p (t n) -> p t n", t=TPC)

        def pM_of(b):
            return pA[b][0:PARTS * QT // 2, 0:P // 2].bitcast(BF16)

        consts_in = sem("consts_in")
        consts_ready = sem("consts_ready")
        a_in = [sem(f"a_in{u}") for u in range(2)]
        b_in = [sem(f"b_in{u}") for u in range(2)]
        max_in = [sem(f"max_in{i}") for i in range(2)]
        a_made = sem("a_made")
        a_used = sem("a_used")
        max_step = sem("max_step")
        b_made = sem("b_made")
        wt_ready = sem("wt_ready")
        wt_used = sem("wt_used")
        o_ready = sem("o_ready")
        oT_made = sem("oT_made")
        o_step = sem("o_step")
        xrow_in = [sem(f"xrow_in{i}") for i in range(2)]
        put = [sem(f"put{i}") for i in range(2)]

        A = [(i, 512 * m, min(512, P * (i + 1) - 512 * m)) for i in range(QT) for m in range(i // 4 + 1)]
        Bp = [(j, kt, max(0, kt - 4 * j) * P) for j in range(NQ) for kt in range(4 * j + 4)]
        NPC = len(A)
        assert len(Bp) == NPC
        HALF = [sum(1 for a in A if a[0] < QT // 2), NPC]
        END = [sum(1 for p in Bp if p[0] <= j) for j in range(NQ)]
        LAG = 3
        M1_AT, M0_AT = 6, HALF[0] + 6
        PER_A = NPC + 2
        assert PER_A % NA == 0 and NPC % NE_ == 0

        def a_step(p):
            return p + (p > M1_AT) + (p > M0_AT)

        def wait(eng, sm, v):
            if not isinstance(v, int) or v > 0:
                eng.wait_ge(sm, v)

        def stack(dst, src, base, head, batch, q_side):
            for r, (g, n) in enumerate(RUNS):
                rows = dst[g * D:(g + n) * D, :]
                if q_side:
                    part = src[0:n, bass.ds(head * D, D), bass.ds(batch * S, S)].rearrange("a p n -> a p n")
                else:
                    part = src[r:r + 1, bass.ds(head * D, D), bass.ds(batch * S, S)].to_broadcast([n, D, S])
                yield rows, part

        def pB_of(p, u):
            return pB[(p + u) % NB]

        block = ctx.enter_context(nc.Block())

        @block.sync
        def _(sp):
            for dst, src in ((hide_f[:, 0], d["c_hide_q"]), (hide_f[:, 1], d["c_hide_k"])):
                sp.dma_start(dst, src).then_inc(consts_in, 16)

            def load_a(n, u):
                wait(sp, a_made, NPC * (n - 1))
                for dst, src in (*stack(qa[u], d["q_parts"], 0, n % H, n // H, True),
                                 *stack(ka[u], d["k_parts"], 0, n % H // 4, n // H, False)):
                    sp.dma_start(dst, src).then_inc(a_in[u], 16)

            def load_b(n, u):
                wait(sp, wt_used, NPC * (n - 1))
                for dst, src in (*stack(qb[u], d["q_parts"], 0, n % H, n // H, True),
                                 *stack(kb[u], d["k_parts"], 0, n % H // 4, n // H, False)):
                    sp.dma_start(dst, src).then_inc(b_in[u], 16)
                v = d["v"][bass.ds(n // H * NQ, NQ), bass.ds(n % H // 4, 1)].rearrange("c o p n -> p (c o) n")
                sp.dma_start(vs[u][:].rearrange("p c t n -> p c (t n)"), v).then_inc(b_in[u], 16)
                first = d["v"][bass.ds(n // H * NQ, 1), bass.ds(n % H // 4, 1), :, 0:VW].rearrange("c o p n -> (c o p) n")
                sp.dma_start(v_first[u][:, 0:VW], first).then_inc(b_in[u], 16)

            def max_store(n, u, half, copied):
                sp.wait_ge(a_used, copied)
                rows = qb[u][STACK:STACK + MR, half * S // 2:(half + 1) * S // 2]
                sp.dma_start(rows.rearrange("a (t n) -> a t n", n=P),
                             max_rows[half][:]).then_inc(max_in[half], 16)

            def round_(n, u):
                max_store(n, u, 1, PER_A * (n + 1) + M1_AT + 2)
                load_b(n + 1, 1 - u)
                load_a(n + 2, u)
                max_store(n + 1, 1 - u, 0, PER_A * (n + 1) + M0_AT + 3)

            load_a(0, 0)
            load_b(0, 0)
            load_a(1, 1)
            max_store(0, 0, 0, M0_AT + 3)
            for n in range(2):
                round_(n, n)
            with sp.Fori(1, HEADS // 2 - 1) as j:
                for u in range(2):
                    round_(2 * j + u, u)
            max_store(HEADS - 2, 0, 1, PER_A * (HEADS - 1) + M1_AT + 2)
            load_b(HEADS - 1, 1)
            max_store(HEADS - 1, 1, 0, PER_A * (HEADS - 1) + M0_AT + 3)
            max_store(HEADS - 1, 1, 1, PER_A * HEADS + 1)

        @block.gpsimd
        def _(pool):
            for u in range(2):
                pool.memset(kb[u][STACK:STACK + MR], 1.0).then_inc(consts_ready, 1)
            for t in range(TILES):
                i = t % 2
                if t >= 2:
                    pool.wait_ge(put[i], 16 * TOPK * (t // 2))
                pool.dma_start(xrow[i][:], d["xn"][t * P:(t + 1) * P]).then_inc(xrow_in[i], 16)
                pool.wait_ge(xrow_in[i], 16 * (t // 2 + 1))
                for k in range(TOPK):
                    c = k * TILES + t
                    pool.indirect_dma_start(
                        out=d["buf"], out_offset=bass.IndirectOffsetOnAxis(ap=s["slot_put"][:, c:c + 1], axis=0),
                        in_=xrow[i][:], in_offset=None, bounds_check=SLOTS - 1, oob_is_err=False,
                    ).then_inc(put[i], 16)
            for i in range(2):
                pool.wait_ge(put[i], 16 * TOPK * (TILES // 2))

        @block.scalar
        def _(act):
            act.wait_ge(consts_in, 32)
            act.copy(hide[:], hide_f[:]).then_inc(consts_ready, 1)
            act.copy(identb[:], ident[:]).then_inc(consts_ready, 1)

            def raw_copy(n, j):
                G = NQ * n + j
                act.wait_ge(wt_used, NPC * n + END[j])
                wait(act, oT_made, G - 1)
                act.copy(raw[j % 2][:], pO[j % 2][:]).then_inc(o_ready, 1)

            def round_(n, u, first):
                for p in range(NPC):
                    j, kt, q0 = Bp[p]
                    N = NPC * n + p
                    act.wait_ge(b_made, N + 1)
                    wait(act, wt_used, N - NE_ + 1)
                    act.activation(wt[p % NE_][:, q0:CH], pB_of(p, u)[:, q0:CH], ACT.Exp,
                                   scale=D ** -0.5).then_inc(wt_ready, 1)
                    for jj in range(NQ):
                        if p == (END[jj] + LAG - 1) % NPC:
                            if jj < NQ - 1:
                                raw_copy(n, jj)
                            elif not first:
                                raw_copy(n - 1, jj)

            for n in range(2):
                round_(n, n, n == 0)
            with act.Fori(1, HEADS // 2) as j:
                for u in range(2):
                    round_(2 * j + u, u, False)
            raw_copy(HEADS - 1, NQ - 1)

        @block.tensor
        def _(pe):
            pe.wait_ge(consts_ready, 7)

            def piece_a(n, u, p):
                i, k0, w = A[p]
                N = PER_A * n + a_step(p)
                b = a_step(p) % NA
                if p == 0:
                    pe.wait_ge(a_in[u], 6 * 16 * (n // 2 + 1))
                wait(pe, a_used, N - NA + 1)
                diag = k0 + w == P * (i + 1)
                ins = pe.matmul(pA[b][:, 0:w], qa[u][:, i * P:(i + 1) * P], ka[u][:, k0:k0 + w],
                                start=True, stop=not diag)
                if diag:
                    ins = pe.matmul(pA[b][:, w - P:w], identb[:], hide[:, 0], start=False, stop=True)
                ins.then_inc(a_made, 1)

            def max_turn(n, half, N, b):
                pe.wait_ge(max_step, 5 * (2 * n + half) + 5)
                wait(pe, a_used, N - NA + 1)
                pe.transpose(pM_of(b), max_parts[:, half].rearrange("p a t -> p (a t)"),
                             identb[:]).then_inc(a_made, 1)

            def piece_b(n, u, p):
                j, kt, q0 = Bp[p]
                N = NPC * n + p
                if p == 0:
                    pe.wait_ge(b_in[u], 8 * 16 * (n // 2 + 1))
                    pe.wait_ge(max_in[0], 16 * (n + 1))
                if p == END[1]:
                    pe.wait_ge(max_in[1], 16 * (n + 1))
                wait(pe, wt_ready, N - NB + 1 + (u == 0 and p < 2))
                diag = kt >= 4 * j
                ins = pe.matmul(pB_of(p, u)[:, q0:CH], kb[u][:, kt * P:(kt + 1) * P],
                                qb[u][:, j * CH + q0:(j + 1) * CH], start=True, stop=not diag)
                if diag:
                    ins = pe.matmul(pB_of(p, u)[:, q0:q0 + P], identb[:], hide[:, 1], start=False, stop=True)
                ins.then_inc(b_made, 1)

            def values(n, u, p4):
                pe.wait_ge(wt_ready, NPC * n + p4 + 4)
                for p in range(p4, p4 + 4):
                    j, kt, q0 = Bp[p]
                    g = kt % 4
                    if kt == 0:
                        wait(pe, o_step, 3 * (NQ * n + j - 2) + 1)
                    if p == 0:
                        pe.matmul(pO[0][:], v_first[u][:], wt[0][:], start=True, stop=False)
                        ins = pe.matmul(pO[0][0:VW, 0:1], v_first[u][:, VW:2 * VW], wt[0][:, 0:1],
                                        start=False, stop=True)
                    else:
                        ins = pe.matmul(pO[j % 2][VW * g:VW * (g + 1), q0:CH], vs[u][:, kt // TPC, kt % TPC, :],
                                        wt[p % NE_][:, q0:CH], start=kt < 4 and j > 0, stop=kt >= 4 * j)
                    ins.then_inc(wt_used, 1)

            def turn(n, j):
                G = NQ * n + j
                pe.wait_ge(o_ready, G + 1)
                for t in range(TPC):
                    ins = pe.transpose(pX_of(j)[:, t, :], raw[j % 2][:, t * P:(t + 1) * P], ident[:])
                ins.then_inc(oT_made, 1)

            def round_(n, u, first, ahead):
                for p in range(NPC):
                    if ahead:
                        piece_a(n + 1, 1 - u, p)
                    if p == M1_AT and ahead:
                        max_turn(n, 1, PER_A * (n + 1) + M1_AT + 1, (M1_AT + 1) % NA)
                    elif p == M1_AT:
                        max_turn(n, 1, PER_A * (n + 1) + NA - 1, 0)
                    if p == M0_AT and ahead:
                        max_turn(n + 1, 0, PER_A * (n + 1) + M0_AT + 2, (M0_AT + 2) % NA)
                    piece_b(n, u, p)
                    if p % 4 == (3 + LAG) % 4:
                        if p >= 3 + LAG:
                            values(n, u, p - 3 - LAG)
                        elif not first:
                            values(n - 1, 1 - u, NPC - 3 - LAG + p)
                    for j in range(NQ):
                        if p == (END[j] + LAG + 2) % NPC:
                            if j < NQ - 1:
                                turn(n, j)
                            elif not first:
                                turn(n - 1, j)

            for p in range(NPC):
                piece_a(0, 0, p)
                if p == M1_AT:
                    pe.wait_ge(a_made, M1_AT + 1)
                    pe.sem_inc(a_made, 1)
                if p == M0_AT:
                    max_turn(0, 0, M0_AT + 2, (M0_AT + 2) % NA)
            for n in range(2):
                round_(n, n, n == 0, True)
            with pe.Fori(1, HEADS // 2 - 1) as j:
                for u in range(2):
                    round_(2 * j + u, u, False, True)
            round_(HEADS - 2, 0, False, True)
            round_(HEADS - 1, 1, False, False)
            values(HEADS - 1, 1, NPC - 4)
            turn(HEADS - 1, NQ - 1)

        @block.vector
        def _(dve):
            dve.memset(piece_max[:], NEG).then_inc(consts_ready, 1)
            for u in range(2):
                dve.memset(v_first[u][:, VW:P], 0.0).then_inc(consts_ready, 1)
            dve.wait_ge(consts_ready, 7)

            def maximum(n, p):
                i, k0, w = A[p]
                dve.wait_ge(a_made, PER_A * n + a_step(p) + 1)
                dve.tensor_reduce(piece_max[:, i, k0 // CH:k0 // CH + 1], pA[a_step(p) % NA][:, 0:w], AX.X,
                                  ALU.max).then_inc(a_used, 1)

            def max_copy(n, half, N, b):
                dve.wait_ge(a_made, N + 1)
                wait(dve, max_in[half], 16 * n)
                dve.tensor_copy(max_rows[half][:], pM_of(b)).then_inc(a_used, 1)

            def cut_max(n, half, step):
                t = slice(half * QT // 2, (half + 1) * QT // 2)
                base = 5 * (2 * n + half)
                if step:
                    dve.wait_ge(max_step, base + step)
                if step == 0:
                    dve.wait_ge(a_used, PER_A * n + a_step(HALF[half] - 1) + 1)
                    ins = dve.tensor_reduce(neg_max[:, t], piece_max[:, t], AX.X, ALU.max, negate=True)
                elif step == 1:
                    ins = dve.tensor_copy(max_parts[:, half, 0], neg_max[:, t])
                elif step == 2:
                    ins = dve.tensor_tensor(neg_rest[:, t], neg_max[:, t], max_parts[:, half, 0], ALU.subtract)
                elif step == 3:
                    ins = dve.tensor_copy(max_parts[:, half, 1], neg_rest[:, t])
                else:
                    ins = dve.tensor_tensor(max_parts[:, half, 2], neg_rest[:, t], max_parts[:, half, 1], ALU.subtract)
                ins.then_inc(max_step, 1)

            def result(n, j, step):
                G = NQ * n + j
                if step == 0:
                    dve.wait_ge(oT_made, G + 1)
                    wait(dve, o_step, 3 * G)
                    src = pX_of(j).rearrange("p t (g n) -> p t n g", g=4)[:, :, 0:D + 1, :]
                    dve.tensor_reduce(osum[:], src, AX.X, ALU.add).then_inc(o_step, 1)
                elif step == 1:
                    dve.wait_ge(o_step, 3 * G + 1)
                    dve.reciprocal(oinv[:], osum[:, :, D]).then_inc(o_step, 1)
                else:
                    dve.wait_ge(o_step, 3 * G + 2)
                    tile0 = n // H * QT + j * TPC
                    dst = attn[:, bass.ds(tile0, TPC), bass.ds(n % H * D, D)]
                    dve.tensor_tensor(dst, osum[:, :, 0:D], oinv[:].unsqueeze(2).to_broadcast([P, TPC, D]),
                                      ALU.mult).then_inc(o_step, 1)

            CUT_1 = {0: (0,), 1: (1, 2), 2: (3, 4)}
            CUT_0 = {HALF[0] + k: (k,) for k in range(5)}

            def round_(n, first, ahead):
                for p in range(NPC):
                    if ahead:
                        maximum(n + 1, p)
                    for step in CUT_1.get(p, ()):
                        cut_max(n, 1, step)
                    if p == M1_AT and ahead:
                        max_copy(n, 1, PER_A * (n + 1) + M1_AT + 1, (M1_AT + 1) % NA)
                    elif p == M1_AT:
                        max_copy(n, 1, PER_A * (n + 1), 0)
                    if ahead:
                        for step in CUT_0.get(p, ()):
                            cut_max(n + 1, 0, step)
                        if p == M0_AT:
                            max_copy(n + 1, 0, PER_A * (n + 1) + M0_AT + 2, (M0_AT + 2) % NA)
                    for j in range(NQ):
                        step = (p - END[j] - LAG - 3) % NPC
                        if step < 3:
                            if j < NQ - 1:
                                result(n, j, step)
                            elif not first:
                                result(n - 1, j, step)

            for p in range(NPC):
                maximum(0, p)
                if p == M1_AT:
                    dve.wait_ge(a_used, M1_AT + 1)
                    dve.sem_inc(a_used, 1)
                for step in CUT_0.get(p, ()):
                    cut_max(0, 0, step)
                if p == M0_AT:
                    max_copy(0, 0, M0_AT + 2, (M0_AT + 2) % NA)
            for n in range(2):
                round_(n, n == 0, True)
            with dve.Fori(1, HEADS // 2 - 1) as j:
                for u in range(2):
                    round_(2 * j + u, False, True)
            round_(HEADS - 2, False, True)
            round_(HEADS - 1, False, False)
            for step in range(3):
                result(HEADS - 1, NQ - 1, step)


def layer1_weights(nc, d, s):
    with ExitStack() as ctx:
        def sb(name, shape, dt=F32):
            return ctx.enter_context(nc.sbuf_tensor("lw_" + name, shape, dt))

        def pb(name, shape, dt=F32):
            return ctx.enter_context(nc.psum_tensor("lw_" + name, shape, dt))

        def sem(name):
            return ctx.enter_context(nc.semaphore("lw_" + name))

        ident = s["ident"]
        gate_n = [sb(f"gate_n{i}", [P, E]) for i in range(2)]
        up_n = [sb(f"up_n{i}", [P, E]) for i in range(2)]
        down_n = [sb(f"down_n{i}", [P, EC, I1]) for i in range(2)]
        route_n = sb("route_n", [NX, E])
        pats = sb("pats", [NPAT, E])
        wq = sb("wq", [P, EC, E])
        wk = sb("wk", [P, EC, E])
        wv = sb("wv", [P, EC, E])
        bq = sb("bq", [P, EC])
        bk = sb("bk", [P, EC])
        bv = sb("bv", [P, E])
        diag = sb("diag", [P, 8, NPAT])
        diag_q = sb("diag_q", [P, 8, NPAT])
        diag_v = sb("diag_v", [P, 4, D])
        bq_wide = sb("bq_wide", [P, EC, P])
        zeros = sb("zeros", [P, P])
        patsT = sb("patsT", [P, EC, NPAT])
        wqT = sb("wqT", [P, EC, E])
        keysT = sb("keysT", [P, EC, NPAT])
        keysT4 = sb("keysT4", [P, EC, 4, NPAT])
        values4 = sb("values4", [P, E])
        key_blocks = sb("key_blocks", [P, EC, 8 * NPAT])

        pG = [pb(f"G{i}", [P, 2 * EC, I1]) for i in range(2)]
        pD = [pb(f"D{i}", [P, EC, P]) for i in range(2)]
        pS = pb("S", [P, EC, NPAT])
        pQ = pb("Q", [P, EC, E])
        pZ = pb("Z", [P, 512])

        mlp_in = [sem(f"mlp_in{i}") for i in range(2)]
        small_in = sem("small_in")
        turned = sem("turned")
        kept = sem("kept")
        pe_step = sem("pe_step")
        dve_step = sem("dve_step")
        MLPS = NX + SI // I1
        at_dve = {}
        order = [("zeros", 1), ("diag_q", 1), ("bq_wide", 2), ("patsT", 1), ("wqT", 1), ("keysT", 2),
                 ("keysT4", 2), ("key_blocks", 2), ("values4", 1), ("values", 1), (("fold", 0), 1), (("fold", 1), 1),
                 ("bias", 1), ("route", 1)]
        n = 0
        for name, count in order:
            n += count
            at_dve[name] = n

        def halves(ap):
            return ap.rearrange("(k p) n -> p k n", p=P)

        block = ctx.enter_context(nc.Block())

        @block.sync
        def _(sp):
            for dst, src in (
                (pats[:], d["key_param"].rearrange("o s e -> (o s) e")), (route_n[:], d["gate_w"]),
                (wq[:], halves(d["Wq"])), (wk[:], halves(d["Wk"])), (wv[:], halves(d["Wv"])), 
                (bq[:], d["bq"].rearrange("(k p) -> p k", p=P)), (bk[:], d["bk"].rearrange("(k p) -> p k", p=P)),
                (bv[:], d["bv"].rearrange("(o n) -> o n", o=1).to_broadcast([P, E])), (diag[:], d["c_diag"]),
                (diag_v[:], d["c_diag_v"]),
            ):
                sp.dma_start(dst, src, allow_slow_non_contiguous=True).then_inc(small_in, 16)
            for e in range(MLPS):
                i = e % 2
                if e >= 2:
                    sp.wait_ge(turned, 2 * (e - 1))
                if e < NX:
                    gate, up, down = d["expert_gate_w"][e], d["expert_up_w"][e], d["expert_down_w"][e]
                else:
                    part = slice((e - NX) * I1, (e - NX + 1) * I1)
                    gate, up, down = d["shared_gate_w"][part], d["shared_up_w"][part], d["shared_down_w"][:, part]
                sp.dma_start(gate_n[i][:], gate).then_inc(mlp_in[i], 16)
                sp.dma_start(up_n[i][:], up).then_inc(mlp_in[i], 16)
                sp.dma_start(down_n[i][:], halves(down)).then_inc(mlp_in[i], 16)

        @block.tensor
        def _(pe):
            st = Steps(pe, pe_step)
            pe.wait_ge(small_in, 16 * 10)
            for k in range(EC):
                ins = pe.transpose(pS[:, k, :], pats[:, k * P:(k + 1) * P], ident[0:NPAT, 0:NPAT])
            st.did(ins)
            for c in range(EC):
                for k in range(EC):
                    ins = pe.transpose(pQ[:, c, k * P:(k + 1) * P], wq[:, k, c * P:(c + 1) * P], ident[:])
            st.did(ins)
            pe.wait_ge(dve_step, at_dve["patsT"])
            for c in range(EC):
                for k in range(EC):
                    ins = pe.matmul(pS[:, c, :], wk[:, k, c * P:(c + 1) * P], patsT[:, k, :], start=(k == 0),
                                    stop=(k == EC - 1))
            st.did(ins)
            pe.wait_ge(dve_step, at_dve["keysT4"])
            for k in range(EC):
                ins = pe.matmul(pZ[:, 0:E], keysT4[:, k].rearrange("p a n -> p (a n)"), wv[:, k, :], start=(k == 0),
                                stop=(k == EC - 1))
            st.did(ins)
            pe.wait_ge(dve_step, at_dve["values4"])
            for k in range(EC):
                for c in range(EC):
                    ins = pe.matmul(pQ[:, c, :], wqT[:, c, k * P:(k + 1) * P], key_blocks[:, c, :], start=True, stop=True)
                st.did(ins)
                pe.wait_ge(dve_step, at_dve["fold", k])
            for c in range(EC):
                ins = pe.matmul(pZ[:, c * E:(c + 1) * E], bq_wide[:, c, :], key_blocks[:, c, :], start=True, stop=True)
            st.did(ins)
            pe.wait_ge(dve_step, at_dve["bias"])
            for k in range(EC):
                ins = pe.transpose(pQ[:, 0, k * NX:(k + 1) * NX], route_n[:, k * P:(k + 1) * P], ident[0:NX, 0:NX])
            st.did(ins)
            for e in range(MLPS):
                i = e % 2
                pe.wait_ge(mlp_in[i], 3 * 16 * (e // 2 + 1))
                if e >= 2:
                    pe.wait_ge(kept, 2 * (e - 1))
                for k in range(EC):
                    cols = slice(k * P, (k + 1) * P)
                    pe.transpose(pG[i][:, k, :], gate_n[i][:, cols], ident[:])
                    ins = pe.transpose(pG[i][:, EC + k, :], up_n[i][:, cols], ident[:])
                ins.then_inc(turned, 1)
                for k in range(EC):
                    ins = pe.transpose(pD[i][:, k, :], down_n[i][:, k, :], ident[:])
                ins.then_inc(turned, 1)

        @block.scalar
        def _(act):
            for e in range(MLPS):
                act.wait_ge(turned, 2 * e + 2)
                act.copy(s["gate_up"][:, e], pG[e % 2][:]).then_inc(kept, 1)
                act.copy(s["down"][:, e], pD[e % 2][:].rearrange("p k n -> p (k n)")).then_inc(kept, 1)

        @block.vector
        def _(dve):
            st = Steps(dve, dve_step)
            st.did(dve.memset(zeros[:], 0.0))
            dve.wait_ge(small_in, 16 * 10)
            st.did(dve.tensor_scalar(diag_q[:], diag[:], D ** -0.5, None, ALU.mult))
            st.all_done()
            for c in range(EC):
                st.did(dve.tensor_scalar(bq_wide[:, c, :], zeros[:], bq[:, c:c + 1], None, ALU.add))
            dve.wait_ge(pe_step, 1)
            st.did(dve.tensor_copy(patsT[:], pS[:]))
            dve.wait_ge(pe_step, 2)
            st.did(dve.tensor_copy(wqT[:], pQ[:]))
            dve.wait_ge(pe_step, 3)
            for c in range(EC):
                st.did(dve.tensor_scalar(keysT[:, c, :], pS[:, c, :], bk[:, c:c + 1], None, ALU.add))
            st.all_done()
            for c in range(EC):
                st.did(dve.tensor_copy(keysT4[:, c], keysT[:, c, :].unsqueeze(1).to_broadcast([P, 4, NPAT])))
            for c in range(EC):
                st.did(dve.tensor_tensor(key_blocks[:, c, :].rearrange("p (h n) -> p h n", n=NPAT), diag_q[:],
                                         keysT[:, c, :].unsqueeze(1).to_broadcast([P, 8, NPAT]), ALU.mult))
            dve.wait_ge(pe_step, 4)
            st.did(dve.tensor_tensor(values4[:], pZ[:, 0:E], bv[:], ALU.add))
            st.all_done()
            st.did(dve.tensor_tensor(s["values"][:], values4[:].rearrange("p (g n) -> p g n", g=4),
                                     diag_v[:].rearrange("p a n -> p (a n)").unsqueeze(1).to_broadcast([P, 4, 4 * D]),
                                     ALU.mult))
            for k in range(EC):
                dve.wait_ge(pe_step, 5 + k)
                st.did(dve.tensor_copy(s["to_scores"][:, k, :], pQ[:].rearrange("p c n -> p (c n)")))
            dve.wait_ge(pe_step, 7)
            st.did(dve.tensor_copy(s["score_bias"][:], pZ[:]))
            dve.wait_ge(pe_step, 8)
            st.did(dve.tensor_copy(s["route"][:].rearrange("p k n -> p (k n)"), pQ[:, 0, 0:EC * NX]))
            assert st.n == at_dve["route"]


def experts(nc, d, s):
    with ExitStack() as ctx:
        def sb(name, shape, dt=F32):
            return ctx.enter_context(nc.sbuf_tensor("ex_" + name, shape, dt))

        def pb(name, shape, dt=F32):
            return ctx.enter_context(nc.psum_tensor("ex_" + name, shape, dt))

        def sem(name):
            return ctx.enter_context(nc.semaphore("ex_" + name))

        RT = 2
        R = RT * P
        PER = CAP // R
        FC = F // P
        assert PER * R == CAP and FC % 4 == 0
        ident = s["ident"]
        w_in = [sb(f"w_in{i}", [P, EC, 2 * F]) for i in range(2)]
        w_out = [sb(f"w_out{i}", [P, FC, E]) for i in range(2)]
        x = [sb(f"x{i}", [P, RT, E]) for i in range(2)]
        xT = [sb(f"xT{i}", [P, EC, R]) for i in range(2)]
        act_a = [sb(f"act_a{i}", [P, R]) for i in range(4)]
        hT = [sb(f"hT{i}", [P, FC, R]) for i in range(2)]
        y = [sb(f"y{i}", [P, RT, E]) for i in range(2)]
        pXT = pb("XT", [P, EC, R])
        pH = [pb(f"H{i}", [P, 2, R]) for i in range(4)]
        pY = [pb(f"Y{i}", [P, RT, E]) for i in range(2)]

        w_loaded = [sem(f"w_loaded{i}") for i in range(2)]
        x_loaded = [sem(f"x_loaded{i}") for i in range(2)]
        xT_made = sem("xT_made")
        xT_ready = sem("xT_ready")
        h_made = sem("h_made")
        act_ready = sem("act_ready")
        h_ready = sem("h_ready")
        y_made = sem("y_made")
        y_ready = sem("y_ready")
        y_stored = [sem(f"y_stored{i}") for i in range(2)]

        rows_in = d["buf"].rearrange("(m t p) e -> m p t e", t=RT, p=P)
        rows_out = d["expert_out"].rearrange("(m t p) e -> m p t e", t=RT, p=P)
        win = d["W_in"].rearrange("x (k p) f -> x p k f", p=P)
        wout = d["W_out"].rearrange("x (k p) e -> x p k e", p=P)

        def one(ap, m):
            return ap[bass.ds(m, 1)].rearrange("o p t e -> (o p) t e")

        def wait(eng, sm, v):
            if not isinstance(v, int) or v > 0:
                eng.wait_ge(sm, v)

        PAIR = 2 * PER
        ROUNDS = NX // 2
        assert PAIR % 2 == 0

        block = ctx.enter_context(nc.Block())

        @block.sync
        def _(sp):
            def weights(e, i):
                wait(sp, y_made, PER * (e - 1))
                sp.dma_start(w_in[i][:], one(win, e)).then_inc(w_loaded[i], 16)
                sp.dma_start(w_out[i][:], one(wout, e)).then_inc(w_loaded[i], 16)

            def rows(m, i):
                wait(sp, xT_made, m - 1)
                sp.dma_start(x[i][:], one(rows_in, m)).then_inc(x_loaded[i], 16)

            def store(m, i):
                sp.wait_ge(y_ready, m + 1)
                sp.dma_start(one(rows_out, m), y[i][:]).then_inc(y_stored[i], 16)

            def round_(j, more):
                for i in range(PAIR):
                    m = PAIR * j + i
                    if i < PAIR - 2 or more:
                        rows(m + 2, i % 2)
                    store(m, i % 2)
                    if i == 0:
                        if not (isinstance(j, int) and j == 0):
                            weights(2 * j + 1, 1)
                    if i == PER and more:
                        weights(2 * j + 2, 0)

            rows(0, 0)
            weights(0, 0)
            rows(1, 1)
            weights(1, 1)
            round_(0, True)
            with sp.Fori(1, ROUNDS - 1) as j:
                round_(j, True)
            round_(ROUNDS - 1, False)
            for i in range(2):
                sp.wait_ge(y_stored[i], 16 * (PAIR // 2 * ROUNDS))

        @block.tensor
        def _(pe):
            def turn(m, i):
                pe.wait_ge(x_loaded[i], 16 * (m // 2 + 1))
                wait(pe, xT_ready, m)
                for t in range(RT):
                    for k in range(EC):
                        ins = pe.transpose(pXT[:, k, t * P:(t + 1) * P], x[i][:, t, k * P:(k + 1) * P], ident[:])
                ins.then_inc(xT_made, 1)

            def hidden(m, i, w, f):
                wait(pe, h_ready, FC * m + f - 3)
                for a in range(2):
                    for k in range(EC):
                        cols = slice(a * F + f * P, a * F + (f + 1) * P)
                        ins = pe.matmul(pH[f][:, a, :], w_in[w][:, k, cols], xT[i][:, k, :],
                                        start=(k == 0), stop=(k == EC - 1))
                ins.then_inc(h_made, 1)

            def output(m, i, w):
                pe.wait_ge(h_ready, FC * m + FC)
                wait(pe, y_ready, m - 1)
                for t in range(RT):
                    for f in range(FC):
                        ins = pe.matmul(pY[i][:, t, :], hT[i][:, f, t * P:(t + 1) * P], w_out[w][:, f, :],
                                        start=(f == 0), stop=(f == FC - 1))
                ins.then_inc(y_made, 1)

            def round_(j, first, last):
                for i in range(PAIR):
                    m, w, b = PAIR * j + i, i // PER, i % 2
                    if i % PER == 0:
                        pe.wait_ge(w_loaded[w], 32 * j + 32)
                    pe.wait_ge(xT_ready, m + 1)
                    for f in range(FC):
                        hidden(m, b, w, f)
                        if f == 0 and not (last and i == PAIR - 1):
                            turn(m + 1, 1 - b)
                        if f == 1 and not (first and i == 0):
                            output(m - 1, 1 - b, (i - 1) % PAIR // PER)

            turn(0, 0)
            round_(0, True, False)
            with pe.Fori(1, ROUNDS - 1) as j:
                round_(j, False, False)
            round_(ROUNDS - 1, False, True)
            output(PAIR * ROUNDS - 1, 1, 1)

        @block.scalar
        def _(act):
            def gelus(m, f):
                act.wait_ge(h_made, FC * m + f + 1)
                act.activation(act_a[f][:], pH[f][:, 0, :], ACT.Gelu).then_inc(act_ready, 1)

            def keep(m, i):
                act.wait_ge(y_made, m + 1)
                wait(act, y_stored[i], 16 * (m // 2))
                act.copy(y[i][:], pY[i][:]).then_inc(y_ready, 1)

            def round_(j, first):
                for i in range(PAIR):
                    m = PAIR * j + i
                    for f in range(FC):
                        gelus(m, f)
                        if f == 1 and not (first and i == 0):
                            keep(m - 1, 1 - i % 2)

            round_(0, True)
            with act.Fori(1, ROUNDS) as j:
                round_(j, False)
            keep(PAIR * ROUNDS - 1, 1)

        @block.vector
        def _(dve):
            def xT_copy(m, i):
                dve.wait_ge(xT_made, m + 1)
                wait(dve, h_made, FC * (m - 1))
                dve.tensor_copy(xT[i][:], pXT[:]).then_inc(xT_ready, 1)

            def round_(j, first, last):
                for i in range(PAIR):
                    m, b = PAIR * j + i, i % 2
                    for f in range(FC):
                        dve.wait_ge(act_ready, FC * m + f + 1)
                        if f == 0:
                            wait(dve, y_made, m - 1)
                        dve.tensor_tensor(hT[b][:, f, :], act_a[f][:], pH[f][:, 1, :], ALU.mult).then_inc(h_ready, 1)
                        if f == 0 and not (last and i == PAIR - 1):
                            xT_copy(m + 1, 1 - b)

            xT_copy(0, 0)
            round_(0, True, False)
            with dve.Fori(1, ROUNDS - 1) as j:
                round_(j, False, False)
            round_(ROUNDS - 1, False, True)


def mixing(nc, d, s):
    with ExitStack() as ctx:
        def sb(name, shape, dt=F32):
            return ctx.enter_context(nc.sbuf_tensor("mx_" + name, shape, dt))

        def pb(name, shape, dt=F32):
            return ctx.enter_context(nc.psum_tensor("mx_" + name, shape, dt))

        def sem(name):
            return ctx.enter_context(nc.semaphore("mx_" + name))

        ident = s["ident"]
        w_out = sb("w_out", [P, EC, E])
        bout = sb("bout", [P, E])
        bo = sb("bo", [P, E])
        x = [sb(f"x{u}", [P, E]) for u in range(2)]
        at = [sb(f"at{u}", [P, E]) for u in range(2)]
        at_slot = [sb(f"at_slot{u}", [P, TOPK], U32) for u in range(2)]
        gate = [sb(f"gate{u}", [P, TOPK]) for u in range(2)]
        ye = [[sb(f"ye{k}{u}", [P, E]) for u in range(2)] for k in range(TOPK)]
        aT = [sb(f"aT{u}", [P, EC, P]) for u in range(2)]
        part = [sb(f"part{u}", [P, 3, E]) for u in range(2)]
        x1 = [sb(f"x1{u}", [P, E]) for u in range(2)]
        xb = [sb(f"xb{u}", [P, E]) for u in range(2)]
        stats = sb("stats", [P, 6])
        carrier = sb("carrier", [P, 1])
        mean_var = sb("mean_var", [P, 2])
        var_eps = sb("var_eps", [P, 1])
        std = sb("std", [P, 1])
        rstd = sb("rstd", [P, 1])
        xn = [sb(f"xn{u}", [P, E]) for u in range(2)]
        xnT = [sb(f"xnT{u}", [P, EC, P]) for u in range(2)]
        pA = [pb(f"A{u}", [P, EC, P]) for u in range(2)]
        pW = [pb(f"W{u}", [P, E]) for u in range(2)]
        pT = [pb(f"T{u}", [P, EC, P]) for u in range(2)]
        pL = [pb(f"L{u}", [P, NX]) for u in range(2)]

        consts_in = sem("consts_in")
        x_in = [sem(f"x_in{u}") for u in range(2)]
        picked = sem("picked")
        rows_in = [sem(f"rows_in{u}") for u in range(2)]
        aT_made = sem("aT_made")
        aT_ready = sem("aT_ready")
        w_made = sem("w_made")
        sums = sem("sums")
        norm = sem("norm")
        std_ready = sem("std_ready")
        xb_ready = sem("xb_ready")
        xb_out = [sem(f"xb_out{u}") for u in range(2)]
        xnT_made = sem("xnT_made")
        xnT_ready = sem("xnT_ready")
        xnT_out = [sem(f"xnT_out{u}") for u in range(2)]
        logits_made = sem("logits_made")
        logits_ready = sem("logits_ready")
        ROUNDS = TILES // 2
        x_rows = d["x"].rearrange("b (t p) e -> (b t) p e", p=P)
        xb_rows = d["x1b"].rearrange("(t p) e -> t p e", p=P)

        def wait(eng, sm, v):
            if not isinstance(v, int) or v > 0:
                eng.wait_ge(sm, v)

        def one(ap, t):
            return ap[bass.ds(t, 1)].rearrange("o p e -> (o p) e")

        def rounds(eng, tile):
            for t in range(2):
                tile(t, t)
            with eng.Fori(1, ROUNDS) as j:
                for u in range(2):
                    tile(2 * j + u, u)

        block = ctx.enter_context(nc.Block())

        @block.sync
        def _(sp):
            sp.dma_start(w_out[:], d["Wout"].rearrange("(k p) n -> p k n", p=P)).then_inc(consts_in, 16)
            sp.dma_start(bout[:], d["bout"].rearrange("(o n) -> o n", o=1).to_broadcast([P, E])).then_inc(consts_in, 16)
            sp.dma_start(bo[:], d["bo"].rearrange("(o n) -> o n", o=1).to_broadcast([P, E])).then_inc(consts_in, 16)

            def tile(t, u):
                wait(sp, sums, 4 * (t - 1))
                wait(sp, aT_made, t - 1)
                sp.dma_start(x[u][:], one(x_rows, t)).then_inc(x_in[u], 16)
                sp.dma_start(at[u][:], s["attn"][:, bass.ds(t, 1), :].rearrange("p o n -> p (o n)")).then_inc(x_in[u], 16)

            rounds(sp, tile)

        @block.gpsimd
        def _(pool):
            def tile(t, u):
                wait(pool, sums, 4 * (t - 1))
                slots = s["slot_get"][:].rearrange("p (k t) -> p k t", k=TOPK)
                pool.tensor_copy(at_slot[u][:], slots[:, :, bass.ds(t, 1)].rearrange("p k o -> p (k o)")).then_inc(picked, 1)
                pool.wait_ge(picked, 2 * t + 1)
                pool.tensor_copy(gate[u][:], s["gates"][:, :, bass.ds(t, 1)].rearrange("p k o -> p (k o)")).then_inc(picked, 1)
                for k in range(TOPK):
                    pool.indirect_dma_start(
                        out=ye[k][u][:], out_offset=None, in_=d["expert_out"],
                        in_offset=bass.IndirectOffsetOnAxis(ap=at_slot[u][:, k:k + 1], axis=0),
                    ).then_inc(rows_in[u], 16)

            rounds(pool, tile)

        @block.tensor
        def _(pe):
            pe.wait_ge(consts_in, 48)

            def project(t, u):
                pe.wait_ge(x_in[u], 32 * (t // 2 + 1))
                wait(pe, aT_ready, t - 1)
                for k in range(EC):
                    ins = pe.transpose(pA[u][:, k, :], at[u][:, k * P:(k + 1) * P], ident[:])
                ins.then_inc(aT_made, 1)
                pe.wait_ge(aT_ready, t + 1)
                wait(pe, sums, 4 * (t - 1))
                for k in range(EC):
                    ins = pe.matmul(pW[u][:], aT[u][:, k, :], w_out[:, k, :], start=(k == 0), stop=(k == EC - 1))
                ins.then_inc(w_made, 1)

            def route(t, u):
                pe.wait_ge(norm, 5 * t + 5)
                wait(pe, xnT_ready, t - 1)
                for k in range(EC):
                    ins = pe.transpose(pT[u][:, k, :], xn[u][:, k * P:(k + 1) * P], ident[:])
                ins.then_inc(xnT_made, 1)
                pe.wait_ge(xnT_ready, t + 1)
                wait(pe, logits_ready, t - 1)
                for k in range(EC):
                    ins = pe.matmul(pL[u][:], xnT[u][:, k, :], s["route"][:, k, :], start=(k == 0), stop=(k == EC - 1))
                ins.then_inc(logits_made, 1)

            project(0, 0)
            project(1, 1)
            route(0, 0)
            with pe.Fori(1, ROUNDS) as j:
                for u in range(2):
                    project(2 * j + u, u)
                    route(2 * j + u - 1, 1 - u)
            route(TILES - 1, 1)

        @block.scalar
        def _(act):
            def turned(t, u):
                act.wait_ge(aT_made, t + 1)
                wait(act, w_made, t - 1)
                act.copy(aT[u][:], pA[u][:]).then_inc(aT_ready, 1)

            def rest(t, u):
                act.wait_ge(norm, 5 * t + 3)
                act.activation(std[:], var_eps[:], ACT.Sqrt).then_inc(std_ready, 1)
                act.wait_ge(xnT_made, t + 1)
                wait(act, logits_made, t - 1)
                wait(act, xnT_out[u], 16 * (t // 2))
                act.copy(xnT[u][:], pT[u][:]).then_inc(xnT_ready, 1)
                act.wait_ge(xnT_ready, t + 1)
                dst = d["x1nT"][:, :, bass.ds(t * P, P)].rearrange("k p n -> p k n")
                act.dma_start(dst, xnT[u][:]).then_inc(xnT_out[u], 16)
                act.wait_ge(xb_ready, t + 1)
                act.dma_start(one(xb_rows, t), xb[u][:]).then_inc(xb_out[u], 16)

            turned(0, 0)
            turned(1, 1)
            rest(0, 0)
            with act.Fori(1, ROUNDS) as j:
                for u in range(2):
                    turned(2 * j + u, u)
                    if u == 0:
                        rest(2 * j - 1, 1)
                    else:
                        rest(2 * j, 0)
            rest(TILES - 1, 1)
            for u in range(2):
                act.wait_ge(xnT_out[u], 16 * ROUNDS)
                act.wait_ge(xb_out[u], 16 * ROUNDS)

        @block.vector
        def _(dve):
            dve.wait_ge(consts_in, 48)

            def total(t, u):
                dve.wait_ge(w_made, t + 1)
                dve.wait_ge(x_in[u], 32 * (t // 2 + 1))
                dve.tensor_tensor(part[u][:, 0], x[u][:], bout[:], ALU.add).then_inc(sums, 1)
                dve.wait_ge(sums, 4 * t + 1)
                dve.tensor_tensor(part[u][:, 1], pW[u][:], part[u][:, 0], ALU.add).then_inc(sums, 1)
                dve.wait_ge(sums, 4 * t + 2)
                dve.wait_ge(rows_in[u], 32 * (t // 2 + 1))
                dve.wait_ge(picked, 2 * t + 2)
                dve.scalar_tensor_tensor(part[u][:, 2], ye[0][u][:], gate[u][:, 0:1], part[u][:, 1], ALU.mult,
                                         ALU.add).then_inc(sums, 1)
                dve.wait_ge(sums, 4 * t + 3)
                wait(dve, xb_ready, t - 1)
                dve.scalar_tensor_tensor(x1[u][:], ye[1][u][:], gate[u][:, 1:2], part[u][:, 2], ALU.mult,
                                         ALU.add).then_inc(sums, 1)
                dve.wait_ge(sums, 4 * t + 4)
                wait(dve, xb_out[u], 16 * (t // 2))
                dve.tensor_tensor(xb[u][:], x1[u][:], bo[:], ALU.add).then_inc(xb_ready, 1)
                dve.bn_stats(stats[:], x1[u][:]).then_inc(norm, 1)
                dve.wait_ge(norm, 5 * t + 1)
                dve.memset(carrier[:], 0.0)
                dve.bn_aggr(mean_var[:], stats[:]).then_inc(norm, 1)
                dve.wait_ge(norm, 5 * t + 2)
                dve.tensor_scalar(var_eps[:], mean_var[:, 1:2], LN_EPS, None, ALU.add).then_inc(norm, 1)
                dve.wait_ge(std_ready, t + 1)
                dve.reciprocal(rstd[:], std[:]).then_inc(norm, 1)
                dve.wait_ge(norm, 5 * t + 4)
                wait(dve, xnT_made, t - 1)
                dve.tensor_scalar(xn[u][:], x1[u][:], mean_var[:, 0:1], rstd[:], ALU.subtract,
                                  ALU.mult).then_inc(norm, 1)

            def logits(t, u):
                dve.wait_ge(logits_made, t + 1)
                dst = s["logits"][:, bass.ds(t, 1), :].rearrange("p o n -> p (o n)")
                dve.tensor_copy(dst, pL[u][:]).then_inc(logits_ready, 1)

            total(0, 0)
            total(1, 1)
            logits(0, 0)
            with dve.Fori(1, ROUNDS) as j:
                for u in range(2):
                    total(2 * j + u, u)
                    logits(2 * j + u - 1, 1 - u)
            logits(TILES - 1, 1)


def weighting(nc, d, s):
    with ExitStack() as ctx:
        def sb(name, shape, dt=F32):
            return ctx.enter_context(nc.sbuf_tensor("wg_" + name, shape, dt))

        def sem(name):
            return ctx.enter_context(nc.semaphore("wg_" + name))

        biased = sb("biased", [P, TILES, NX])
        bias = sb("bias", [P, NX])
        iota = sb("iota", [P, NX])
        ones = sb("ones", [P, P])
        top = sb("top", [P, TILES, 8])
        top_at = sb("top_at", [P, TILES, 8], U32)
        expert = sb("expert", [P, TOPK, TILES])
        chosen = sb("chosen", [P, TOPK, TILES, NX])
        score = sb("score", [P, TOPK, TILES])
        both = sb("both", [P, TILES])
        both_eps = sb("both_eps", [P, TILES])
        inv = sb("inv", [P, TILES])
        share = sb("share", [P, TOPK, TILES])
        picked = sb("picked", [P, TILES, NX])
        shares = sb("shares", [P, TOPK, TILES, NX])
        shared_sum = sb("shared_sum", [P, TILES, NX])
        sums = sb("sums", [P, 2, NX])
        count = sb("count", [P, NX])
        inv_count = sb("inv_count", [P, NX])
        mean = sb("mean", [P, NX])
        pS = ctx.enter_context(nc.psum_tensor("wg_pS", [P, 2 * NX], F32))

        consts_in = sem("consts_in")
        ones_ready = sem("ones_ready")
        dve_step = sem("dve_step")
        scored = sem("scored")
        summed = sem("summed")
        after = {}
        block = ctx.enter_context(nc.Block())

        def over_experts(ap):
            return ap.unsqueeze(len(ap.shape)).to_broadcast(list(ap.shape) + [NX])

        def over_tiles(ap):
            return ap.unsqueeze(1).to_broadcast([P, TILES, NX])

        @block.sync
        def _(sp):
            sp.dma_start(iota[:], d["c_iota"]).then_inc(consts_in, 16)
            sp.dma_start(bias[:], d["lb_bias"].rearrange("(o n) -> o n", o=1).to_broadcast([P, NX])).then_inc(consts_in, 16)

        @block.gpsimd
        def _(pool):
            pool.memset(ones[:], 1.0).then_inc(ones_ready, 1)

        @block.vector
        def _(dve):
            st = Steps(dve, dve_step)
            dve.wait_ge(consts_in, 32)
            st.did(dve.tensor_tensor(biased[:], s["logits"][:], over_tiles(bias[:]), ALU.add))
            st.all_done()
            for t in range(TILES):
                st.did(dve.max(top[:, t], biased[:, t]))
            st.all_done()
            after["top"] = st.n
            for t in range(TILES):
                st.did(dve.max_index(top_at[:, t], top[:, t], biased[:, t]))
            st.all_done()
            for k in range(TOPK):
                st.did(dve.tensor_copy(expert[:, k], top_at[:, :, k]))
            st.all_done()
            for k in range(TOPK):
                st.did(dve.tensor_tensor(chosen[:, k], over_tiles(iota[:]), over_experts(expert[:, k]), ALU.is_equal))
            dve.wait_ge(scored, TOPK)
            st.did(dve.tensor_tensor(both[:], score[:, 0], score[:, 1], ALU.add))
            st.all_done()
            st.did(dve.tensor_scalar(both_eps[:], both[:], 1e-8, None, ALU.add))
            st.all_done()
            st.did(dve.reciprocal(inv[:], both_eps[:]))
            st.all_done()
            for k in range(TOPK):
                st.did(dve.tensor_tensor(share[:, k], score[:, k], inv[:], ALU.mult))
            st.did(dve.tensor_tensor(picked[:], chosen[:, 0], chosen[:, 1], ALU.add))
            st.all_done()
            for k in range(TOPK):
                st.did(dve.tensor_tensor(shares[:, k], chosen[:, k], over_experts(share[:, k]), ALU.mult))
            st.did(dve.tensor_reduce(sums[:, 0], picked[:].rearrange("p t e -> p e t"), AX.X, ALU.add))
            st.all_done()
            st.did(dve.tensor_tensor(shared_sum[:], shares[:, 0], shares[:, 1], ALU.add))
            st.all_done()
            st.did(dve.tensor_reduce(sums[:, 1], shared_sum[:].rearrange("p t e -> p e t"), AX.X, ALU.add))
            after["sums"] = st.n
            dve.wait_ge(summed, 1)
            st.did(dve.tensor_scalar(count[:], pS[:, 0:NX], 1.0, None, ALU.max))
            st.all_done()
            st.did(dve.reciprocal(inv_count[:], count[:]))
            st.all_done()
            st.did(dve.tensor_tensor(mean[:], pS[:, NX:2 * NX], inv_count[:], ALU.mult))
            st.all_done()
            st.did(dve.tensor_tensor(s["weight"][:], picked[:], over_tiles(mean[:]), ALU.mult))

        @block.scalar
        def _(act):
            act.wait_ge(dve_step, after["top"])
            for k in range(TOPK):
                act.activation(score[:, k], top[:, :, k], ACT.Sigmoid).then_inc(scored, 1)

        @block.tensor
        def _(pe):
            pe.wait_ge(ones_ready, 1)
            pe.wait_ge(dve_step, after["sums"])
            pe.matmul(pS[:], ones[:], sums[:].rearrange("p a e -> p (a e)"), start=True, stop=True).then_inc(summed, 1)


def layer1(nc, d, s):
    with ExitStack() as ctx:
        def sb(name, shape, dt=F32):
            return ctx.enter_context(nc.sbuf_tensor("l1_" + name, shape, dt))

        def pb(name, shape, dt=F32):
            return ctx.enter_context(nc.psum_tensor("l1_" + name, shape, dt))

        def sem(name):
            return ctx.enter_context(nc.semaphore("l1_" + name))

        ident = s["ident"]
        MLPS = NX + SI // I1
        ORDER = list(range(NX, MLPS)) + list(range(NX))
        ADDS = MLPS - 1
        PD = TPC // 2
        SUMS = 2 * PD * ADDS
        ZW = H * NPAT
        MIX, SCORE = 2, 6
        seg = sb("seg", [P, TPC * ZW])
        inv_k = sb("inv_k", [P, NPAT])
        xT = s["attn"][:].rearrange("p t e -> p (t e)").rearrange("p (k n) -> p k n", k=EC)
        xT_score = sb("xT_score", [P, EC, TPC, P])
        weight = [sb(f"weight{u}", [P, TPC, NX]) for u in range(2)]
        act_g = [sb(f"act_g{i}", [P, CH]) for i in range(2)]
        hT = [sb(f"hT{i}", [P, CH]) for i in range(2)]
        sumy = [sb(f"sumy{u}", [P, TPC, E]) for u in range(2)]
        z = [sb(f"z{u}", [P, TPC, ZW]) for u in range(2)]
        order = [sb(f"order{i}", [P, TPC * ZW]) for i in range(2)]
        tau = sb("tau", [P, TPC * H])
        over = sb("over", [P, TPC, ZW])
        wts = sb("wts", [P, TPC, ZW])
        wT = [sb(f"wT{i}", [P, 4, P]) for i in range(2)]

        pG = [pb(f"G{i}", [P, CH]) for i in range(2)]
        pU = [pb(f"U{i}", [P, CH]) for i in range(2)]
        pD = [pb(f"D{i}", [P, 2, E]) for i in range(PD)]
        pZ = pb("Z", [P, ZW])
        pO = pb("O", [P, E])

        consts_in = sem("consts_in")
        xT_in = [sem(f"xT_in{b}") for b in range(B)]
        score_cols = sem("score_cols")
        base_in = [sem(f"base_in{u}") for u in range(2)]
        weight_ready = sem("weight_ready")
        gate_made = sem("gate_made")
        up_made = sem("up_made")
        act_ready = sem("act_ready")
        h_ready = sem("h_ready")
        down_made = sem("down_made")
        sum_step = sem("sum_step")
        z_made = sem("z_made")
        z_ready = sem("z_ready")
        sort_step = sem("sort_step")
        over_ready = sem("over_ready")
        wts_ready = sem("wts_ready")
        wT_made = sem("wT_made")
        wT_ready = sem("wT_ready")
        ao_made = sem("ao_made")
        ao_ready = sem("ao_ready")
        stored = [sem(f"stored{u}") for u in range(2)]

        STAGES = []
        size = 2
        while size <= NPAT:
            STAGES.append((size, 0))
            dist = size // 4
            while dist:
                STAGES.append((2 * dist, dist))
                dist //= 2
            size *= 2
        SORTS = 2 * len(STAGES)
        SORT_STEPS = SORTS + 3
        ITEMS = len(STAGES) + 1
        partial = d["partial"].rearrange("(c t p) e -> c p t e", t=TPC, p=P)
        xb_rows = d["x1b"].rearrange("(c t p) e -> c p t e", t=TPC, p=P)

        def wait(eng, sm, v):
            if not isinstance(v, int) or v > 0:
                eng.wait_ge(sm, v)

        def one(ap, c):
            return ap[bass.ds(c, 1)].rearrange("o p t e -> (o p) t e")

        def rounds(eng, chunk):
            for c in range(2):
                chunk(c, c, 2)
            with eng.Fori(1, NCH // 2 - 1) as j:
                for u in range(2):
                    chunk(2 * j + u, u, 2)
            chunk(NCH - 2, 0, 1)
            chunk(NCH - 1, 1, 0)

        block = ctx.enter_context(nc.Block())

        @block.sync
        def _(sp):
            sp.dma_start(seg[:], d["c_seg"]).then_inc(consts_in, 16)
            sp.dma_start(inv_k[:], d["c_inv_k"]).then_inc(consts_in, 16)

            for b in range(B):
                cols = slice(b * S, (b + 1) * S)
                sp.dma_start(xT[:, :, cols], d["x1nT"][:, :, cols].rearrange("k p n -> p k n")).then_inc(xT_in[b], 16)

            def load(c, u):
                wait(sp, stored[u], 16 * (c // 2))
                sp.dma_start(sumy[u][:], one(xb_rows, c)).then_inc(base_in[u], 16)

            def chunk(c, u, behind):
                if behind:
                    load(c + 1, 1 - u)
                sp.wait_ge(sum_step, SUMS * (c + 1))
                sp.dma_start(one(partial, c), sumy[u][:]).then_inc(stored[u], 16)

            load(0, 0)
            rounds(sp, chunk)
            for u in range(2):
                sp.wait_ge(stored[u], 16 * (NCH // 2))

        @block.gpsimd
        def _(pool):
            def above(c, u):
                pool.wait_ge(sort_step, SORT_STEPS * (c + 1))
                wait(pool, wts_ready, c)
                zv = z[u][:].rearrange("p t (h n) -> p (t h) n", n=NPAT)
                ov = over[:].rearrange("p t (h n) -> p (t h) n", n=NPAT)
                pool.tensor_tensor(ov, zv, tau[:].unsqueeze(2).to_broadcast([P, TPC * H, NPAT]),
                                   ALU.subtract).then_inc(over_ready, 1)

            def columns(c):
                wait(pool, z_made, TPC * c)
                cols = xT[:, :, bass.ds(c // NQ * S, S)].rearrange("p k (r j) -> p k j r", j=QT)
                for k in range(EC):
                    pool.tensor_copy(xT_score[:, k], cols[:, k, bass.ds(c % NQ * TPC, TPC), :]).then_inc(score_cols, 1)

            def chunk(c, u, behind):
                wait(pool, sum_step, SUMS * (c - 1))
                pool.tensor_copy(weight[u][:], s["weight"][:, bass.ds(c * TPC, TPC), :]).then_inc(weight_ready, 1)
                if behind == 2:
                    columns(c + 2)
                if behind:
                    above(c + 1, 1 - u)

            for b in range(B):
                pool.wait_ge(xT_in[b], 16)
            columns(0)
            columns(1)
            above(0, 0)
            rounds(pool, chunk)

        @block.tensor
        def _(pe):
            def scores(c, t):
                if t == 0:
                    pe.wait_ge(score_cols, EC * (c + 1))
                    wait(pe, wT_ready, TPC * (c - 1))
                wait(pe, z_ready, TPC * c + t)
                for k in range(EC):
                    ins = pe.matmul(pZ[:], xT_score[:, k, t, :], s["to_scores"][:, k, :],
                                    start=(k == 0), stop=(k == EC - 1))
                ins.then_inc(z_made, 1)

            def mix(c, t, behind):
                if t == 0:
                    pe.wait_ge(wts_ready, c + 1)
                    pe.wait_ge(z_ready, TPC * (c + 2 if behind else NCH))
                n = TPC * c + t
                wait(pe, wT_ready, n)
                for g in range(4):
                    ins = pe.transpose(pZ[:, g * P:(g + 1) * P], wts[:, t, g * P:(g + 1) * P], ident[:])
                ins.then_inc(wT_made, 1)
                pe.wait_ge(wT_ready, n + 1)
                wait(pe, ao_ready, n)
                for g in range(4):
                    ins = pe.matmul(pO[:, g * 4 * D:(g + 1) * 4 * D], wT[t % 2][:, g, :], s["values"][:, g, :],
                                    start=True, stop=True)
                ins.then_inc(ao_made, 1)

            def up(c, u, i):
                n, e = MLPS * c + i, ORDER[i]
                wait(pe, act_ready, n - 1)
                for k in range(EC):
                    ins = pe.matmul(pG[i % 2][:], s["gate_up"][:, e, k, :], xT[:, k, bass.ds(c * CH, CH)], start=(k == 0),
                                    stop=(k == EC - 1))
                ins.then_inc(gate_made, 1)
                wait(pe, h_ready, n - 1)
                for k in range(EC):
                    ins = pe.matmul(pU[i % 2][:], s["gate_up"][:, e, EC + k, :], xT[:, k, bass.ds(c * CH, CH)], start=(k == 0),
                                    stop=(k == EC - 1))
                ins.then_inc(up_made, 1)

            def down(c, i):
                if i == 0:
                    return
                halves = (0, 1) if i == 1 else (i,)
                pe.wait_ge(h_ready, MLPS * c + i + 1)
                for q in range(PD):
                    n = PD * (ADDS * c + i - 1) + q
                    wait(pe, sum_step, 2 * (n - PD + 1))
                    for t in range(2):
                        cols = slice((2 * q + t) * P, (2 * q + t + 1) * P)
                        for m in halves:
                            ins = pe.matmul(pD[q][:, t, :], hT[m % 2][:, cols], s["down"][:, ORDER[m], :],
                                            start=(m == halves[0]), stop=(m == halves[-1]))
                    ins.then_inc(down_made, 1)

            def chunk(c, u, behind):
                for i in range(MLPS):
                    up(c, u, i)
                    if MIX <= i < MIX + TPC:
                        mix(c, i - MIX, behind)
                    if behind == 2 and SCORE <= i < SCORE + TPC:
                        scores(c + 2, i - SCORE)
                    if i:
                        down(c, i - 1)
                down(c, MLPS - 1)

            for b in range(B):
                pe.wait_ge(xT_in[b], 16)
            for c in range(2):
                for t in range(TPC):
                    scores(c, t)
            rounds(pe, chunk)

        @block.scalar
        def _(act):
            def mixed(c, t):
                n = TPC * c + t
                act.wait_ge(wT_made, n + 1)
                wait(act, ao_made, n - 1)
                act.copy(wT[t % 2][:].rearrange("p g n -> p (g n)"), pZ[:]).then_inc(wT_ready, 1)
                act.wait_ge(ao_made, n + 1)
                dst = s["mixed"][:, bass.ds(n, 1), :].rearrange("p o n -> p (o n)")
                act.copy(dst, pO[:]).then_inc(ao_ready, 1)

            def chunk(c, u, behind):
                for i in range(MLPS):
                    n = MLPS * c + i
                    act.wait_ge(gate_made, n + 1)
                    wait(act, h_ready, n - 1)
                    act.activation(act_g[i % 2][:], pG[i % 2][:], ACT.Silu).then_inc(act_ready, 1)
                    if i == MIX - 1:
                        act.wait_ge(over_ready, c + 1)
                        wait(act, wT_made, TPC * c)
                        act.activation(wts[:], over[:], ACT.Relu).then_inc(wts_ready, 1)
                    if MIX <= i < MIX + TPC:
                        mixed(c, i - MIX)

            rounds(act, chunk)

        @block.vector
        def _(dve):
            dve.wait_ge(consts_in, 32)

            def keep_scores(c, u, t):
                dve.wait_ge(z_made, TPC * c + t + 1)
                if t == 0:
                    wait(dve, over_ready, c - 1)
                dve.tensor_tensor(z[u][:, t, :], pZ[:], s["score_bias"][:], ALU.add).then_inc(z_ready, 1)

            def sort(c, u, k):
                size, dist = STAGES[k]
                first = SORT_STEPS * c + 2 * k
                src = z[u][:].rearrange("p t n -> p (t n)") if k == 0 else order[(k - 1) % 2][:]
                sv = src.rearrange("p (b n) -> p b n", n=size)
                dv = order[k % 2][:].rearrange("p (b n) -> p b n", n=size)
                half = size // 2
                low, high = sv[:, :, 0:half], sv[:, :, half:size]
                if dist or half == 1:
                    low_m, high_m = low, high
                else:
                    low_m, high_m = sv[:, :, half - 1::-1], sv[:, :, size - 1:half - 1:-1]
                if k == 0:
                    dve.wait_ge(z_ready, TPC * c + TPC)
                wait(dve, sort_step, first)
                dve.tensor_tensor(dv[:, :, 0:half], low, high_m, ALU.max).then_inc(sort_step, 1)
                dve.tensor_tensor(dv[:, :, half:size], high, low_m, ALU.min).then_inc(sort_step, 1)

            def threshold(c):
                done = SORT_STEPS * c + SORTS
                top = order[(len(STAGES) - 1) % 2]
                run = order[len(STAGES) % 2]
                run_v, top_v = (a[:].rearrange("p (b n) -> p b n", n=NPAT) for a in (run, top))
                dve.wait_ge(sort_step, done)
                dve.tensor_tensor_scan(run[:], seg[:], top[:], 0.0, ALU.mult, ALU.add).then_inc(sort_step, 1)
                dve.wait_ge(sort_step, done + 1)
                dve.scalar_tensor_tensor(top_v, run_v, -1.0, inv_k[:].unsqueeze(1).to_broadcast([P, TPC * H, NPAT]),
                                         ALU.add, ALU.mult).then_inc(sort_step, 1)
                dve.wait_ge(sort_step, done + 2)
                wait(dve, over_ready, c)
                dve.tensor_reduce(tau[:], top_v, AX.X, ALU.max).then_inc(sort_step, 1)

            def hidden(c, i):
                n = MLPS * c + i
                dve.wait_ge(act_ready, n + 1)
                dve.wait_ge(up_made, n + 1)
                used = ADDS * c + (max(1, i - 2) if i >= 2 else i - 1)
                wait(dve, down_made, PD * used)
                dve.tensor_tensor(hT[i % 2][:], act_g[i % 2][:], pU[i % 2][:], ALU.mult).then_inc(h_ready, 1)

            def add(c, u, i):
                if i == 0:
                    return
                for q in range(PD):
                    n = PD * (ADDS * c + i - 1) + q
                    dve.wait_ge(down_made, n + 1)
                    if i == 1:
                        if q == 0:
                            dve.wait_ge(base_in[u], 16 * (c // 2 + 1))
                            dve.wait_ge(weight_ready, c + 1)
                        pair = slice(2 * q, 2 * q + 2)
                        dve.tensor_tensor(sumy[u][:, pair, :], pD[q][:], sumy[u][:, pair, :],
                                          ALU.add).then_inc(sum_step, 2)
                        continue
                    dve.wait_ge(sum_step, 2 * (n - PD + 1))
                    for t in range(2):
                        tt = 2 * q + t
                        dve.scalar_tensor_tensor(sumy[u][:, tt, :], pD[q][:, t, :],
                                                 weight[u][:, tt, ORDER[i]:ORDER[i] + 1], sumy[u][:, tt, :],
                                                 ALU.mult, ALU.add).then_inc(sum_step, 1)

            def chunk(c, u, behind):
                for i in range(MLPS):
                    hidden(c, i)
                    if behind:
                        for k in range(ITEMS * i // MLPS, ITEMS * (i + 1) // MLPS):
                            if k < len(STAGES):
                                sort(c + 1, 1 - u, k)
                            else:
                                threshold(c + 1)
                    if behind == 2 and SCORE <= i < SCORE + TPC:
                        keep_scores(c + 2, u, i - SCORE)
                    if i:
                        add(c, u, i - 1)
                add(c, u, MLPS - 1)

            for c in range(2):
                for t in range(TPC):
                    keep_scores(c, c, t)
            for k in range(len(STAGES)):
                sort(0, 0, k)
            threshold(0)
            rounds(dve, chunk)


def finish(nc, d, s):
    with ExitStack() as ctx:
        def sb(name, shape, dt=F32):
            return ctx.enter_context(nc.sbuf_tensor("fi_" + name, shape, dt))

        def pb(name, shape, dt=F32):
            return ctx.enter_context(nc.psum_tensor("fi_" + name, shape, dt))

        def sem(name):
            return ctx.enter_context(nc.semaphore("fi_" + name))

        ident = s["ident"]
        wo = sb("wo", [P, EC, E])
        head = [sb(f"head{u}", [P, E]) for u in range(2)]
        part = [sb(f"part{u}", [P, E]) for u in range(2)]
        hT = [sb(f"hT{u}", [P, EC, P]) for u in range(2)]
        res = [sb(f"res{u}", [P, E]) for u in range(2)]
        pT = [pb(f"T{u}", [P, EC, P]) for u in range(2)]
        pO = [pb(f"O{u}", [P, E]) for u in range(2)]
        wo_in = sem("wo_in")
        part_in = [sem(f"part_in{u}") for u in range(2)]
        head_ready = sem("head_ready")
        hT_made = sem("hT_made")
        hT_ready = sem("hT_ready")
        o_made = sem("o_made")
        res_ready = sem("res_ready")
        stored = [sem(f"stored{u}") for u in range(2)]
        ROUNDS = TILES // 2
        part_rows = d["partial"].rearrange("(t p) e -> t p e", p=P)
        out_rows = d["out"].rearrange("b (t p) e -> (b t) p e", p=P)

        def wait(eng, sm, v):
            if not isinstance(v, int) or v > 0:
                eng.wait_ge(sm, v)

        def one(ap, t):
            return ap[bass.ds(t, 1)].rearrange("o p e -> (o p) e")

        def rounds(eng, tile):
            for t in range(2):
                tile(t, t)
            with eng.Fori(1, ROUNDS) as j:
                for u in range(2):
                    tile(2 * j + u, u)

        block = ctx.enter_context(nc.Block())

        @block.sync
        def _(sp):
            sp.dma_start(wo[:], d["Wo"].rearrange("(k p) n -> p k n", p=P)).then_inc(wo_in, 16)

            def store(t, u):
                sp.wait_ge(res_ready, t + 1)
                sp.dma_start(one(out_rows, t), res[u][:]).then_inc(stored[u], 16)

            for t in range(2):
                sp.dma_start(part[t][:], one(part_rows, t)).then_inc(part_in[t], 16)
            with sp.Fori(1, ROUNDS) as j:
                for u in range(2):
                    store(2 * j + u - 2, u)
                    sp.dma_start(part[u][:], one(part_rows, 2 * j + u)).then_inc(part_in[u], 16)
            for u in range(2):
                store(TILES - 2 + u, u)
            for u in range(2):
                sp.wait_ge(stored[u], 16 * ROUNDS)

        @block.gpsimd
        def _(pool):
            def tile(t, u):
                wait(pool, hT_made, t - 1)
                src = s["mixed"][:, bass.ds(t // H * QT, QT), bass.ds(t % H * D, D)]
                pool.tensor_copy(head[u][:].rearrange("p (j n) -> p j n", n=D), src).then_inc(head_ready, 1)

            rounds(pool, tile)

        @block.tensor
        def _(pe):
            pe.wait_ge(wo_in, 16)

            def tile(t, u):
                pe.wait_ge(head_ready, t + 1)
                wait(pe, hT_ready, t - 1)
                for k in range(EC):
                    ins = pe.transpose(pT[u][:, k, :], head[u][:, k * P:(k + 1) * P], ident[:])
                ins.then_inc(hT_made, 1)
                pe.wait_ge(hT_ready, t + 1)
                wait(pe, res_ready, t - 1)
                for k in range(EC):
                    ins = pe.matmul(pO[u][:], hT[u][:, k, :], wo[:, k, :], start=(k == 0), stop=(k == EC - 1))
                ins.then_inc(o_made, 1)

            rounds(pe, tile)

        @block.scalar
        def _(act):
            def tile(t, u):
                act.wait_ge(hT_made, t + 1)
                wait(act, o_made, t - 1)
                act.copy(hT[u][:], pT[u][:]).then_inc(hT_ready, 1)

            rounds(act, tile)

        @block.vector
        def _(dve):
            def tile(t, u):
                dve.wait_ge(o_made, t + 1)
                dve.wait_ge(part_in[u], 16 * (t // 2 + 1))
                wait(dve, stored[u], 16 * (t // 2))
                dve.tensor_tensor(res[u][:], pO[u][:], part[u][:], ALU.add).then_inc(res_ready, 1)

            rounds(dve, tile)


def build(nc, d):
    with ExitStack() as ctx:
        for name, shape, dt in (
            ("xn", [NT, E], F32), ("v", [NCH, KVH, P, TPC * VW], F32),
            ("q_parts", [PARTS, H * D, NT], BF16), ("k_parts", [PARTS, KVH * D, NT], BF16),
            ("buf", [SLOTS, E], F32), ("expert_out", [SLOTS, E], F32),
            ("x1b", [NT, E], F32), ("x1nT", [EC, P, NT], F32),
            ("partial", [NT, E], F32),
        ):
            d[name] = nc.dram_tensor(name, shape, dt, kind="Internal").ap()
        s = {}

        def keep(name, shape, dt=F32):
            s[name] = ctx.enter_context(nc.sbuf_tensor("s_" + name, shape, dt))

        keep("ident", [P, P])
        keep("logits", [P, TILES, NX])
        keep("gates", [P, TOPK, TILES])
        keep("slot_get", [P, TOPK * TILES], U32)
        keep("slot_put", [P, TOPK * TILES], U32)
        keep("attn", [P, TILES, E])
        keep("gate_up", [P, NX + SI // I1, 2 * EC, I1])
        keep("down", [P, NX + SI // I1, E])
        keep("route", [P, EC, NX])
        keep("to_scores", [P, EC, H * NPAT])
        keep("score_bias", [P, H * NPAT])
        keep("values", [P, 4, 4 * D])
        keep("weight", [P, TILES, NX])
        latents(nc, d, s)
        routing(nc, d, s)
        attention(nc, d, s)
        layer1_weights(nc, d, s)
        experts(nc, d, s)
        mixing(nc, d, s)
        weighting(nc, d, s)
        keep("mixed", [P, TILES, E])
        layer1(nc, d, s)
        finish(nc, d, s)


_NAMES = {
    "x": "L0_attn_x", "Wqa": "L0_attn_Wqa", "Wqb": "L0_attn_Wqb", "Wkva": "L0_attn_Wkva", "Wkvb": "L0_attn_Wkvb",
    "Wout": "L0_attn_Wout", "bout": "L0_attn_bout", "Wg": "L0_ffn_Wg", "W_in": "L0_ffn_W_in", "W_out": "L0_ffn_W_out",
    "key_param": "L1_attn_key_param", "Wq": "L1_attn_Wq", "bq": "L1_attn_bq", "Wk": "L1_attn_Wk", "bk": "L1_attn_bk",
    "Wv": "L1_attn_Wv", "bv": "L1_attn_bv", "Wo": "L1_attn_Wo", "bo": "L1_attn_bo", "gate_w": "L1_ffn_gate_w",
    "lb_bias": "L1_ffn_lb_bias", "expert_gate_w": "L1_ffn_expert_gate_w", "expert_up_w": "L1_ffn_expert_up_w",
    "expert_down_w": "L1_ffn_expert_down_w", "shared_gate_w": "L1_ffn_shared_gate_w",
    "shared_up_w": "L1_ffn_shared_up_w", "shared_down_w": "L1_ffn_shared_down_w",
}


def constants():
    import numpy as np

    f = np.float32
    at = np.arange(P)
    freq = (f(1.0) / f(10000.0) ** (np.arange(0, D, 2, dtype=f) / f(D))).astype(f)
    angle = np.outer(np.arange(S, dtype=f), freq).astype(f)[:, at % D // 2].T
    sign = np.where(at % 2 == 0, f(-1), f(1))[:, None]
    hide = np.where(at[None, :] > at[:, None], f(NEG), f(0))
    diag = (at[:, None] // D == np.arange(8)[None, :]).astype(f)
    return {
        "c_cos": np.ascontiguousarray(np.cos(angle).astype(f)),
        "c_sin": np.ascontiguousarray((np.sin(angle) * sign).astype(f)),
        "c_ident": np.eye(P, dtype=f),
        "c_iota": np.tile(np.arange(NX, dtype=f), (P, 1)),
        "c_below": (at[:, None] < at[None, :]).astype(f),
        "c_hide_q": hide,
        "c_hide_k": np.ascontiguousarray(hide.T),
        "c_diag": np.repeat(diag[:, :, None], NPAT, axis=2),
        "c_diag_v": np.repeat((at[:, None] // NPAT == np.arange(4)[None, :]).astype(f)[:, :, None], D, axis=2),
        "c_seg": np.tile((np.arange(TPC * H * NPAT) % NPAT != 0).astype(f), (P, 1)),
        "c_inv_k": np.tile((f(1) / np.arange(1, NPAT + 1, dtype=f)).astype(f), (P, 1)),
    }


def kernel(**inputs):
    import numpy as np
    import concourse.bacc as bacc
    from concourse.bass_utils import run_bass_kernel_spmd

    nc = bacc.Bacc("TRN2", target_bir_lowering=False, num_devices=1)
    arrays, d = {}, {}
    for name, a in [(n, np.ascontiguousarray(inputs[full])) for n, full in _NAMES.items()] + list(constants().items()):
        arrays["in_" + name] = a
        d[name] = nc.dram_tensor("in_" + name, a.shape, mybir.dt.from_np(a.dtype), kind="ExternalInput").ap()
    d["out"] = nc.dram_tensor("out_0", (B, S, E), F32, kind="ExternalOutput").ap()
    build(nc, d)
    r = run_bass_kernel_spmd(nc, [arrays], core_ids=[0])
    return r.results[0]["out_0"]
```

```python
from contextlib import ExitStack

import concourse.bass as bass
from concourse import mybir

F32 = mybir.dt.float32
F32R = mybir.dt.float32r
BF16 = mybir.dt.bfloat16
U32 = mybir.dt.uint32
ALU = mybir.AluOpType
ACT = mybir.ActivationFunctionType
AX = mybir.AxisListType

P = 128
B, S, E = 2, 2048, 256
NT = B * S
TILES = NT // P
EC = E // P
CH = 512
NCH = NT // CH
TPC = CH // P
H, KVH, D = 16, 4, 16
QL, KVL = 64, 32
NX, TOPK, F = 8, 2, 512
CAP = -(-TOPK * NT * 5 // (NX * 4))
SLOTS = NX * CAP
NPAT = 32
I1, SI = 128, 256
LN_EPS = 1e-5
LAT = QL + KVL
COMB = LAT + NX
NEG = -1.0e30
PARTS = 3
VW = 32
RUNS = ((0, 3), (3, 2), (5, 1))
STACK = 6 * D
TERMS = ((0, 0), (0, 1), (1, 0))
NQ = S // CH
QT = S // P
HEADS = B * H



class Steps:

    def __init__(self, eng, sem):
        self.eng, self.sem, self.n = eng, sem, 0

    def did(self, ins):
        ins.then_inc(self.sem, 1)
        self.n += 1

    def all_done(self):
        self.eng.wait_ge(self.sem, self.n)


def latents(nc, d, s):
    with ExitStack() as ctx:
        def sb(name, shape, dt=F32):
            return ctx.enter_context(nc.sbuf_tensor(name, shape, dt))

        def pb(name, shape, dt=F32):
            return ctx.enter_context(nc.psum_tensor(name, shape, dt))

        def sem(name):
            return ctx.enter_context(nc.semaphore("lat_" + name))

        ident = s["ident"]
        logits = s["logits"]
        wcomb = sb("wcomb", [P, EC, COMB])
        wqb = sb("wqb", [QL, H * D])
        wqb_swap = sb("wqb_swap", [QL, H * D])
        wkvb = sb("wkvb", [LAT, KVH * D, 2])
        wk = sb("wk", [LAT, KVH * D])
        wk_swap = sb("wk_swap", [LAT, KVH * D])
        wv = sb("wv", [LAT, KVH * D])
        cos = sb("cos", [P, S])
        sin = sb("sin", [P, S])
        x = [sb(f"x{u}", [P, TPC, E]) for u in range(2)]
        stats = sb("stats", [P, TPC, 6])
        carrier = sb("carrier", [P, 1])
        mean_var = sb("mean_var", [P, TPC, 2])
        var_eps = sb("var_eps", [P, TPC])
        std = sb("std", [P, TPC])
        rstd = sb("rstd", [P, TPC])
        xn = [sb(f"xn{u}", [P, TPC, E]) for u in range(2)]
        xnT = [sb(f"xnT{u}", [P, EC, CH]) for u in range(2)]
        comb = [sb(f"comb{u}", [COMB, CH]) for u in range(2)]
        by_cos = [sb(f"by_cos{k}", [P, CH]) for k in range(3)]
        by_sin = [sb(f"by_sin{k}", [P, CH]) for k in range(3)]
        rot = [sb(f"rot{k}", [P, CH]) for k in range(3)]
        rest = [sb(f"rest{k}", [P, CH]) for k in range(3)]
        parts = [sb(f"parts{k}", [P, PARTS, CH], BF16) for k in range(3)]
        vtok = [sb(f"vtok{u}", [P, KVH, TPC, VW]) for u in range(2)]

        zeros = sb("zeros", [P, 8 * E])

        pT = pb("pT", [P, EC, CH])
        pC = pb("pC", [COMB, CH])
        pR = [pb(f"pR{m}", [P, 2, CH]) for m in range(2)]
        pM = pb("pM", [P, 512])
        pV = pM[:, 0:TPC * KVH * D].rearrange("p (t n) -> p t n", t=TPC)
        pL = pT[:, 0, 0:TPC * NX].rearrange("p (t n) -> p t n", t=TPC)

        weights_in = sem("weights_in")
        tables_in = sem("tables_in")
        swapped = sem("swapped")
        x_in = [sem(f"x_in{u}") for u in range(2)]
        stats_ready = sem("stats_ready")
        var_ready = sem("var_ready")
        std_ready = sem("std_ready")
        rstd_ready = sem("rstd_ready")
        xn_ready = sem("xn_ready")
        xn_out = [sem(f"xn_out{u}") for u in range(2)]
        xnT_made = sem("xnT_made")
        xnT_ready = sem("xnT_ready")
        comb_made = sem("comb_made")
        comb_ready = sem("comb_ready")
        vl_made = sem("vl_made")
        vl_ready = sem("vl_ready")
        v_filled = sem("v_filled")
        zeros_ready = sem("zeros_ready")
        buf_blank = sem("buf_blank")
        v_out = [sem(f"v_out{u}") for u in range(2)]
        pair_made = sem("pair_made")
        pair_used = sem("pair_used")
        rot_ready = sem("rot_ready")
        high_ready = sem("high_ready")
        rest_ready = sem("rest_ready")
        mid_ready = sem("mid_ready")
        low_ready = sem("low_ready")
        parts_out = [sem(f"parts_out{k}") for k in range(3)]

        PAIRS = 3
        ROUNDS = NCH // 2
        x_rows = d["x"].rearrange("b (c t p) e -> (b c) p t e", t=TPC, p=P)
        xn_rows = d["xn"].rearrange("(c t p) e -> c p t e", t=TPC, p=P)

        def one(ap, c):
            return ap[bass.ds(c, 1)].rearrange("o p t e -> (o p) t e")

        def rounds(eng, chunk):
            with eng.Fori(0, ROUNDS - 2) as j:
                for u in range(2):
                    chunk(2 * j + u, u, 4)
            for c in range(NCH - 4, NCH):
                chunk(c, c % 2, NCH - 1 - c)

        def rows_of(k):
            return P if k < 2 else KVH * D

        block = ctx.enter_context(nc.Block())

        @block.sync
        def _(sp):
            for u in range(2):
                sp.dma_start(x[u][:], x_rows[u]).then_inc(x_in[u], 16)
            sp.dma_start(ident[:], d["c_ident"]).then_inc(weights_in, 16)
            for dst, src in (
                (wcomb[:, :, 0:QL], d["Wqa"].rearrange("(k p) n -> p k n", p=P)),
                (wcomb[:, :, QL:LAT], d["Wkva"].rearrange("(k p) n -> p k n", p=P)),
                (wcomb[:, :, LAT:COMB], d["Wg"].rearrange("(k p) n -> p k n", p=P)),
                (wqb[:], d["Wqb"]),
                (wkvb[QL:LAT], d["Wkvb"].rearrange("k (n two) -> k n two", two=2)),
            ):
                sp.dma_start(dst, src).then_inc(weights_in, 16)
            sp.dma_start(cos[:], d["c_cos"]).then_inc(tables_in, 16)
            sp.dma_start(sin[:], d["c_sin"]).then_inc(tables_in, 16)
            for u in range(2):
                sp.sem_inc(xn_out[u], 16)
                sp.sem_inc(v_out[u], 16)
            for k in range(PAIRS):
                sp.sem_inc(parts_out[k], 16)

            def xn_store(c, u, load):
                sp.wait_ge(xn_ready, 4 * c + 4)
                if load:
                    sp.dma_start(x[u][:], one(x_rows, c + 2)).then_inc(x_in[u], 16)
                sp.dma_start(one(xn_rows, c), xn[u][:]).then_inc(xn_out[u], 16)

            def chunk(c, u, behind):
                if behind >= 2:
                    xn_store(c + 2, u, behind == 4)
                sp.wait_ge(vl_ready, 2 * c + 4)
                sp.dma_start(d["v"][bass.ds(c, 1)].rearrange("o h p n -> p (o h) n"),
                             vtok[u][:].rearrange("p h t n -> p h (t n)")).then_inc(v_out[u], 16)
                for k in range(PAIRS):
                    sp.wait_ge(low_ready, PAIRS * c + k + 1)
                    dst = d["q_parts"][:, k * P:(k + 1) * P] if k < 2 else d["k_parts"]
                    sp.dma_start(dst[:, :, bass.ds(c * CH, CH)].rearrange("a p n -> p a n"),
                                 parts[k][0:rows_of(k)]).then_inc(parts_out[k], 16)

            for c in range(2):
                xn_store(c, c, True)
            rounds(sp, chunk)
            for u in range(2):
                sp.wait_ge(xn_out[u], 16 * (ROUNDS + 1))
                sp.wait_ge(v_out[u], 16 * (ROUNDS + 1))
            for k in range(PAIRS):
                sp.wait_ge(parts_out[k], 16 * (NCH + 1))

        @block.gpsimd
        def _(pool):
            pool.memset(zeros[:], 0.0).then_inc(zeros_ready, 1)
            pool.wait_ge(zeros_ready, 1)
            blank = d["buf"].rearrange("(a p r) e -> a p (r e)", p=P, r=8)
            for a in range(SLOTS // P // 8):
                pool.dma_start(blank[a], zeros[:]).then_inc(buf_blank, 16)

            def turned(c, k):
                pool.wait_ge(pair_used, 2 * (PAIRS * c + k) + 6)
                rows = rows_of(k)
                pool.tensor_tensor(rot[k][0:rows], by_cos[k][0:rows], by_sin[k][0:rows], ALU.add).then_inc(rot_ready, 1)

            def left(c, k):
                pool.wait_ge(high_ready, PAIRS * c + k + 1)
                rows = rows_of(k)
                pool.tensor_tensor(rest[k][0:rows], rot[k][0:rows], parts[k][0:rows, 0],
                                   ALU.subtract).then_inc(rest_ready, 1)

            def chunk(c, u, behind):
                turned(c, 0)
                for k in range(1, PAIRS):
                    turned(c, k)
                    left(c, k - 1)
                left(c, PAIRS - 1)

            rounds(pool, chunk)
            pool.wait_ge(buf_blank, 16 * (SLOTS // P // 8))

        @block.scalar
        def _(act):
            def std_of(c):
                act.wait_ge(var_ready, 5 * c + 5)
                act.activation(std[:], var_eps[:], ACT.Sqrt).then_inc(std_ready, 1)

            def xnT_copy(c, u):
                act.wait_ge(xnT_made, c + 1)
                act.copy(xnT[u][:, 0], pT[:, 0]).then_inc(xnT_ready, 1)
                act.copy(xnT[u][:, 1], pT[:, 1]).then_inc(xnT_ready, 1)

            def comb_copy(c, u):
                act.wait_ge(comb_made, c + 1)
                act.copy(comb[u][:], pC[:]).then_inc(comb_ready, 1)

            def high(c, k):
                act.wait_ge(rot_ready, PAIRS * c + k + 1)
                act.wait_ge(parts_out[k], 16 * (c + 1))
                act.copy(parts[k][0:rows_of(k), 0], rot[k][0:rows_of(k)]).then_inc(high_ready, 1)

            def mid(c, k):
                act.wait_ge(rest_ready, PAIRS * c + k + 1)
                act.copy(parts[k][0:rows_of(k), 1], rest[k][0:rows_of(k)]).then_inc(mid_ready, 1)

            def chunk(c, u, behind):
                high(c, 0)
                if behind:
                    xnT_copy(c + 1, 1 - u)
                high(c, 1)
                mid(c, 0)
                if behind:
                    comb_copy(c + 1, 1 - u)
                high(c, 2)
                mid(c, 1)
                if behind >= 2:
                    std_of(c + 2)
                mid(c, PAIRS - 1)

            std_of(0)
            act.wait_ge(weights_in, 16 * 6)
            q_pair = wqb[:].rearrange("k (n two) -> k n two", two=2)
            q_swap = wqb_swap[:].rearrange("k (n two) -> k n two", two=2)
            k_pair = wkvb[QL:LAT, :, 0].rearrange("k (n two) -> k n two", two=2)
            k_swap = wk_swap[QL:LAT].rearrange("k (n two) -> k n two", two=2)
            for dst, src in (
                (q_swap[:, :, 0], q_pair[:, :, 1]), (q_swap[:, :, 1], q_pair[:, :, 0]),
                (k_swap[:, :, 0], k_pair[:, :, 1]), (k_swap[:, :, 1], k_pair[:, :, 0]),
                (wk[QL:LAT], wkvb[QL:LAT, :, 0]), (wv[QL:LAT], wkvb[QL:LAT, :, 1]),
            ):
                act.copy(dst, src).then_inc(swapped, 1)
            std_of(1)
            xnT_copy(0, 0)
            comb_copy(0, 0)
            rounds(act, chunk)

        @block.tensor
        def _(pe):
            def turn(c, u):
                pe.wait_ge(xn_ready, 4 * c + 4)
                pe.wait_ge(xnT_ready, 2 * c + 2)
                if not isinstance(c, int) or c:
                    pe.wait_ge(vl_ready, 2 * c)
                for t in range(TPC):
                    for k in range(EC):
                        ins = pe.transpose(pT[:, k, t * P:(t + 1) * P], xn[u][:, t, k * P:(k + 1) * P], ident[:])
                ins.then_inc(xnT_made, 1)

            def combined(c, u):
                pe.wait_ge(xnT_ready, 2 * c + 4)
                pe.wait_ge(comb_ready, c + 1)
                for k in range(EC):
                    ins = pe.matmul(pC[:], wcomb[:, k, :], xnT[u][:, k, :], start=(k == 0), stop=(k == EC - 1))
                ins.then_inc(comb_made, 1)

            def pair(c, u, k):
                n, m = PAIRS * c + k, (PAIRS * u + k) % 2
                pe.wait_ge(pair_used, 2 * n + 2)
                for a in range(2):
                    w = (wqb, wqb_swap)[a][:, k * P:(k + 1) * P] if k < 2 else (wk, wk_swap)[a][QL:LAT]
                    rows = slice(0, QL) if k < 2 else slice(QL, LAT)
                    ins = pe.matmul(pR[m][0:rows_of(k), a], w, comb[u][rows, :], start=True, stop=True)
                ins.then_inc(pair_made, 1)

            def v_and_logits(c, u):
                pe.wait_ge(vl_ready, 2 * c + 2)
                for t in range(TPC):
                    pe.matmul(pV[:, t, :], comb[u][QL:LAT, t * P:(t + 1) * P], wv[QL:LAT, :], start=True, stop=True)
                for t in range(TPC):
                    cols = slice(t * P, (t + 1) * P)
                    ins = pe.transpose(pL[:, t, :], comb[u][LAT:COMB, cols], ident[LAT:COMB, LAT:COMB])
                ins.then_inc(vl_made, 1)

            def chunk(c, u, behind):
                pe.wait_ge(comb_ready, c + 2)
                pair(c, u, 0)
                pair(c, u, 1)
                if behind:
                    turn(c + 1, 1 - u)
                pair(c, u, 2)
                if behind:
                    combined(c + 1, 1 - u)
                v_and_logits(c, u)

            pe.sem_inc(xnT_ready, 2)
            pe.sem_inc(comb_ready, 1)
            pe.sem_inc(vl_ready, 2)
            pe.sem_inc(pair_used, 4)
            pe.wait_ge(weights_in, 16 * 6)
            turn(0, 0)
            combined(0, 0)
            pe.wait_ge(swapped, 6)
            rounds(pe, chunk)

        @block.vector
        def _(dve):
            def statistics(c, u, x_loads):
                dve.wait_ge(x_in[u], 16 * x_loads)
                for t in range(TPC):
                    dve.bn_stats(stats[:, t], x[u][:, t]).then_inc(stats_ready, 1)

            def variances(c):
                dve.wait_ge(stats_ready, 4 * c + 4)
                dve.memset(carrier[:], 0.0)
                for t in range(TPC):
                    dve.bn_aggr(mean_var[:, t], stats[:, t]).then_inc(var_ready, 1)
                dve.wait_ge(var_ready, 5 * c + 4)
                dve.tensor_scalar(var_eps[:], mean_var[:, :, 1], LN_EPS, None, ALU.add).then_inc(var_ready, 1)

            def normalise(c, u, x_loads):
                dve.wait_ge(std_ready, c + 1)
                dve.reciprocal(rstd[:], std[:]).then_inc(rstd_ready, 1)
                dve.wait_ge(rstd_ready, c + 1)
                dve.wait_ge(xn_out[u], 16 * x_loads)
                for t in range(TPC):
                    dve.tensor_scalar(xn[u][:, t], x[u][:, t], mean_var[:, t, 0:1], rstd[:, t:t + 1],
                                      ALU.subtract, ALU.mult).then_inc(xn_ready, 1)

            def products(c, u, k):
                n, m = PAIRS * c + k, (PAIRS * u + k) % 2
                rows = rows_of(k)
                at = bass.ds(c % NQ * CH, CH)
                dve.wait_ge(pair_made, n + 1)
                dve.tensor_tensor(by_cos[k][0:rows], pR[m][0:rows, 0], cos[0:rows, at], ALU.mult).then_inc(pair_used, 1)
                dve.tensor_tensor(by_sin[k][0:rows], pR[m][0:rows, 1], sin[0:rows, at], ALU.mult).then_inc(pair_used, 1)

            def low(c, k):
                dve.wait_ge(mid_ready, PAIRS * c + k + 1)
                dve.tensor_tensor(parts[k][0:rows_of(k), 2], rest[k][0:rows_of(k)], parts[k][0:rows_of(k), 1],
                                  ALU.subtract).then_inc(low_ready, 1)

            def chunk(c, u, behind):
                products(c, u, 0)
                products(c, u, 1)
                products(c, u, 2)
                ahead = behind >= 2
                if ahead:
                    statistics(c + 2, u, c // 2 + 2)
                low(c, 0)
                if ahead:
                    variances(c + 2)
                low(c, 1)
                if ahead:
                    normalise(c + 2, u, c // 2 + 2)
                low(c, 2)
                dve.wait_ge(vl_made, c + 1)
                dve.wait_ge(v_out[u], 16 * (c // 2) + 16)
                dve.tensor_copy(vtok[u][:, :, :, 0:D],
                                pV.rearrange("p t (h n) -> p h t n", h=KVH)).then_inc(vl_ready, 1)
                dve.tensor_copy(logits[:, bass.ds(c * TPC, TPC), :], pL).then_inc(vl_ready, 1)

            for u in range(2):
                dve.memset(vtok[u][:], 0.0).then_inc(v_filled, 1)
                dve.wait_ge(v_filled, 2 * u + 1)
                dve.memset(vtok[u][:, :, :, D:D + 1], 1.0).then_inc(v_filled, 1)
            dve.wait_ge(v_filled, 4)
            for c in range(2):
                statistics(c, c, 1)
                if c:
                    dve.wait_ge(xn_ready, 4 * c)
                variances(c)
                normalise(c, c, 1)
            dve.wait_ge(tables_in, 32)
            rounds(dve, chunk)


def routing(nc, d, s):
    with ExitStack() as ctx:
        def sb(name, shape, dt=F32):
            return ctx.enter_context(nc.sbuf_tensor("rt_" + name, shape, dt))

        def pb(name, shape, dt=F32):
            return ctx.enter_context(nc.psum_tensor("rt_" + name, shape, dt))

        def sem(name):
            return ctx.enter_context(nc.semaphore("rt_" + name))

        logits, gates = s["logits"], s["gates"]
        top = sb("top", [P, TILES, 8])
        top_at = sb("top_at", [P, TILES, 8], U32)
        expert = sb("expert", [P, TOPK, TILES])
        iota = sb("iota", [P, NX])
        below = sb("below", [P, P])
        ones = sb("ones", [P, P])
        chosen = sb("chosen", [P, TOPK, TILES, NX])
        shifted = sb("shifted", [P, TILES, NX])
        exps = sb("exps", [P, TILES, NX])
        total = sb("total", [P, TILES])
        inv = sb("inv", [P, TILES])
        top_shift = sb("top_shift", [P, TOPK, TILES])
        top_exp = sb("top_exp", [P, TOPK, TILES])
        prob = sb("prob", [P, TOPK, TILES])
        tile_count = sb("tile_count", [P, TOPK * TILES, NX])
        run_count = sb("run_count", [P, TOPK * TILES, NX])
        before = sb("before", [P, TOPK * TILES, NX])
        ahead = sb("ahead", [P, TOPK * TILES, NX])
        loc = sb("loc", [P, TOPK * TILES])
        keep = sb("keep", [P, TOPK * TILES])
        drop = sb("drop", [P, TOPK * TILES])
        slot = sb("slot", [P, TOPK * TILES])
        slot_low = sb("slot_low", [P, TOPK * TILES])
        slot_put = sb("slot_put", [P, TOPK * TILES])
        kept = sb("kept", [P, TOPK * TILES])
        denom = sb("denom", [P, TILES])
        denom_low = sb("denom_low", [P, TILES])
        inv_denom = sb("inv_denom", [P, TILES])
        pB = pb("p_before", [P, TOPK * TILES * NX])
        pN = pb("p_count", [P, TOPK * TILES * NX])

        consts_in = sem("consts_in")
        ones_ready = sem("ones_ready")
        dve_step = sem("dve_step")
        exp_ready = sem("exp_ready")
        counted = sem("counted")
        FAR = float(1 << 20)

        block = ctx.enter_context(nc.Block())
        after = {}

        def over_experts(ap):
            return ap.unsqueeze(len(ap.shape)).to_broadcast(list(ap.shape) + [NX])

        @block.sync
        def _(sp):
            sp.dma_start(iota[:], d["c_iota"]).then_inc(consts_in, 16)
            sp.dma_start(below[:], d["c_below"]).then_inc(consts_in, 16)

        @block.gpsimd
        def _(pool):
            pool.memset(ones[:], 1.0).then_inc(ones_ready, 1)

        @block.vector
        def _(dve):
            st = Steps(dve, dve_step)
            for t in range(TILES):
                st.did(dve.max(top[:, t], logits[:, t]))
            st.all_done()
            for t in range(TILES):
                st.did(dve.max_index(top_at[:, t], top[:, t], logits[:, t]))
            st.did(dve.tensor_tensor(shifted[:], logits[:], over_experts(top[:, :, 0]), ALU.subtract))
            for k in range(TOPK):
                st.did(dve.tensor_tensor(top_shift[:, k], top[:, :, k], top[:, :, 0], ALU.subtract))
            after["shifts"] = st.n
            st.all_done()
            for k in range(TOPK):
                st.did(dve.tensor_copy(expert[:, k], top_at[:, :, k]))
            st.all_done()
            dve.wait_ge(consts_in, 32)
            for k in range(TOPK):
                st.did(dve.tensor_tensor(chosen[:, k], iota[:].unsqueeze(1).to_broadcast([P, TILES, NX]),
                                         over_experts(expert[:, k]), ALU.is_equal))
            after["chosen"] = st.n
            dve.wait_ge(exp_ready, 2)
            st.did(dve.tensor_reduce(total[:], exps[:], AX.X, ALU.add))
            st.all_done()
            st.did(dve.reciprocal(inv[:], total[:]))
            st.all_done()
            for k in range(TOPK):
                st.did(dve.tensor_tensor(prob[:, k], top_exp[:, k], inv[:], ALU.mult))
            dve.wait_ge(counted, 2)
            st.did(dve.tensor_copy(tile_count[:].rearrange("p c e -> p (c e)"), pN[:]))
            st.all_done()
            for e in range(NX):
                st.did(dve.tensor_tensor_scan(run_count[:, :, e], ones[:, 0:TOPK * TILES], tile_count[:, :, e],
                                              0.0, ALU.mult, ALU.add))
            st.all_done()
            st.did(dve.tensor_tensor(before[:], run_count[:], tile_count[:], ALU.subtract))
            st.all_done()
            st.did(dve.tensor_tensor(ahead[:], before[:], pB[:].rearrange("p (c e) -> p c e", e=NX), ALU.add))
            st.all_done()
            st.did(dve.tensor_tensor(before[:], ahead[:], chosen[:].rearrange("p k t e -> p (k t) e"), ALU.mult))
            st.all_done()
            st.did(dve.tensor_reduce(loc[:], before[:], AX.X, ALU.add))
            st.all_done()
            experts_flat = expert[:].rearrange("p k t -> p (k t)")
            st.did(dve.tensor_scalar(keep[:], loc[:], float(CAP), None, ALU.is_lt))
            st.did(dve.tensor_scalar(drop[:], loc[:], float(CAP), FAR, ALU.is_ge, ALU.mult))
            st.did(dve.scalar_tensor_tensor(slot[:], experts_flat, float(CAP), loc[:], ALU.mult, ALU.add))
            st.all_done()
            st.did(dve.tensor_scalar(slot_low[:], slot[:], float(SLOTS - 1), None, ALU.min))
            st.did(dve.tensor_tensor(slot_put[:], slot[:], drop[:], ALU.add))
            st.did(dve.tensor_tensor(kept[:], prob[:].rearrange("p k t -> p (k t)"), keep[:], ALU.mult))
            st.all_done()
            st.did(dve.tensor_copy(s["slot_get"][:], slot_low[:]))
            st.did(dve.tensor_copy(s["slot_put"][:], slot_put[:]))
            st.did(dve.tensor_tensor(denom[:], kept[:, 0:TILES], kept[:, TILES:2 * TILES], ALU.add))
            st.all_done()
            st.did(dve.tensor_scalar(denom_low[:], denom[:], 1e-9, None, ALU.max))
            st.all_done()
            st.did(dve.reciprocal(inv_denom[:], denom_low[:]))
            st.all_done()
            for k in range(TOPK):
                st.did(dve.tensor_tensor(gates[:, k], kept[:, k * TILES:(k + 1) * TILES], inv_denom[:], ALU.mult))

        @block.scalar
        def _(act):
            act.wait_ge(dve_step, after["shifts"])
            act.activation(exps[:], shifted[:], ACT.Exp).then_inc(exp_ready, 1)
            act.activation(top_exp[:], top_shift[:], ACT.Exp).then_inc(exp_ready, 1)

        @block.tensor
        def _(pe):
            pe.wait_ge(consts_in, 32)
            pe.wait_ge(ones_ready, 1)
            pe.wait_ge(dve_step, after["chosen"])
            flat = chosen[:].rearrange("p k t e -> p (k t e)")
            pe.matmul(pB[:], below[:], flat, start=True, stop=True).then_inc(counted, 1)
            pe.matmul(pN[:], ones[:], flat, start=True, stop=True).then_inc(counted, 1)


def attention(nc, d, s):
    with ExitStack() as ctx:
        def sb(name, shape, dt=F32):
            return ctx.enter_context(nc.sbuf_tensor("at_" + name, shape, dt))

        def pb(name, shape, dt=F32):
            return ctx.enter_context(nc.psum_tensor("at_" + name, shape, dt))

        def sem(name):
            return ctx.enter_context(nc.semaphore("at_" + name))

        attn, ident = s["attn"], s["ident"]
        NA, NB, NE_ = 3, 3, 8
        MR = PARTS
        qa = [sb(f"qa{u}", [STACK, S], BF16) for u in range(2)]
        ka = [sb(f"ka{u}", [STACK, S], BF16) for u in range(2)]
        qb = [sb(f"qb{u}", [STACK + MR, S], BF16) for u in range(2)]
        kb = [sb(f"kb{u}", [STACK + MR, S], BF16) for u in range(2)]
        vs = [sb(f"v{u}", [P, NQ, TPC, VW]) for u in range(2)]
        v_first = [sb(f"v_first{u}", [P, P]) for u in range(2)]
        identb = sb("identb", [P, P], BF16)
        hide_f = sb("hide_f", [P, 2, P])
        hide = sb("hide", [P, 2, P], BF16)
        piece_max = sb("piece_max", [P, QT, NQ])
        neg_max = sb("neg_max", [P, QT])
        neg_rest = sb("neg_rest", [P, QT])
        max_parts = sb("max_parts", [P, 2, PARTS, QT // 2], BF16)
        max_rows = [sb(f"max_rows{i}", [PARTS * QT // 2, P], BF16) for i in range(2)]
        wt = [sb(f"wt{i}", [P, CH]) for i in range(NE_)]
        raw = [sb(f"raw{i}", [P, CH]) for i in range(2)]
        osum = sb("osum", [P, TPC, D + 1])
        oinv = sb("oinv", [P, TPC])
        xrow = [sb(f"xrow{i}", [P, E]) for i in range(2)]

        pA = [pb(f"A{i}", [P, CH]) for i in range(NA)]
        pB = [pb(f"B{i}", [P, CH]) for i in range(NB)]
        pO = [pb(f"O{i}", [P, CH]) for i in range(2)]

        def pX_of(j):
            return pO[j % 2][:].rearrange("p (t n) -> p t n", t=TPC)

        def pM_of(b):
            return pA[b][0:PARTS * QT // 2, 0:P // 2].bitcast(BF16)

        consts_in = sem("consts_in")
        consts_ready = sem("consts_ready")
        a_in = [sem(f"a_in{u}") for u in range(2)]
        b_in = [sem(f"b_in{u}") for u in range(2)]
        max_in = [sem(f"max_in{i}") for i in range(2)]
        a_made = sem("a_made")
        a_used = sem("a_used")
        max_step = sem("max_step")
        b_made = sem("b_made")
        wt_ready = sem("wt_ready")
        wt_used = sem("wt_used")
        o_ready = sem("o_ready")
        oT_made = sem("oT_made")
        o_step = sem("o_step")
        xrow_in = [sem(f"xrow_in{i}") for i in range(2)]
        put = [sem(f"put{i}") for i in range(2)]

        A = [(i, 512 * m, min(512, P * (i + 1) - 512 * m)) for i in range(QT) for m in range(i // 4 + 1)]
        Bp = [(j, kt, max(0, kt - 4 * j) * P) for j in range(NQ) for kt in range(4 * j + 4)]
        NPC = len(A)
        assert len(Bp) == NPC
        HALF = [sum(1 for a in A if a[0] < QT // 2), NPC]
        END = [sum(1 for p in Bp if p[0] <= j) for j in range(NQ)]
        LAG = 3
        M1_AT, M0_AT = 6, HALF[0] + 6
        PER_A = NPC + 2
        assert PER_A % NA == 0 and NPC % NE_ == 0

        def a_step(p):
            return p + (p > M1_AT) + (p > M0_AT)

        def wait(eng, sm, v):
            if not isinstance(v, int) or v > 0:
                eng.wait_ge(sm, v)

        def stack(dst, src, base, head, batch, q_side):
            for r, (g, n) in enumerate(RUNS):
                rows = dst[g * D:(g + n) * D, :]
                if q_side:
                    part = src[0:n, bass.ds(head * D, D), bass.ds(batch * S, S)].rearrange("a p n -> a p n")
                else:
                    part = src[r:r + 1, bass.ds(head * D, D), bass.ds(batch * S, S)].to_broadcast([n, D, S])
                yield rows, part

        def pB_of(p, u):
            return pB[(p + u) % NB]

        block = ctx.enter_context(nc.Block())

        @block.sync
        def _(sp):
            for dst, src in ((hide_f[:, 0], d["c_hide_q"]), (hide_f[:, 1], d["c_hide_k"])):
                sp.dma_start(dst, src).then_inc(consts_in, 16)

            def load_a(n, u):
                wait(sp, a_made, NPC * (n - 1))
                for dst, src in (*stack(qa[u], d["q_parts"], 0, n % H, n // H, True),
                                 *stack(ka[u], d["k_parts"], 0, n % H // 4, n // H, False)):
                    sp.dma_start(dst, src).then_inc(a_in[u], 16)

            def load_b(n, u):
                wait(sp, wt_used, NPC * (n - 1))
                for dst, src in (*stack(qb[u], d["q_parts"], 0, n % H, n // H, True),
                                 *stack(kb[u], d["k_parts"], 0, n % H // 4, n // H, False)):
                    sp.dma_start(dst, src).then_inc(b_in[u], 16)
                v = d["v"][bass.ds(n // H * NQ, NQ), bass.ds(n % H // 4, 1)].rearrange("c o p n -> p (c o) n")
                sp.dma_start(vs[u][:].rearrange("p c t n -> p c (t n)"), v).then_inc(b_in[u], 16)
                first = d["v"][bass.ds(n // H * NQ, 1), bass.ds(n % H // 4, 1), :, 0:VW].rearrange("c o p n -> (c o p) n")
                sp.dma_start(v_first[u][:, 0:VW], first).then_inc(b_in[u], 16)

            def max_store(n, u, half, copied):
                sp.wait_ge(a_used, copied)
                rows = qb[u][STACK:STACK + MR, half * S // 2:(half + 1) * S // 2]
                sp.dma_start(rows.rearrange("a (t n) -> a t n", n=P),
                             max_rows[half][:]).then_inc(max_in[half], 16)

            def round_(n, u):
                max_store(n, u, 1, PER_A * (n + 1) + M1_AT + 2)
                load_b(n + 1, 1 - u)
                load_a(n + 2, u)
                max_store(n + 1, 1 - u, 0, PER_A * (n + 1) + M0_AT + 3)

            load_a(0, 0)
            load_b(0, 0)
            load_a(1, 1)
            max_store(0, 0, 0, M0_AT + 3)
            for n in range(2):
                round_(n, n)
            with sp.Fori(1, HEADS // 2 - 1) as j:
                for u in range(2):
                    round_(2 * j + u, u)
            max_store(HEADS - 2, 0, 1, PER_A * (HEADS - 1) + M1_AT + 2)
            load_b(HEADS - 1, 1)
            max_store(HEADS - 1, 1, 0, PER_A * (HEADS - 1) + M0_AT + 3)
            max_store(HEADS - 1, 1, 1, PER_A * HEADS + 1)

        @block.gpsimd
        def _(pool):
            for u in range(2):
                pool.memset(kb[u][STACK:STACK + MR], 1.0).then_inc(consts_ready, 1)
            for t in range(TILES):
                i = t % 2
                if t >= 2:
                    pool.wait_ge(put[i], 16 * TOPK * (t // 2))
                pool.dma_start(xrow[i][:], d["xn"][t * P:(t + 1) * P]).then_inc(xrow_in[i], 16)
                pool.wait_ge(xrow_in[i], 16 * (t // 2 + 1))
                for k in range(TOPK):
                    c = k * TILES + t
                    pool.indirect_dma_start(
                        out=d["buf"], out_offset=bass.IndirectOffsetOnAxis(ap=s["slot_put"][:, c:c + 1], axis=0),
                        in_=xrow[i][:], in_offset=None, bounds_check=SLOTS - 1, oob_is_err=False,
                    ).then_inc(put[i], 16)
            for i in range(2):
                pool.wait_ge(put[i], 16 * TOPK * (TILES // 2))

        @block.scalar
        def _(act):
            act.wait_ge(consts_in, 32)
            act.copy(hide[:], hide_f[:]).then_inc(consts_ready, 1)
            act.copy(identb[:], ident[:]).then_inc(consts_ready, 1)

            def raw_copy(n, j):
                G = NQ * n + j
                act.wait_ge(wt_used, NPC * n + END[j])
                wait(act, oT_made, G - 1)
                act.copy(raw[j % 2][:], pO[j % 2][:]).then_inc(o_ready, 1)

            def round_(n, u, first):
                for p in range(NPC):
                    j, kt, q0 = Bp[p]
                    N = NPC * n + p
                    act.wait_ge(b_made, N + 1)
                    wait(act, wt_used, N - NE_ + 1)
                    act.activation(wt[p % NE_][:, q0:CH], pB_of(p, u)[:, q0:CH], ACT.Exp,
                                   scale=D ** -0.5).then_inc(wt_ready, 1)
                    for jj in range(NQ):
                        if p == (END[jj] + LAG - 1) % NPC:
                            if jj < NQ - 1:
                                raw_copy(n, jj)
                            elif not first:
                                raw_copy(n - 1, jj)

            for n in range(2):
                round_(n, n, n == 0)
            with act.Fori(1, HEADS // 2) as j:
                for u in range(2):
                    round_(2 * j + u, u, False)
            raw_copy(HEADS - 1, NQ - 1)

        @block.tensor
        def _(pe):
            pe.wait_ge(consts_ready, 7)

            def piece_a(n, u, p):
                i, k0, w = A[p]
                N = PER_A * n + a_step(p)
                b = a_step(p) % NA
                if p == 0:
                    pe.wait_ge(a_in[u], 6 * 16 * (n // 2 + 1))
                wait(pe, a_used, N - NA + 1)
                diag = k0 + w == P * (i + 1)
                ins = pe.matmul(pA[b][:, 0:w], qa[u][:, i * P:(i + 1) * P], ka[u][:, k0:k0 + w],
                                start=True, stop=not diag)
                if diag:
                    ins = pe.matmul(pA[b][:, w - P:w], identb[:], hide[:, 0], start=False, stop=True)
                ins.then_inc(a_made, 1)

            def max_turn(n, half, N, b):
                pe.wait_ge(max_step, 5 * (2 * n + half) + 5)
                wait(pe, a_used, N - NA + 1)
                pe.transpose(pM_of(b), max_parts[:, half].rearrange("p a t -> p (a t)"),
                             identb[:]).then_inc(a_made, 1)

            def piece_b(n, u, p):
                j, kt, q0 = Bp[p]
                N = NPC * n + p
                if p == 0:
                    pe.wait_ge(b_in[u], 8 * 16 * (n // 2 + 1))
                    pe.wait_ge(max_in[0], 16 * (n + 1))
                if p == END[1]:
                    pe.wait_ge(max_in[1], 16 * (n + 1))
                wait(pe, wt_ready, N - NB + 1 + (u == 0 and p < 2))
                diag = kt >= 4 * j
                ins = pe.matmul(pB_of(p, u)[:, q0:CH], kb[u][:, kt * P:(kt + 1) * P],
                                qb[u][:, j * CH + q0:(j + 1) * CH], start=True, stop=not diag)
                if diag:
                    ins = pe.matmul(pB_of(p, u)[:, q0:q0 + P], identb[:], hide[:, 1], start=False, stop=True)
                ins.then_inc(b_made, 1)

            def values(n, u, p4):
                pe.wait_ge(wt_ready, NPC * n + p4 + 4)
                for p in range(p4, p4 + 4):
                    j, kt, q0 = Bp[p]
                    g = kt % 4
                    if kt == 0:
                        wait(pe, o_step, 3 * (NQ * n + j - 2) + 1)
                    if p == 0:
                        pe.matmul(pO[0][:], v_first[u][:], wt[0][:], start=True, stop=False)
                        ins = pe.matmul(pO[0][0:VW, 0:1], v_first[u][:, VW:2 * VW], wt[0][:, 0:1],
                                        start=False, stop=True)
                    else:
                        ins = pe.matmul(pO[j % 2][VW * g:VW * (g + 1), q0:CH], vs[u][:, kt // TPC, kt % TPC, :],
                                        wt[p % NE_][:, q0:CH], start=kt < 4 and j > 0, stop=kt >= 4 * j)
                    ins.then_inc(wt_used, 1)

            def turn(n, j):
                G = NQ * n + j
                pe.wait_ge(o_ready, G + 1)
                for t in range(TPC):
                    ins = pe.transpose(pX_of(j)[:, t, :], raw[j % 2][:, t * P:(t + 1) * P], ident[:])
                ins.then_inc(oT_made, 1)

            def round_(n, u, first, ahead):
                for p in range(NPC):
                    if ahead:
                        piece_a(n + 1, 1 - u, p)
                    if p == M1_AT and ahead:
                        max_turn(n, 1, PER_A * (n + 1) + M1_AT + 1, (M1_AT + 1) % NA)
                    elif p == M1_AT:
                        max_turn(n, 1, PER_A * (n + 1) + NA - 1, 0)
                    if p == M0_AT and ahead:
                        max_turn(n + 1, 0, PER_A * (n + 1) + M0_AT + 2, (M0_AT + 2) % NA)
                    piece_b(n, u, p)
                    if p % 4 == (3 + LAG) % 4:
                        if p >= 3 + LAG:
                            values(n, u, p - 3 - LAG)
                        elif not first:
                            values(n - 1, 1 - u, NPC - 3 - LAG + p)
                    for j in range(NQ):
                        if p == (END[j] + LAG + 2) % NPC:
                            if j < NQ - 1:
                                turn(n, j)
                            elif not first:
                                turn(n - 1, j)

            for p in range(NPC):
                piece_a(0, 0, p)
                if p == M1_AT:
                    pe.wait_ge(a_made, M1_AT + 1)
                    pe.sem_inc(a_made, 1)
                if p == M0_AT:
                    max_turn(0, 0, M0_AT + 2, (M0_AT + 2) % NA)
            for n in range(2):
                round_(n, n, n == 0, True)
            with pe.Fori(1, HEADS // 2 - 1) as j:
                for u in range(2):
                    round_(2 * j + u, u, False, True)
            round_(HEADS - 2, 0, False, True)
            round_(HEADS - 1, 1, False, False)
            values(HEADS - 1, 1, NPC - 4)
            turn(HEADS - 1, NQ - 1)

        @block.vector
        def _(dve):
            dve.memset(piece_max[:], NEG).then_inc(consts_ready, 1)
            for u in range(2):
                dve.memset(v_first[u][:, VW:P], 0.0).then_inc(consts_ready, 1)
            dve.wait_ge(consts_ready, 7)

            def maximum(n, p):
                i, k0, w = A[p]
                dve.wait_ge(a_made, PER_A * n + a_step(p) + 1)
                dve.tensor_reduce(piece_max[:, i, k0 // CH:k0 // CH + 1], pA[a_step(p) % NA][:, 0:w], AX.X,
                                  ALU.max).then_inc(a_used, 1)

            def max_copy(n, half, N, b):
                dve.wait_ge(a_made, N + 1)
                wait(dve, max_in[half], 16 * n)
                dve.tensor_copy(max_rows[half][:], pM_of(b)).then_inc(a_used, 1)

            def cut_max(n, half, step):
                t = slice(half * QT // 2, (half + 1) * QT // 2)
                base = 5 * (2 * n + half)
                if step:
                    dve.wait_ge(max_step, base + step)
                if step == 0:
                    dve.wait_ge(a_used, PER_A * n + a_step(HALF[half] - 1) + 1)
                    ins = dve.tensor_reduce(neg_max[:, t], piece_max[:, t], AX.X, ALU.max, negate=True)
                elif step == 1:
                    ins = dve.tensor_copy(max_parts[:, half, 0], neg_max[:, t])
                elif step == 2:
                    ins = dve.tensor_tensor(neg_rest[:, t], neg_max[:, t], max_parts[:, half, 0], ALU.subtract)
                elif step == 3:
                    ins = dve.tensor_copy(max_parts[:, half, 1], neg_rest[:, t])
                else:
                    ins = dve.tensor_tensor(max_parts[:, half, 2], neg_rest[:, t], max_parts[:, half, 1], ALU.subtract)
                ins.then_inc(max_step, 1)

            def result(n, j, step):
                G = NQ * n + j
                if step == 0:
                    dve.wait_ge(oT_made, G + 1)
                    wait(dve, o_step, 3 * G)
                    src = pX_of(j).rearrange("p t (g n) -> p t n g", g=4)[:, :, 0:D + 1, :]
                    dve.tensor_reduce(osum[:], src, AX.X, ALU.add).then_inc(o_step, 1)
                elif step == 1:
                    dve.wait_ge(o_step, 3 * G + 1)
                    dve.reciprocal(oinv[:], osum[:, :, D]).then_inc(o_step, 1)
                else:
                    dve.wait_ge(o_step, 3 * G + 2)
                    tile0 = n // H * QT + j * TPC
                    dst = attn[:, bass.ds(tile0, TPC), bass.ds(n % H * D, D)]
                    dve.tensor_tensor(dst, osum[:, :, 0:D], oinv[:].unsqueeze(2).to_broadcast([P, TPC, D]),
                                      ALU.mult).then_inc(o_step, 1)

            CUT_1 = {0: (0,), 1: (1, 2), 2: (3, 4)}
            CUT_0 = {HALF[0] + k: (k,) for k in range(5)}

            def round_(n, first, ahead):
                for p in range(NPC):
                    if ahead:
                        maximum(n + 1, p)
                    for step in CUT_1.get(p, ()):
                        cut_max(n, 1, step)
                    if p == M1_AT and ahead:
                        max_copy(n, 1, PER_A * (n + 1) + M1_AT + 1, (M1_AT + 1) % NA)
                    elif p == M1_AT:
                        max_copy(n, 1, PER_A * (n + 1), 0)
                    if ahead:
                        for step in CUT_0.get(p, ()):
                            cut_max(n + 1, 0, step)
                        if p == M0_AT:
                            max_copy(n + 1, 0, PER_A * (n + 1) + M0_AT + 2, (M0_AT + 2) % NA)
                    for j in range(NQ):
                        step = (p - END[j] - LAG - 3) % NPC
                        if step < 3:
                            if j < NQ - 1:
                                result(n, j, step)
                            elif not first:
                                result(n - 1, j, step)

            for p in range(NPC):
                maximum(0, p)
                if p == M1_AT:
                    dve.wait_ge(a_used, M1_AT + 1)
                    dve.sem_inc(a_used, 1)
                for step in CUT_0.get(p, ()):
                    cut_max(0, 0, step)
                if p == M0_AT:
                    max_copy(0, 0, M0_AT + 2, (M0_AT + 2) % NA)
            for n in range(2):
                round_(n, n == 0, True)
            with dve.Fori(1, HEADS // 2 - 1) as j:
                for u in range(2):
                    round_(2 * j + u, False, True)
            round_(HEADS - 2, False, True)
            round_(HEADS - 1, False, False)
            for step in range(3):
                result(HEADS - 1, NQ - 1, step)


def layer1_weights(nc, d, s):
    with ExitStack() as ctx:
        def sb(name, shape, dt=F32):
            return ctx.enter_context(nc.sbuf_tensor("lw_" + name, shape, dt))

        def pb(name, shape, dt=F32):
            return ctx.enter_context(nc.psum_tensor("lw_" + name, shape, dt))

        def sem(name):
            return ctx.enter_context(nc.semaphore("lw_" + name))

        ident = s["ident"]
        gate_n = [sb(f"gate_n{i}", [P, E]) for i in range(2)]
        up_n = [sb(f"up_n{i}", [P, E]) for i in range(2)]
        down_n = [sb(f"down_n{i}", [P, EC, I1]) for i in range(2)]
        route_n = sb("route_n", [NX, E])
        pats = sb("pats", [NPAT, E])
        wq = sb("wq", [P, EC, E])
        wk = sb("wk", [P, EC, E])
        wv = sb("wv", [P, EC, E])
        bq = sb("bq", [P, EC])
        bk = sb("bk", [P, EC])
        bv = sb("bv", [P, E])
        diag = sb("diag", [P, 8, NPAT])
        diag_q = sb("diag_q", [P, 8, NPAT])
        diag_v = sb("diag_v", [P, 4, D])
        bq_wide = sb("bq_wide", [P, EC, P])
        zeros = sb("zeros", [P, P])
        patsT = sb("patsT", [P, EC, NPAT])
        wqT = sb("wqT", [P, EC, E])
        keysT = sb("keysT", [P, EC, NPAT])
        keysT4 = sb("keysT4", [P, EC, 4, NPAT])
        values4 = sb("values4", [P, E])
        key_blocks = sb("key_blocks", [P, EC, 8 * NPAT])

        pG = [pb(f"G{i}", [P, 2 * EC, I1]) for i in range(2)]
        pD = [pb(f"D{i}", [P, EC, P]) for i in range(2)]
        pS = pb("S", [P, EC, NPAT])
        pQ = pb("Q", [P, EC, E])
        pZ = pb("Z", [P, 512])

        mlp_in = [sem(f"mlp_in{i}") for i in range(2)]
        small_in = sem("small_in")
        turned = sem("turned")
        kept = sem("kept")
        pe_step = sem("pe_step")
        dve_step = sem("dve_step")
        MLPS = NX + SI // I1
        at_dve = {}
        order = [("zeros", 1), ("diag_q", 1), ("bq_wide", 2), ("patsT", 1), ("wqT", 1), ("keysT", 2),
                 ("keysT4", 2), ("key_blocks", 2), ("values4", 1), ("values", 1), (("fold", 0), 1), (("fold", 1), 1),
                 ("bias", 1), ("route", 1)]
        n = 0
        for name, count in order:
            n += count
            at_dve[name] = n

        def halves(ap):
            return ap.rearrange("(k p) n -> p k n", p=P)

        block = ctx.enter_context(nc.Block())

        @block.sync
        def _(sp):
            for dst, src in (
                (pats[:], d["key_param"].rearrange("o s e -> (o s) e")), (route_n[:], d["gate_w"]),
                (wq[:], halves(d["Wq"])), (wk[:], halves(d["Wk"])), (wv[:], halves(d["Wv"])), 
                (bq[:], d["bq"].rearrange("(k p) -> p k", p=P)), (bk[:], d["bk"].rearrange("(k p) -> p k", p=P)),
                (bv[:], d["bv"].rearrange("(o n) -> o n", o=1).to_broadcast([P, E])), (diag[:], d["c_diag"]),
                (diag_v[:], d["c_diag_v"]),
            ):
                sp.dma_start(dst, src, allow_slow_non_contiguous=True).then_inc(small_in, 16)
            for e in range(MLPS):
                i = e % 2
                if e >= 2:
                    sp.wait_ge(turned, 2 * (e - 1))
                if e < NX:
                    gate, up, down = d["expert_gate_w"][e], d["expert_up_w"][e], d["expert_down_w"][e]
                else:
                    part = slice((e - NX) * I1, (e - NX + 1) * I1)
                    gate, up, down = d["shared_gate_w"][part], d["shared_up_w"][part], d["shared_down_w"][:, part]
                sp.dma_start(gate_n[i][:], gate).then_inc(mlp_in[i], 16)
                sp.dma_start(up_n[i][:], up).then_inc(mlp_in[i], 16)
                sp.dma_start(down_n[i][:], halves(down)).then_inc(mlp_in[i], 16)

        @block.tensor
        def _(pe):
            st = Steps(pe, pe_step)
            pe.wait_ge(small_in, 16 * 10)
            for k in range(EC):
                ins = pe.transpose(pS[:, k, :], pats[:, k * P:(k + 1) * P], ident[0:NPAT, 0:NPAT])
            st.did(ins)
            for c in range(EC):
                for k in range(EC):
                    ins = pe.transpose(pQ[:, c, k * P:(k + 1) * P], wq[:, k, c * P:(c + 1) * P], ident[:])
            st.did(ins)
            pe.wait_ge(dve_step, at_dve["patsT"])
            for c in range(EC):
                for k in range(EC):
                    ins = pe.matmul(pS[:, c, :], wk[:, k, c * P:(c + 1) * P], patsT[:, k, :], start=(k == 0),
                                    stop=(k == EC - 1))
            st.did(ins)
            pe.wait_ge(dve_step, at_dve["keysT4"])
            for k in range(EC):
                ins = pe.matmul(pZ[:, 0:E], keysT4[:, k].rearrange("p a n -> p (a n)"), wv[:, k, :], start=(k == 0),
                                stop=(k == EC - 1))
            st.did(ins)
            pe.wait_ge(dve_step, at_dve["values4"])
            for k in range(EC):
                for c in range(EC):
                    ins = pe.matmul(pQ[:, c, :], wqT[:, c, k * P:(k + 1) * P], key_blocks[:, c, :], start=True, stop=True)
                st.did(ins)
                pe.wait_ge(dve_step, at_dve["fold", k])
            for c in range(EC):
                ins = pe.matmul(pZ[:, c * E:(c + 1) * E], bq_wide[:, c, :], key_blocks[:, c, :], start=True, stop=True)
            st.did(ins)
            pe.wait_ge(dve_step, at_dve["bias"])
            for k in range(EC):
                ins = pe.transpose(pQ[:, 0, k * NX:(k + 1) * NX], route_n[:, k * P:(k + 1) * P], ident[0:NX, 0:NX])
            st.did(ins)
            for e in range(MLPS):
                i = e % 2
                pe.wait_ge(mlp_in[i], 3 * 16 * (e // 2 + 1))
                if e >= 2:
                    pe.wait_ge(kept, 2 * (e - 1))
                for k in range(EC):
                    cols = slice(k * P, (k + 1) * P)
                    pe.transpose(pG[i][:, k, :], gate_n[i][:, cols], ident[:])
                    ins = pe.transpose(pG[i][:, EC + k, :], up_n[i][:, cols], ident[:])
                ins.then_inc(turned, 1)
                for k in range(EC):
                    ins = pe.transpose(pD[i][:, k, :], down_n[i][:, k, :], ident[:])
                ins.then_inc(turned, 1)

        @block.scalar
        def _(act):
            for e in range(MLPS):
                act.wait_ge(turned, 2 * e + 2)
                act.copy(s["gate_up"][:, e], pG[e % 2][:]).then_inc(kept, 1)
                act.copy(s["down"][:, e], pD[e % 2][:].rearrange("p k n -> p (k n)")).then_inc(kept, 1)

        @block.vector
        def _(dve):
            st = Steps(dve, dve_step)
            st.did(dve.memset(zeros[:], 0.0))
            dve.wait_ge(small_in, 16 * 10)
            st.did(dve.tensor_scalar(diag_q[:], diag[:], D ** -0.5, None, ALU.mult))
            st.all_done()
            for c in range(EC):
                st.did(dve.tensor_scalar(bq_wide[:, c, :], zeros[:], bq[:, c:c + 1], None, ALU.add))
            dve.wait_ge(pe_step, 1)
            st.did(dve.tensor_copy(patsT[:], pS[:]))
            dve.wait_ge(pe_step, 2)
            st.did(dve.tensor_copy(wqT[:], pQ[:]))
            dve.wait_ge(pe_step, 3)
            for c in range(EC):
                st.did(dve.tensor_scalar(keysT[:, c, :], pS[:, c, :], bk[:, c:c + 1], None, ALU.add))
            st.all_done()
            for c in range(EC):
                st.did(dve.tensor_copy(keysT4[:, c], keysT[:, c, :].unsqueeze(1).to_broadcast([P, 4, NPAT])))
            for c in range(EC):
                st.did(dve.tensor_tensor(key_blocks[:, c, :].rearrange("p (h n) -> p h n", n=NPAT), diag_q[:],
                                         keysT[:, c, :].unsqueeze(1).to_broadcast([P, 8, NPAT]), ALU.mult))
            dve.wait_ge(pe_step, 4)
            st.did(dve.tensor_tensor(values4[:], pZ[:, 0:E], bv[:], ALU.add))
            st.all_done()
            st.did(dve.tensor_tensor(s["values"][:], values4[:].rearrange("p (g n) -> p g n", g=4),
                                     diag_v[:].rearrange("p a n -> p (a n)").unsqueeze(1).to_broadcast([P, 4, 4 * D]),
                                     ALU.mult))
            for k in range(EC):
                dve.wait_ge(pe_step, 5 + k)
                st.did(dve.tensor_copy(s["to_scores"][:, k, :], pQ[:].rearrange("p c n -> p (c n)")))
            dve.wait_ge(pe_step, 7)
            st.did(dve.tensor_copy(s["score_bias"][:], pZ[:]))
            dve.wait_ge(pe_step, 8)
            st.did(dve.tensor_copy(s["route"][:].rearrange("p k n -> p (k n)"), pQ[:, 0, 0:EC * NX]))
            assert st.n == at_dve["route"]


def experts(nc, d, s):
    with ExitStack() as ctx:
        def sb(name, shape, dt=F32):
            return ctx.enter_context(nc.sbuf_tensor("ex_" + name, shape, dt))

        def pb(name, shape, dt=F32):
            return ctx.enter_context(nc.psum_tensor("ex_" + name, shape, dt))

        def sem(name):
            return ctx.enter_context(nc.semaphore("ex_" + name))

        RT = 2
        R = RT * P
        PER = CAP // R
        FC = F // P
        assert PER * R == CAP and FC % 4 == 0
        ident = s["ident"]
        raw_in = sb("raw_in", [P, EC, 2 * F])
        raw_out = sb("raw_out", [P, FC, E])
        w_in = [[sb(f"w_in{i}{a}", [P, EC, 2 * F], F32R) for a in range(2)] for i in range(2)]
        w_out = [[sb(f"w_out{i}{a}", [P, FC, E], F32R) for a in range(2)] for i in range(2)]
        x = [sb(f"x{i}", [P, RT, E]) for i in range(2)]
        xT = [[sb(f"xT{i}{a}", [P, EC, R], F32R) for a in range(2)] for i in range(2)]
        act_a = [sb(f"act_a{i}", [P, R]) for i in range(4)]
        h = [sb(f"h{i}", [P, FC, R]) for i in range(2)]
        hT = [[sb(f"hT{i}{a}", [P, FC, R], F32R) for a in range(2)] for i in range(2)]
        y = [sb(f"y{i}", [P, RT, E]) for i in range(2)]
        pXT = pb("XT", [P, EC, R])
        pH = [pb(f"H{i}", [P, 2, R]) for i in range(4)]
        pY = [pb(f"Y{i}", [P, RT, E]) for i in range(2)]

        w_loaded = sem("w_loaded")
        w_high = sem("w_high")
        w_low = sem("w_low")
        x_loaded = [sem(f"x_loaded{i}") for i in range(2)]
        xT_made = sem("xT_made")
        xT_high = sem("xT_high")
        xT_low = sem("xT_low")
        h_made = sem("h_made")
        act_ready = sem("act_ready")
        h_ready = sem("h_ready")
        h_high = sem("h_high")
        h_low = sem("h_low")
        y_made = sem("y_made")
        y_ready = sem("y_ready")
        y_stored = [sem(f"y_stored{i}") for i in range(2)]

        rows_in = d["buf"].rearrange("(m t p) e -> m p t e", t=RT, p=P)
        rows_out = d["expert_out"].rearrange("(m t p) e -> m p t e", t=RT, p=P)
        win = d["W_in"].rearrange("x (k p) f -> x p k f", p=P)
        wout = d["W_out"].rearrange("x (k p) e -> x p k e", p=P)

        def one(ap, m):
            return ap[bass.ds(m, 1)].rearrange("o p t e -> (o p) t e")

        def wait(eng, sm, v):
            if not isinstance(v, int) or v > 0:
                eng.wait_ge(sm, v)

        def pieces(w):
            flat = "p a b -> p (a b)"
            found = []
            for raw, parts in ((raw_in, w_in[w]), (raw_out, w_out[w])):
                views = [t[:].rearrange(flat) for t in (raw, *parts)]
                found += [tuple(v[:, c:c + 512] for v in views) for c in range(0, views[0].shape[1], 512)]
            return found

        CUTS = len(pieces(0))
        CUT_IN = {2: (0, 1), 3: (2, 3), 4: (4, 5)}
        CUTS_IN = 4
        assert CUTS == 6 and PER == 5

        PAIR = 2 * PER
        ROUNDS = NX // 2
        assert PAIR % 2 == 0

        def cuts(cut, j, i, last):
            e = 2 * j + i // PER
            if not (last and i >= PER):
                for q in CUT_IN.get(i % PER, ()):
                    cut(e + 1, 1 - i // PER, q)

        block = ctx.enter_context(nc.Block())

        @block.sync
        def _(sp):
            def weights(e):
                wait(sp, w_low, CUTS * e)
                sp.dma_start(raw_in[:], one(win, e)).then_inc(w_loaded, 16)
                sp.dma_start(raw_out[:], one(wout, e)).then_inc(w_loaded, 16)

            def rows(m, i):
                wait(sp, xT_made, m - 1)
                sp.dma_start(x[i][:], one(rows_in, m)).then_inc(x_loaded[i], 16)

            def round_(j, more):
                for i in range(PAIR):
                    m = PAIR * j + i
                    if i < PAIR - 2 or more:
                        rows(m + 2, i % 2)
                    if i % PER == 0 and (i < PER or more):
                        weights(2 * j + i // PER + 1)

            weights(0)
            rows(0, 0)
            rows(1, 1)
            with sp.Fori(0, ROUNDS - 1) as j:
                round_(j, True)
            round_(ROUNDS - 1, False)

        @block.tensor
        def _(pe):
            def turn(m, i):
                pe.wait_ge(x_loaded[i], 16 * (m // 2 + 1))
                wait(pe, xT_low, m)
                for t in range(RT):
                    for k in range(EC):
                        ins = pe.transpose(pXT[:, k, t * P:(t + 1) * P], x[i][:, t, k * P:(k + 1) * P], ident[:])
                ins.then_inc(xT_made, 1)

            def hidden(m, i, w, f):
                wait(pe, h_ready, FC * m + f - 3)
                for a in range(2):
                    terms = [(k, *q) for k in range(EC) for q in TERMS]
                    for n, (k, wq, xq) in enumerate(terms):
                        cols = slice(a * F + f * P, a * F + (f + 1) * P)
                        ins = pe.matmul(pH[f][:, a, :], w_in[w][wq][:, k, cols], xT[i][xq][:, k, :],
                                        start=(n == 0), stop=(n == len(terms) - 1))
                ins.then_inc(h_made, 1)

            def output(m, i, w):
                pe.wait_ge(h_low, FC * m + FC)
                wait(pe, y_ready, m - 1)
                for t in range(RT):
                    terms = [(f, *q) for f in range(FC) for q in TERMS]
                    for n, (f, hq, wq) in enumerate(terms):
                        ins = pe.matmul(pY[i][:, t, :], hT[i][hq][:, f, t * P:(t + 1) * P], w_out[w][wq][:, f, :],
                                        start=(n == 0), stop=(n == len(terms) - 1))
                ins.then_inc(y_made, 1)

            def round_(j, first, last):
                for i in range(PAIR):
                    m, w, b = PAIR * j + i, i // PER, i % 2
                    if i % PER == 0:
                        pe.wait_ge(w_low, CUTS * (2 * j + w) + CUTS_IN)
                    pe.wait_ge(xT_low, m + 1)
                    for f in range(FC):
                        hidden(m, b, w, f)
                        if f == 0 and not (last and i == PAIR - 1):
                            turn(m + 1, 1 - b)
                        if f == 1 and not (first and i == 0):
                            if i % PER == 1:
                                pe.wait_ge(w_low, CUTS * (2 * j + w + 1))
                            output(m - 1, 1 - b, (i - 1) % PAIR // PER)

            turn(0, 0)
            round_(0, True, False)
            with pe.Fori(1, ROUNDS - 1) as j:
                round_(j, False, False)
            round_(ROUNDS - 1, False, True)
            output(PAIR * ROUNDS - 1, 1, 1)

        @block.gpsimd
        def _(pool):
            with pool.Fori(0, ROUNDS) as j:
                for i in range(PAIR):
                    for f in range(FC):
                        pool.wait_ge(h_high, FC * (PAIR * j + i) + f + 1)
                        pool.tensor_tensor(hT[i % 2][1][:, f, :], h[i % 2][:, f, :],
                                           hT[i % 2][0][:, f, :].bitcast(F32), ALU.subtract).then_inc(h_low, 1)

        @block.scalar
        def _(act):
            def gelus(m, f):
                act.wait_ge(h_made, FC * m + f + 1)
                act.activation(act_a[f][:], pH[f][:, 0, :], ACT.Gelu).then_inc(act_ready, 1)

            def high(m, i, f):
                act.wait_ge(h_ready, FC * m + f + 1)
                act.copy(hT[i][0][:, f, :], h[i][:, f, :]).then_inc(h_high, 1)

            def keep(m, i):
                act.wait_ge(y_made, m + 1)
                wait(act, y_stored[i], 16 * (m // 2))
                act.copy(y[i][:], pY[i][:]).then_inc(y_ready, 1)

            def store(m, i):
                act.wait_ge(y_ready, m + 1)
                act.dma_start(one(rows_out, m), y[i][:]).then_inc(y_stored[i], 16)

            def xT_copy(m, i):
                act.wait_ge(xT_made, m + 1)
                wait(act, h_made, FC * (m - 1))
                act.copy(xT[i][0][:], pXT[:]).then_inc(xT_high, 1)

            def cut(e, w, q):
                raw, parts = pieces(w)[q][0], pieces(w)[q][1:]
                act.wait_ge(w_loaded, 32 * (e + 1))
                act.copy(parts[0], raw).then_inc(w_high, 1)

            def round_(j, first, last):
                for i in range(PAIR):
                    m, b = PAIR * j + i, i % 2
                    for f in range(FC):
                        gelus(m, f)
                        if f == 0 and not (last and i == PAIR - 1):
                            xT_copy(m + 1, 1 - b)
                        if f:
                            high(m, b, f - 1)
                        if f == 1 and not (first and i == 0):
                            keep(m - 1, 1 - b)
                        if f == 2 and not (first and i == 0):
                            store(m - 1, 1 - b)
                        if f == 2:
                            cuts(cut, j, i, last)
                    high(m, b, FC - 1)

            for q in range(CUTS):
                cut(0, 0, q)
            xT_copy(0, 0)
            round_(0, True, False)
            with act.Fori(1, ROUNDS - 1) as j:
                round_(j, False, False)
            round_(ROUNDS - 1, False, True)
            keep(PAIR * ROUNDS - 1, 1)
            store(PAIR * ROUNDS - 1, 1)
            for i in range(2):
                act.wait_ge(y_stored[i], 16 * (PAIR // 2 * ROUNDS))

        @block.vector
        def _(dve):
            def xT_rest(m, i):
                dve.wait_ge(xT_high, m + 1)
                dve.tensor_tensor(xT[i][1][:], pXT[:], xT[i][0][:].bitcast(F32), ALU.subtract).then_inc(xT_low, 1)

            def cut(e, w, q):
                raw, high, low = pieces(w)[q]
                dve.wait_ge(w_high, CUTS * e + q + 1)
                dve.tensor_tensor(low, raw, high.bitcast(F32), ALU.subtract).then_inc(w_low, 1)

            def round_(j, first, last):
                for i in range(PAIR):
                    m, b = PAIR * j + i, i % 2
                    for f in range(FC):
                        dve.wait_ge(act_ready, FC * m + f + 1)
                        if f == 0:
                            wait(dve, y_made, m - 1)
                        dve.tensor_tensor(h[b][:, f, :], act_a[f][:], pH[f][:, 1, :], ALU.mult).then_inc(h_ready, 1)
                        if f == 0 and not (last and i == PAIR - 1):
                            xT_rest(m + 1, 1 - b)
                        if f == 2:
                            cuts(cut, j, i, last)

            for q in range(CUTS):
                cut(0, 0, q)
            xT_rest(0, 0)
            round_(0, True, False)
            with dve.Fori(1, ROUNDS - 1) as j:
                round_(j, False, False)
            round_(ROUNDS - 1, False, True)


def mixing(nc, d, s):
    with ExitStack() as ctx:
        def sb(name, shape, dt=F32):
            return ctx.enter_context(nc.sbuf_tensor("mx_" + name, shape, dt))

        def pb(name, shape, dt=F32):
            return ctx.enter_context(nc.psum_tensor("mx_" + name, shape, dt))

        def sem(name):
            return ctx.enter_context(nc.semaphore("mx_" + name))

        ident = s["ident"]
        w_out = sb("w_out", [P, EC, E])
        bout = sb("bout", [P, E])
        bo = sb("bo", [P, E])
        x = [sb(f"x{u}", [P, E]) for u in range(2)]
        at = [sb(f"at{u}", [P, E]) for u in range(2)]
        at_slot = [sb(f"at_slot{u}", [P, TOPK], U32) for u in range(2)]
        gate = [sb(f"gate{u}", [P, TOPK]) for u in range(2)]
        ye = [[sb(f"ye{k}{u}", [P, E]) for u in range(2)] for k in range(TOPK)]
        aT = [sb(f"aT{u}", [P, EC, P]) for u in range(2)]
        part = [sb(f"part{u}", [P, 3, E]) for u in range(2)]
        x1 = [sb(f"x1{u}", [P, E]) for u in range(2)]
        xb = [sb(f"xb{u}", [P, E]) for u in range(2)]
        stats = sb("stats", [P, 6])
        carrier = sb("carrier", [P, 1])
        mean_var = sb("mean_var", [P, 2])
        var_eps = sb("var_eps", [P, 1])
        std = sb("std", [P, 1])
        rstd = sb("rstd", [P, 1])
        xn = [sb(f"xn{u}", [P, E]) for u in range(2)]
        xnT = [sb(f"xnT{u}", [P, EC, P]) for u in range(2)]
        pA = [pb(f"A{u}", [P, EC, P]) for u in range(2)]
        pW = [pb(f"W{u}", [P, E]) for u in range(2)]
        pT = [pb(f"T{u}", [P, EC, P]) for u in range(2)]
        pL = [pb(f"L{u}", [P, NX]) for u in range(2)]

        consts_in = sem("consts_in")
        x_in = [sem(f"x_in{u}") for u in range(2)]
        picked = sem("picked")
        rows_in = [sem(f"rows_in{u}") for u in range(2)]
        aT_made = sem("aT_made")
        aT_ready = sem("aT_ready")
        w_made = sem("w_made")
        sums = sem("sums")
        norm = sem("norm")
        std_ready = sem("std_ready")
        xb_ready = sem("xb_ready")
        xb_out = [sem(f"xb_out{u}") for u in range(2)]
        xnT_made = sem("xnT_made")
        xnT_ready = sem("xnT_ready")
        xnT_out = [sem(f"xnT_out{u}") for u in range(2)]
        logits_made = sem("logits_made")
        logits_ready = sem("logits_ready")
        ROUNDS = TILES // 2
        x_rows = d["x"].rearrange("b (t p) e -> (b t) p e", p=P)
        xb_rows = d["x1b"].rearrange("(t p) e -> t p e", p=P)

        def wait(eng, sm, v):
            if not isinstance(v, int) or v > 0:
                eng.wait_ge(sm, v)

        def one(ap, t):
            return ap[bass.ds(t, 1)].rearrange("o p e -> (o p) e")

        def rounds(eng, tile):
            for t in range(2):
                tile(t, t)
            with eng.Fori(1, ROUNDS) as j:
                for u in range(2):
                    tile(2 * j + u, u)

        block = ctx.enter_context(nc.Block())

        @block.sync
        def _(sp):
            sp.dma_start(w_out[:], d["Wout"].rearrange("(k p) n -> p k n", p=P)).then_inc(consts_in, 16)
            sp.dma_start(bout[:], d["bout"].rearrange("(o n) -> o n", o=1).to_broadcast([P, E])).then_inc(consts_in, 16)
            sp.dma_start(bo[:], d["bo"].rearrange("(o n) -> o n", o=1).to_broadcast([P, E])).then_inc(consts_in, 16)

            def tile(t, u):
                wait(sp, sums, 4 * (t - 1))
                wait(sp, aT_made, t - 1)
                sp.dma_start(x[u][:], one(x_rows, t)).then_inc(x_in[u], 16)
                sp.dma_start(at[u][:], s["attn"][:, bass.ds(t, 1), :].rearrange("p o n -> p (o n)")).then_inc(x_in[u], 16)

            rounds(sp, tile)

        @block.gpsimd
        def _(pool):
            def tile(t, u):
                wait(pool, sums, 4 * (t - 1))
                slots = s["slot_get"][:].rearrange("p (k t) -> p k t", k=TOPK)
                pool.tensor_copy(at_slot[u][:], slots[:, :, bass.ds(t, 1)].rearrange("p k o -> p (k o)")).then_inc(picked, 1)
                pool.wait_ge(picked, 2 * t + 1)
                pool.tensor_copy(gate[u][:], s["gates"][:, :, bass.ds(t, 1)].rearrange("p k o -> p (k o)")).then_inc(picked, 1)
                for k in range(TOPK):
                    pool.indirect_dma_start(
                        out=ye[k][u][:], out_offset=None, in_=d["expert_out"],
                        in_offset=bass.IndirectOffsetOnAxis(ap=at_slot[u][:, k:k + 1], axis=0),
                    ).then_inc(rows_in[u], 16)

            rounds(pool, tile)

        @block.tensor
        def _(pe):
            pe.wait_ge(consts_in, 48)

            def project(t, u):
                pe.wait_ge(x_in[u], 32 * (t // 2 + 1))
                wait(pe, aT_ready, t - 1)
                for k in range(EC):
                    ins = pe.transpose(pA[u][:, k, :], at[u][:, k * P:(k + 1) * P], ident[:])
                ins.then_inc(aT_made, 1)
                pe.wait_ge(aT_ready, t + 1)
                wait(pe, sums, 4 * (t - 1))
                for k in range(EC):
                    ins = pe.matmul(pW[u][:], aT[u][:, k, :], w_out[:, k, :], start=(k == 0), stop=(k == EC - 1))
                ins.then_inc(w_made, 1)

            def route(t, u):
                pe.wait_ge(norm, 5 * t + 5)
                wait(pe, xnT_ready, t - 1)
                for k in range(EC):
                    ins = pe.transpose(pT[u][:, k, :], xn[u][:, k * P:(k + 1) * P], ident[:])
                ins.then_inc(xnT_made, 1)
                pe.wait_ge(xnT_ready, t + 1)
                wait(pe, logits_ready, t - 1)
                for k in range(EC):
                    ins = pe.matmul(pL[u][:], xnT[u][:, k, :], s["route"][:, k, :], start=(k == 0), stop=(k == EC - 1))
                ins.then_inc(logits_made, 1)

            project(0, 0)
            project(1, 1)
            route(0, 0)
            with pe.Fori(1, ROUNDS) as j:
                for u in range(2):
                    project(2 * j + u, u)
                    route(2 * j + u - 1, 1 - u)
            route(TILES - 1, 1)

        @block.scalar
        def _(act):
            def turned(t, u):
                act.wait_ge(aT_made, t + 1)
                wait(act, w_made, t - 1)
                act.copy(aT[u][:], pA[u][:]).then_inc(aT_ready, 1)

            def rest(t, u):
                act.wait_ge(norm, 5 * t + 3)
                act.activation(std[:], var_eps[:], ACT.Sqrt).then_inc(std_ready, 1)
                act.wait_ge(xnT_made, t + 1)
                wait(act, logits_made, t - 1)
                wait(act, xnT_out[u], 16 * (t // 2))
                act.copy(xnT[u][:], pT[u][:]).then_inc(xnT_ready, 1)
                act.wait_ge(xnT_ready, t + 1)
                dst = d["x1nT"][:, :, bass.ds(t * P, P)].rearrange("k p n -> p k n")
                act.dma_start(dst, xnT[u][:]).then_inc(xnT_out[u], 16)
                act.wait_ge(xb_ready, t + 1)
                act.dma_start(one(xb_rows, t), xb[u][:]).then_inc(xb_out[u], 16)

            turned(0, 0)
            turned(1, 1)
            rest(0, 0)
            with act.Fori(1, ROUNDS) as j:
                for u in range(2):
                    turned(2 * j + u, u)
                    if u == 0:
                        rest(2 * j - 1, 1)
                    else:
                        rest(2 * j, 0)
            rest(TILES - 1, 1)
            for u in range(2):
                act.wait_ge(xnT_out[u], 16 * ROUNDS)
                act.wait_ge(xb_out[u], 16 * ROUNDS)

        @block.vector
        def _(dve):
            dve.wait_ge(consts_in, 48)

            def total(t, u):
                dve.wait_ge(w_made, t + 1)
                dve.wait_ge(x_in[u], 32 * (t // 2 + 1))
                dve.tensor_tensor(part[u][:, 0], x[u][:], bout[:], ALU.add).then_inc(sums, 1)
                dve.wait_ge(sums, 4 * t + 1)
                dve.tensor_tensor(part[u][:, 1], pW[u][:], part[u][:, 0], ALU.add).then_inc(sums, 1)
                dve.wait_ge(sums, 4 * t + 2)
                dve.wait_ge(rows_in[u], 32 * (t // 2 + 1))
                dve.wait_ge(picked, 2 * t + 2)
                dve.scalar_tensor_tensor(part[u][:, 2], ye[0][u][:], gate[u][:, 0:1], part[u][:, 1], ALU.mult,
                                         ALU.add).then_inc(sums, 1)
                dve.wait_ge(sums, 4 * t + 3)
                wait(dve, xb_ready, t - 1)
                dve.scalar_tensor_tensor(x1[u][:], ye[1][u][:], gate[u][:, 1:2], part[u][:, 2], ALU.mult,
                                         ALU.add).then_inc(sums, 1)
                dve.wait_ge(sums, 4 * t + 4)
                wait(dve, xb_out[u], 16 * (t // 2))
                dve.tensor_tensor(xb[u][:], x1[u][:], bo[:], ALU.add).then_inc(xb_ready, 1)
                dve.bn_stats(stats[:], x1[u][:]).then_inc(norm, 1)
                dve.wait_ge(norm, 5 * t + 1)
                dve.memset(carrier[:], 0.0)
                dve.bn_aggr(mean_var[:], stats[:]).then_inc(norm, 1)
                dve.wait_ge(norm, 5 * t + 2)
                dve.tensor_scalar(var_eps[:], mean_var[:, 1:2], LN_EPS, None, ALU.add).then_inc(norm, 1)
                dve.wait_ge(std_ready, t + 1)
                dve.reciprocal(rstd[:], std[:]).then_inc(norm, 1)
                dve.wait_ge(norm, 5 * t + 4)
                wait(dve, xnT_made, t - 1)
                dve.tensor_scalar(xn[u][:], x1[u][:], mean_var[:, 0:1], rstd[:], ALU.subtract,
                                  ALU.mult).then_inc(norm, 1)

            def logits(t, u):
                dve.wait_ge(logits_made, t + 1)
                dst = s["logits"][:, bass.ds(t, 1), :].rearrange("p o n -> p (o n)")
                dve.tensor_copy(dst, pL[u][:]).then_inc(logits_ready, 1)

            total(0, 0)
            total(1, 1)
            logits(0, 0)
            with dve.Fori(1, ROUNDS) as j:
                for u in range(2):
                    total(2 * j + u, u)
                    logits(2 * j + u - 1, 1 - u)
            logits(TILES - 1, 1)


def weighting(nc, d, s):
    with ExitStack() as ctx:
        def sb(name, shape, dt=F32):
            return ctx.enter_context(nc.sbuf_tensor("wg_" + name, shape, dt))

        def sem(name):
            return ctx.enter_context(nc.semaphore("wg_" + name))

        biased = sb("biased", [P, TILES, NX])
        bias = sb("bias", [P, NX])
        iota = sb("iota", [P, NX])
        ones = sb("ones", [P, P])
        top = sb("top", [P, TILES, 8])
        top_at = sb("top_at", [P, TILES, 8], U32)
        expert = sb("expert", [P, TOPK, TILES])
        chosen = sb("chosen", [P, TOPK, TILES, NX])
        score = sb("score", [P, TOPK, TILES])
        both = sb("both", [P, TILES])
        both_eps = sb("both_eps", [P, TILES])
        inv = sb("inv", [P, TILES])
        share = sb("share", [P, TOPK, TILES])
        picked = sb("picked", [P, TILES, NX])
        shares = sb("shares", [P, TOPK, TILES, NX])
        shared_sum = sb("shared_sum", [P, TILES, NX])
        sums = sb("sums", [P, 2, NX])
        count = sb("count", [P, NX])
        inv_count = sb("inv_count", [P, NX])
        mean = sb("mean", [P, NX])
        pS = ctx.enter_context(nc.psum_tensor("wg_pS", [P, 2 * NX], F32))

        consts_in = sem("consts_in")
        ones_ready = sem("ones_ready")
        dve_step = sem("dve_step")
        scored = sem("scored")
        summed = sem("summed")
        after = {}
        block = ctx.enter_context(nc.Block())

        def over_experts(ap):
            return ap.unsqueeze(len(ap.shape)).to_broadcast(list(ap.shape) + [NX])

        def over_tiles(ap):
            return ap.unsqueeze(1).to_broadcast([P, TILES, NX])

        @block.sync
        def _(sp):
            sp.dma_start(iota[:], d["c_iota"]).then_inc(consts_in, 16)
            sp.dma_start(bias[:], d["lb_bias"].rearrange("(o n) -> o n", o=1).to_broadcast([P, NX])).then_inc(consts_in, 16)

        @block.gpsimd
        def _(pool):
            pool.memset(ones[:], 1.0).then_inc(ones_ready, 1)

        @block.vector
        def _(dve):
            st = Steps(dve, dve_step)
            dve.wait_ge(consts_in, 32)
            st.did(dve.tensor_tensor(biased[:], s["logits"][:], over_tiles(bias[:]), ALU.add))
            st.all_done()
            for t in range(TILES):
                st.did(dve.max(top[:, t], biased[:, t]))
            st.all_done()
            after["top"] = st.n
            for t in range(TILES):
                st.did(dve.max_index(top_at[:, t], top[:, t], biased[:, t]))
            st.all_done()
            for k in range(TOPK):
                st.did(dve.tensor_copy(expert[:, k], top_at[:, :, k]))
            st.all_done()
            for k in range(TOPK):
                st.did(dve.tensor_tensor(chosen[:, k], over_tiles(iota[:]), over_experts(expert[:, k]), ALU.is_equal))
            dve.wait_ge(scored, TOPK)
            st.did(dve.tensor_tensor(both[:], score[:, 0], score[:, 1], ALU.add))
            st.all_done()
            st.did(dve.tensor_scalar(both_eps[:], both[:], 1e-8, None, ALU.add))
            st.all_done()
            st.did(dve.reciprocal(inv[:], both_eps[:]))
            st.all_done()
            for k in range(TOPK):
                st.did(dve.tensor_tensor(share[:, k], score[:, k], inv[:], ALU.mult))
            st.did(dve.tensor_tensor(picked[:], chosen[:, 0], chosen[:, 1], ALU.add))
            st.all_done()
            for k in range(TOPK):
                st.did(dve.tensor_tensor(shares[:, k], chosen[:, k], over_experts(share[:, k]), ALU.mult))
            st.did(dve.tensor_reduce(sums[:, 0], picked[:].rearrange("p t e -> p e t"), AX.X, ALU.add))
            st.all_done()
            st.did(dve.tensor_tensor(shared_sum[:], shares[:, 0], shares[:, 1], ALU.add))
            st.all_done()
            st.did(dve.tensor_reduce(sums[:, 1], shared_sum[:].rearrange("p t e -> p e t"), AX.X, ALU.add))
            after["sums"] = st.n
            dve.wait_ge(summed, 1)
            st.did(dve.tensor_scalar(count[:], pS[:, 0:NX], 1.0, None, ALU.max))
            st.all_done()
            st.did(dve.reciprocal(inv_count[:], count[:]))
            st.all_done()
            st.did(dve.tensor_tensor(mean[:], pS[:, NX:2 * NX], inv_count[:], ALU.mult))
            st.all_done()
            st.did(dve.tensor_tensor(s["weight"][:], picked[:], over_tiles(mean[:]), ALU.mult))

        @block.scalar
        def _(act):
            act.wait_ge(dve_step, after["top"])
            for k in range(TOPK):
                act.activation(score[:, k], top[:, :, k], ACT.Sigmoid).then_inc(scored, 1)

        @block.tensor
        def _(pe):
            pe.wait_ge(ones_ready, 1)
            pe.wait_ge(dve_step, after["sums"])
            pe.matmul(pS[:], ones[:], sums[:].rearrange("p a e -> p (a e)"), start=True, stop=True).then_inc(summed, 1)


def layer1(nc, d, s):
    with ExitStack() as ctx:
        def sb(name, shape, dt=F32):
            return ctx.enter_context(nc.sbuf_tensor("l1_" + name, shape, dt))

        def pb(name, shape, dt=F32):
            return ctx.enter_context(nc.psum_tensor("l1_" + name, shape, dt))

        def sem(name):
            return ctx.enter_context(nc.semaphore("l1_" + name))

        ident = s["ident"]
        MLPS = NX + SI // I1
        ORDER = list(range(NX, MLPS)) + list(range(NX))
        ADDS = MLPS - 1
        PD = TPC // 2
        ZW = H * NPAT
        MIX, SCORE = 2, 6
        seg = sb("seg", [P, TPC * ZW])
        inv_k = sb("inv_k", [P, NPAT])
        xT = s["attn"][:].rearrange("p t e -> p (t e)").rearrange("p (k n) -> p k n", k=EC)
        xT_score = sb("xT_score", [P, EC, TPC, P])
        weight = [sb(f"weight{u}", [P, TPC, NX]) for u in range(2)]
        act_g = [sb(f"act_g{i}", [P, CH]) for i in range(2)]
        hT = [sb(f"hT{i}", [P, CH]) for i in range(2)]
        scaled = [sb(f"scaled{i}", [P, TPC, E]) for i in range(2)]
        sumy = [sb(f"sumy{u}", [P, TPC, E]) for u in range(2)]
        z = [sb(f"z{u}", [P, TPC, ZW]) for u in range(2)]
        order = [sb(f"order{i}", [P, TPC * ZW]) for i in range(2)]
        tau = sb("tau", [P, TPC * H])
        over = sb("over", [P, TPC, ZW])
        wts = sb("wts", [P, TPC, ZW])
        wT = [sb(f"wT{i}", [P, 4, P]) for i in range(2)]

        pG = [pb(f"G{i}", [P, CH]) for i in range(2)]
        pU = [pb(f"U{i}", [P, CH]) for i in range(2)]
        pD = [pb(f"D{i}", [P, 2, E]) for i in range(PD)]
        pZ = pb("Z", [P, ZW])
        pO = pb("O", [P, E])

        consts_in = sem("consts_in")
        xT_in = [sem(f"xT_in{b}") for b in range(B)]
        score_cols = sem("score_cols")
        base_in = [sem(f"base_in{u}") for u in range(2)]
        weight_ready = sem("weight_ready")
        gate_made = sem("gate_made")
        up_made = sem("up_made")
        act_ready = sem("act_ready")
        h_ready = sem("h_ready")
        down_made = sem("down_made")
        scale_step = sem("scale_step")
        sum_step = sem("sum_step")
        z_made = sem("z_made")
        z_ready = sem("z_ready")
        sort_step = sem("sort_step")
        over_ready = sem("over_ready")
        wts_ready = sem("wts_ready")
        wT_made = sem("wT_made")
        wT_ready = sem("wT_ready")
        ao_made = sem("ao_made")
        ao_ready = sem("ao_ready")
        stored = [sem(f"stored{u}") for u in range(2)]

        STAGES = []
        size = 2
        while size <= NPAT:
            STAGES.append((size, 0))
            dist = size // 4
            while dist:
                STAGES.append((2 * dist, dist))
                dist //= 2
            size *= 2
        SORTS = 2 * len(STAGES)
        SORT_STEPS = SORTS + 3
        ITEMS = len(STAGES) + 1
        partial = d["partial"].rearrange("(c t p) e -> c p t e", t=TPC, p=P)
        xb_rows = d["x1b"].rearrange("(c t p) e -> c p t e", t=TPC, p=P)

        def wait(eng, sm, v):
            if not isinstance(v, int) or v > 0:
                eng.wait_ge(sm, v)

        def one(ap, c):
            return ap[bass.ds(c, 1)].rearrange("o p t e -> (o p) t e")

        def rounds(eng, chunk):
            for c in range(2):
                chunk(c, c, 2)
            with eng.Fori(1, NCH // 2 - 1) as j:
                for u in range(2):
                    chunk(2 * j + u, u, 2)
            chunk(NCH - 2, 0, 1)
            chunk(NCH - 1, 1, 0)

        def first(c):
            return isinstance(c, int) and c == 0

        def buffer(u, i):
            return scaled[(ADDS * u + i - 1) % 2]

        block = ctx.enter_context(nc.Block())

        @block.sync
        def _(sp):
            sp.dma_start(seg[:], d["c_seg"]).then_inc(consts_in, 16)
            sp.dma_start(inv_k[:], d["c_inv_k"]).then_inc(consts_in, 16)

            for b in range(B):
                cols = slice(b * S, (b + 1) * S)
                sp.dma_start(xT[:, :, cols], d["x1nT"][:, :, cols].rearrange("k p n -> p k n")).then_inc(xT_in[b], 16)

            def load(c, u):
                wait(sp, stored[u], 16 * (c // 2))
                sp.dma_start(sumy[u][:], one(xb_rows, c)).then_inc(base_in[u], 16)

            def chunk(c, u, behind):
                if behind:
                    load(c + 1, 1 - u)
                sp.wait_ge(sum_step, ADDS * (c + 1))
                sp.dma_start(one(partial, c), sumy[u][:]).then_inc(stored[u], 16)

            load(0, 0)
            rounds(sp, chunk)
            for u in range(2):
                sp.wait_ge(stored[u], 16 * (NCH // 2))

        @block.gpsimd
        def _(pool):
            def above(c, u):
                pool.wait_ge(sort_step, SORT_STEPS * (c + 1))
                wait(pool, wts_ready, c)
                zv = z[u][:].rearrange("p t (h n) -> p (t h) n", n=NPAT)
                ov = over[:].rearrange("p t (h n) -> p (t h) n", n=NPAT)
                pool.tensor_tensor(ov, zv, tau[:].unsqueeze(2).to_broadcast([P, TPC * H, NPAT]),
                                   ALU.subtract).then_inc(over_ready, 1)

            def columns(c):
                wait(pool, z_made, TPC * c)
                cols = xT[:, :, bass.ds(c // NQ * S, S)].rearrange("p k (r j) -> p k j r", j=QT)
                for k in range(EC):
                    pool.tensor_copy(xT_score[:, k], cols[:, k, bass.ds(c % NQ * TPC, TPC), :]).then_inc(score_cols, 1)

            def add(c, u, i):
                n = ADDS * c + i - 1
                if i == 1:
                    pool.wait_ge(base_in[u], 16 * (c // 2 + 1))
                pool.wait_ge(scale_step, 2 * PD * (n + 1))
                wait(pool, sum_step, n)
                pool.tensor_tensor(sumy[u][:], sumy[u][:], buffer(u, i)[:], ALU.add).then_inc(sum_step, 1)

            def chunk(c, u, behind):
                wait(pool, sum_step, ADDS * (c - 1))
                pool.tensor_copy(weight[u][:], s["weight"][:, bass.ds(c * TPC, TPC), :]).then_inc(weight_ready, 1)
                if not first(c):
                    above(c - 1, 1 - u)
                for i in range(1, MLPS):
                    if i == 2 and behind:
                        columns(c + 1)
                    add(c, u, i)

            for b in range(B):
                pool.wait_ge(xT_in[b], 16)
            columns(0)
            rounds(pool, chunk)
            above(NCH - 1, 1)

        @block.tensor
        def _(pe):
            def scores(c, t):
                if t == 0:
                    pe.wait_ge(score_cols, EC * (c + 1))
                    wait(pe, wT_ready, TPC * (c - 1))
                wait(pe, z_ready, TPC * c + t)
                for k in range(EC):
                    ins = pe.matmul(pZ[:], xT_score[:, k, t, :], s["to_scores"][:, k, :],
                                    start=(k == 0), stop=(k == EC - 1))
                ins.then_inc(z_made, 1)

            def mix(c, t):
                if t == 0:
                    pe.wait_ge(wts_ready, c + 1)
                    last = isinstance(c, int) and c == NCH - 1
                    pe.wait_ge(z_ready, TPC * (NCH if last else c + 2))
                n = TPC * c + t
                wait(pe, wT_ready, n)
                for g in range(4):
                    ins = pe.transpose(pZ[:, g * P:(g + 1) * P], wts[:, t, g * P:(g + 1) * P], ident[:])
                ins.then_inc(wT_made, 1)
                pe.wait_ge(wT_ready, n + 1)
                wait(pe, ao_ready, n)
                for g in range(4):
                    ins = pe.matmul(pO[:, g * 4 * D:(g + 1) * 4 * D], wT[t % 2][:, g, :], s["values"][:, g, :],
                                    start=True, stop=True)
                ins.then_inc(ao_made, 1)

            def up(c, u, i):
                n, e = MLPS * c + i, ORDER[i]
                wait(pe, act_ready, n - 1)
                for k in range(EC):
                    ins = pe.matmul(pG[i % 2][:], s["gate_up"][:, e, k, :], xT[:, k, bass.ds(c * CH, CH)], start=(k == 0),
                                    stop=(k == EC - 1))
                ins.then_inc(gate_made, 1)
                wait(pe, h_ready, n - 1)
                for k in range(EC):
                    ins = pe.matmul(pU[i % 2][:], s["gate_up"][:, e, EC + k, :], xT[:, k, bass.ds(c * CH, CH)], start=(k == 0),
                                    stop=(k == EC - 1))
                ins.then_inc(up_made, 1)

            def down(c, i):
                if i == 0:
                    return
                halves = (0, 1) if i == 1 else (i,)
                pe.wait_ge(h_ready, MLPS * c + i + 1)
                for q in range(PD):
                    n = PD * (ADDS * c + i - 1) + q
                    wait(pe, scale_step, 2 * (n - PD + 1))
                    for t in range(2):
                        cols = slice((2 * q + t) * P, (2 * q + t + 1) * P)
                        for m in halves:
                            ins = pe.matmul(pD[q][:, t, :], hT[m % 2][:, cols], s["down"][:, ORDER[m], :],
                                            start=(m == halves[0]), stop=(m == halves[-1]))
                    ins.then_inc(down_made, 1)

            def chunk(c, u, behind):
                for i in range(MLPS):
                    up(c, u, i)
                    if MIX <= i < MIX + TPC and not first(c):
                        mix(c - 1, i - MIX)
                    if behind and SCORE <= i < SCORE + TPC:
                        scores(c + 1, i - SCORE)
                    if i:
                        down(c, i - 1)
                down(c, MLPS - 1)

            for b in range(B):
                pe.wait_ge(xT_in[b], 16)
            for t in range(TPC):
                scores(0, t)
            rounds(pe, chunk)
            for t in range(TPC):
                mix(NCH - 1, t)

        @block.scalar
        def _(act):
            def mixed(c, t):
                n = TPC * c + t
                act.wait_ge(wT_made, n + 1)
                wait(act, ao_made, n - 1)
                act.copy(wT[t % 2][:].rearrange("p g n -> p (g n)"), pZ[:]).then_inc(wT_ready, 1)
                act.wait_ge(ao_made, n + 1)
                dst = s["mixed"][:, bass.ds(n, 1), :].rearrange("p o n -> p (o n)")
                act.copy(dst, pO[:]).then_inc(ao_ready, 1)

            def relu(c):
                act.wait_ge(over_ready, c + 1)
                wait(act, wT_made, TPC * c)
                act.activation(wts[:], over[:], ACT.Relu).then_inc(wts_ready, 1)

            def scale(c, u, i):
                for q in range(PD):
                    n = ADDS * c + i - 1
                    act.wait_ge(down_made, PD * n + q + 1)
                    if q == 0:
                        wait(act, sum_step, n - 1)
                    if i == 1:
                        act.copy(buffer(u, i)[:, 2 * q:2 * q + 2, :], pD[q][:]).then_inc(scale_step, 2)
                        continue
                    if i == 2 and q == 0:
                        act.wait_ge(weight_ready, c + 1)
                    for t in range(2):
                        tt = 2 * q + t
                        act.activation(buffer(u, i)[:, tt, :], pD[q][:, t, :], ACT.Copy,
                                       scale=weight[u][:, tt, ORDER[i]:ORDER[i] + 1]).then_inc(scale_step, 1)

            def chunk(c, u, behind):
                for i in range(MLPS):
                    n = MLPS * c + i
                    act.wait_ge(gate_made, n + 1)
                    wait(act, h_ready, n - 1)
                    act.activation(act_g[i % 2][:], pG[i % 2][:], ACT.Silu).then_inc(act_ready, 1)
                    if not first(c):
                        if i == MIX - 1:
                            relu(c - 1)
                        if MIX <= i < MIX + TPC:
                            mixed(c - 1, i - MIX)
                    if i > 1:
                        scale(c, u, i - 1)
                scale(c, u, MLPS - 1)

            rounds(act, chunk)
            relu(NCH - 1)
            for t in range(TPC):
                mixed(NCH - 1, t)

        @block.vector
        def _(dve):
            dve.wait_ge(consts_in, 32)

            def keep_scores(c, u, t):
                dve.wait_ge(z_made, TPC * c + t + 1)
                if t == 0:
                    wait(dve, over_ready, c - 1)
                dve.tensor_tensor(z[u][:, t, :], pZ[:], s["score_bias"][:], ALU.add).then_inc(z_ready, 1)

            def sort(c, u, k):
                size, dist = STAGES[k]
                first = SORT_STEPS * c + 2 * k
                src = z[u][:].rearrange("p t n -> p (t n)") if k == 0 else order[(k - 1) % 2][:]
                sv = src.rearrange("p (b n) -> p b n", n=size)
                dv = order[k % 2][:].rearrange("p (b n) -> p b n", n=size)
                half = size // 2
                low, high = sv[:, :, 0:half], sv[:, :, half:size]
                if dist or half == 1:
                    low_m, high_m = low, high
                else:
                    low_m, high_m = sv[:, :, half - 1::-1], sv[:, :, size - 1:half - 1:-1]
                if k == 0:
                    dve.wait_ge(z_ready, TPC * c + TPC)
                wait(dve, sort_step, first)
                dve.tensor_tensor(dv[:, :, 0:half], low, high_m, ALU.max).then_inc(sort_step, 1)
                dve.tensor_tensor(dv[:, :, half:size], high, low_m, ALU.min).then_inc(sort_step, 1)

            def threshold(c):
                done = SORT_STEPS * c + SORTS
                top = order[(len(STAGES) - 1) % 2]
                run = order[len(STAGES) % 2]
                run_v, top_v = (a[:].rearrange("p (b n) -> p b n", n=NPAT) for a in (run, top))
                dve.wait_ge(sort_step, done)
                dve.tensor_tensor_scan(run[:], seg[:], top[:], 0.0, ALU.mult, ALU.add).then_inc(sort_step, 1)
                dve.wait_ge(sort_step, done + 1)
                dve.scalar_tensor_tensor(top_v, run_v, -1.0, inv_k[:].unsqueeze(1).to_broadcast([P, TPC * H, NPAT]),
                                         ALU.add, ALU.mult).then_inc(sort_step, 1)
                dve.wait_ge(sort_step, done + 2)
                wait(dve, over_ready, c)
                dve.tensor_reduce(tau[:], top_v, AX.X, ALU.max).then_inc(sort_step, 1)

            def hidden(c, i):
                n = MLPS * c + i
                dve.wait_ge(act_ready, n + 1)
                dve.wait_ge(up_made, n + 1)
                used = ADDS * c + (max(1, i - 2) if i >= 2 else i - 1)
                wait(dve, down_made, PD * used)
                dve.tensor_tensor(hT[i % 2][:], act_g[i % 2][:], pU[i % 2][:], ALU.mult).then_inc(h_ready, 1)

            def chunk(c, u, behind):
                for i in range(MLPS):
                    hidden(c, i)
                    for k in range(ITEMS * i // MLPS, ITEMS * (i + 1) // MLPS):
                        if k < len(STAGES):
                            sort(c, u, k)
                        else:
                            threshold(c)
                    if behind and SCORE <= i < SCORE + TPC:
                        keep_scores(c + 1, 1 - u, i - SCORE)

            for t in range(TPC):
                keep_scores(0, 0, t)
            rounds(dve, chunk)


def finish(nc, d, s):
    with ExitStack() as ctx:
        def sb(name, shape, dt=F32):
            return ctx.enter_context(nc.sbuf_tensor("fi_" + name, shape, dt))

        def pb(name, shape, dt=F32):
            return ctx.enter_context(nc.psum_tensor("fi_" + name, shape, dt))

        def sem(name):
            return ctx.enter_context(nc.semaphore("fi_" + name))

        ident = s["ident"]
        wo = sb("wo", [P, EC, E])
        head = [sb(f"head{u}", [P, E]) for u in range(2)]
        part = [sb(f"part{u}", [P, E]) for u in range(2)]
        hT = [sb(f"hT{u}", [P, EC, P]) for u in range(2)]
        res = [sb(f"res{u}", [P, E]) for u in range(2)]
        pT = [pb(f"T{u}", [P, EC, P]) for u in range(2)]
        pO = [pb(f"O{u}", [P, E]) for u in range(2)]
        wo_in = sem("wo_in")
        part_in = [sem(f"part_in{u}") for u in range(2)]
        head_ready = sem("head_ready")
        hT_made = sem("hT_made")
        hT_ready = sem("hT_ready")
        o_made = sem("o_made")
        res_ready = sem("res_ready")
        stored = [sem(f"stored{u}") for u in range(2)]
        ROUNDS = TILES // 2
        part_rows = d["partial"].rearrange("(t p) e -> t p e", p=P)
        out_rows = d["out"].rearrange("b (t p) e -> (b t) p e", p=P)

        def wait(eng, sm, v):
            if not isinstance(v, int) or v > 0:
                eng.wait_ge(sm, v)

        def one(ap, t):
            return ap[bass.ds(t, 1)].rearrange("o p e -> (o p) e")

        def rounds(eng, tile):
            for t in range(2):
                tile(t, t)
            with eng.Fori(1, ROUNDS) as j:
                for u in range(2):
                    tile(2 * j + u, u)

        block = ctx.enter_context(nc.Block())

        @block.sync
        def _(sp):
            sp.dma_start(wo[:], d["Wo"].rearrange("(k p) n -> p k n", p=P)).then_inc(wo_in, 16)

            def store(t, u):
                sp.wait_ge(res_ready, t + 1)
                sp.dma_start(one(out_rows, t), res[u][:]).then_inc(stored[u], 16)

            for t in range(2):
                sp.dma_start(part[t][:], one(part_rows, t)).then_inc(part_in[t], 16)
            with sp.Fori(1, ROUNDS) as j:
                for u in range(2):
                    store(2 * j + u - 2, u)
                    sp.dma_start(part[u][:], one(part_rows, 2 * j + u)).then_inc(part_in[u], 16)
            for u in range(2):
                store(TILES - 2 + u, u)
            for u in range(2):
                sp.wait_ge(stored[u], 16 * ROUNDS)

        @block.gpsimd
        def _(pool):
            def tile(t, u):
                wait(pool, hT_made, t - 1)
                src = s["mixed"][:, bass.ds(t // H * QT, QT), bass.ds(t % H * D, D)]
                pool.tensor_copy(head[u][:].rearrange("p (j n) -> p j n", n=D), src).then_inc(head_ready, 1)

            rounds(pool, tile)

        @block.tensor
        def _(pe):
            pe.wait_ge(wo_in, 16)

            def tile(t, u):
                pe.wait_ge(head_ready, t + 1)
                wait(pe, hT_ready, t - 1)
                for k in range(EC):
                    ins = pe.transpose(pT[u][:, k, :], head[u][:, k * P:(k + 1) * P], ident[:])
                ins.then_inc(hT_made, 1)
                pe.wait_ge(hT_ready, t + 1)
                wait(pe, res_ready, t - 1)
                for k in range(EC):
                    ins = pe.matmul(pO[u][:], hT[u][:, k, :], wo[:, k, :], start=(k == 0), stop=(k == EC - 1))
                ins.then_inc(o_made, 1)

            rounds(pe, tile)

        @block.scalar
        def _(act):
            def tile(t, u):
                act.wait_ge(hT_made, t + 1)
                wait(act, o_made, t - 1)
                act.copy(hT[u][:], pT[u][:]).then_inc(hT_ready, 1)

            rounds(act, tile)

        @block.vector
        def _(dve):
            def tile(t, u):
                dve.wait_ge(o_made, t + 1)
                dve.wait_ge(part_in[u], 16 * (t // 2 + 1))
                wait(dve, stored[u], 16 * (t // 2))
                dve.tensor_tensor(res[u][:], pO[u][:], part[u][:], ALU.add).then_inc(res_ready, 1)

            rounds(dve, tile)


def build(nc, d):
    with ExitStack() as ctx:
        for name, shape, dt in (
            ("xn", [NT, E], F32), ("v", [NCH, KVH, P, TPC * VW], F32),
            ("q_parts", [PARTS, H * D, NT], BF16), ("k_parts", [PARTS, KVH * D, NT], BF16),
            ("buf", [SLOTS, E], F32), ("expert_out", [SLOTS, E], F32),
            ("x1b", [NT, E], F32), ("x1nT", [EC, P, NT], F32),
            ("partial", [NT, E], F32),
        ):
            d[name] = nc.dram_tensor(name, shape, dt, kind="Internal").ap()
        s = {}

        def keep(name, shape, dt=F32):
            s[name] = ctx.enter_context(nc.sbuf_tensor("s_" + name, shape, dt))

        keep("ident", [P, P])
        keep("logits", [P, TILES, NX])
        keep("gates", [P, TOPK, TILES])
        keep("slot_get", [P, TOPK * TILES], U32)
        keep("slot_put", [P, TOPK * TILES], U32)
        keep("attn", [P, TILES, E])
        keep("gate_up", [P, NX + SI // I1, 2 * EC, I1])
        keep("down", [P, NX + SI // I1, E])
        keep("route", [P, EC, NX])
        keep("to_scores", [P, EC, H * NPAT])
        keep("score_bias", [P, H * NPAT])
        keep("values", [P, 4, 4 * D])
        keep("weight", [P, TILES, NX])
        latents(nc, d, s)
        routing(nc, d, s)
        attention(nc, d, s)
        layer1_weights(nc, d, s)
        experts(nc, d, s)
        mixing(nc, d, s)
        weighting(nc, d, s)
        keep("mixed", [P, TILES, E])
        layer1(nc, d, s)
        finish(nc, d, s)


_NAMES = {
    "x": "L0_attn_x", "Wqa": "L0_attn_Wqa", "Wqb": "L0_attn_Wqb", "Wkva": "L0_attn_Wkva", "Wkvb": "L0_attn_Wkvb",
    "Wout": "L0_attn_Wout", "bout": "L0_attn_bout", "Wg": "L0_ffn_Wg", "W_in": "L0_ffn_W_in", "W_out": "L0_ffn_W_out",
    "key_param": "L1_attn_key_param", "Wq": "L1_attn_Wq", "bq": "L1_attn_bq", "Wk": "L1_attn_Wk", "bk": "L1_attn_bk",
    "Wv": "L1_attn_Wv", "bv": "L1_attn_bv", "Wo": "L1_attn_Wo", "bo": "L1_attn_bo", "gate_w": "L1_ffn_gate_w",
    "lb_bias": "L1_ffn_lb_bias", "expert_gate_w": "L1_ffn_expert_gate_w", "expert_up_w": "L1_ffn_expert_up_w",
    "expert_down_w": "L1_ffn_expert_down_w", "shared_gate_w": "L1_ffn_shared_gate_w",
    "shared_up_w": "L1_ffn_shared_up_w", "shared_down_w": "L1_ffn_shared_down_w",
}


def constants():
    import numpy as np

    f = np.float32
    at = np.arange(P)
    freq = (f(1.0) / f(10000.0) ** (np.arange(0, D, 2, dtype=f) / f(D))).astype(f)
    angle = np.outer(np.arange(S, dtype=f), freq).astype(f)[:, at % D // 2].T
    sign = np.where(at % 2 == 0, f(-1), f(1))[:, None]
    hide = np.where(at[None, :] > at[:, None], f(NEG), f(0))
    diag = (at[:, None] // D == np.arange(8)[None, :]).astype(f)
    return {
        "c_cos": np.ascontiguousarray(np.cos(angle).astype(f)),
        "c_sin": np.ascontiguousarray((np.sin(angle) * sign).astype(f)),
        "c_ident": np.eye(P, dtype=f),
        "c_iota": np.tile(np.arange(NX, dtype=f), (P, 1)),
        "c_below": (at[:, None] < at[None, :]).astype(f),
        "c_hide_q": hide,
        "c_hide_k": np.ascontiguousarray(hide.T),
        "c_diag": np.repeat(diag[:, :, None], NPAT, axis=2),
        "c_diag_v": np.repeat((at[:, None] // NPAT == np.arange(4)[None, :]).astype(f)[:, :, None], D, axis=2),
        "c_seg": np.tile((np.arange(TPC * H * NPAT) % NPAT != 0).astype(f), (P, 1)),
        "c_inv_k": np.tile((f(1) / np.arange(1, NPAT + 1, dtype=f)).astype(f), (P, 1)),
    }


def kernel(**inputs):
    import numpy as np
    import concourse.bacc as bacc
    from concourse.bass_utils import run_bass_kernel_spmd

    nc = bacc.Bacc("TRN2", target_bir_lowering=False, num_devices=1)
    arrays, d = {}, {}
    for name, a in [(n, np.ascontiguousarray(inputs[full])) for n, full in _NAMES.items()] + list(constants().items()):
        arrays["in_" + name] = a
        d[name] = nc.dram_tensor("in_" + name, a.shape, mybir.dt.from_np(a.dtype), kind="ExternalInput").ap()
    d["out"] = nc.dram_tensor("out_0", (B, S, E), F32, kind="ExternalOutput").ap()
    build(nc, d)
    r = run_bass_kernel_spmd(nc, [arrays], core_ids=[0])
    return r.results[0]["out_0"]
```

```python
from contextlib import ExitStack

import concourse.bass as bass
from concourse import mybir

F32 = mybir.dt.float32
F32R = mybir.dt.float32r
BF16 = mybir.dt.bfloat16
U32 = mybir.dt.uint32
ALU = mybir.AluOpType
ACT = mybir.ActivationFunctionType
AX = mybir.AxisListType

P = 128
B, S, E = 2, 2048, 256
NT = B * S
TILES = NT // P
EC = E // P
CH = 512
NCH = NT // CH
TPC = CH // P
H, KVH, D = 16, 4, 16
QL, KVL = 64, 32
NX, TOPK, F = 8, 2, 512
CAP = -(-TOPK * NT * 5 // (NX * 4))
SLOTS = NX * CAP
NPAT = 32
I1, SI = 128, 256
LN_EPS = 1e-5
LAT = QL + KVL
COMB = LAT + NX
NEG = -1.0e30
PARTS = 3
VW = 32
RUNS = ((0, 3), (3, 2), (5, 1))
STACK = 6 * D
TERMS = ((0, 0), (0, 1), (1, 0))
NQ = S // CH
QT = S // P
HEADS = B * H



class Steps:

    def __init__(self, eng, sem):
        self.eng, self.sem, self.n = eng, sem, 0

    def did(self, ins):
        ins.then_inc(self.sem, 1)
        self.n += 1

    def all_done(self):
        self.eng.wait_ge(self.sem, self.n)


def latents(nc, d, s):
    with ExitStack() as ctx:
        def sb(name, shape, dt=F32):
            return ctx.enter_context(nc.sbuf_tensor(name, shape, dt))

        def pb(name, shape, dt=F32):
            return ctx.enter_context(nc.psum_tensor(name, shape, dt))

        def sem(name):
            return ctx.enter_context(nc.semaphore("lat_" + name))

        ident = s["ident"]
        logits = s["logits"]
        wcomb = sb("wcomb", [P, EC, COMB])
        wqb = sb("wqb", [QL, H * D])
        wqb_swap = sb("wqb_swap", [QL, H * D])
        wkvb = sb("wkvb", [LAT, KVH * D, 2])
        wk = sb("wk", [LAT, KVH * D])
        wk_swap = sb("wk_swap", [LAT, KVH * D])
        wv = sb("wv", [LAT, KVH * D])
        cos = sb("cos", [P, S])
        sin = sb("sin", [P, S])
        x = [sb(f"x{u}", [P, TPC, E]) for u in range(2)]
        stats = sb("stats", [P, TPC, 6])
        carrier = sb("carrier", [P, 1])
        mean_var = sb("mean_var", [P, TPC, 2])
        var_eps = sb("var_eps", [P, TPC])
        std = sb("std", [P, TPC])
        rstd = sb("rstd", [P, TPC])
        xn = [sb(f"xn{u}", [P, TPC, E]) for u in range(2)]
        xnT = [sb(f"xnT{u}", [P, EC, CH]) for u in range(2)]
        comb = [sb(f"comb{u}", [COMB, CH]) for u in range(2)]
        by_cos = [sb(f"by_cos{k}", [P, CH]) for k in range(3)]
        by_sin = [sb(f"by_sin{k}", [P, CH]) for k in range(3)]
        rot = [sb(f"rot{k}", [P, CH]) for k in range(3)]
        rest = [sb(f"rest{k}", [P, CH]) for k in range(3)]
        parts = [sb(f"parts{k}", [P, PARTS, CH], BF16) for k in range(3)]
        vtok = [sb(f"vtok{u}", [P, KVH, TPC, VW]) for u in range(2)]

        zeros = sb("zeros", [P, 8 * E])

        pT = pb("pT", [P, EC, CH])
        pC = pb("pC", [COMB, CH])
        pR = [pb(f"pR{m}", [P, 2, CH]) for m in range(2)]
        pM = pb("pM", [P, 512])
        pV = pM[:, 0:TPC * KVH * D].rearrange("p (t n) -> p t n", t=TPC)
        pL = pT[:, 0, 0:TPC * NX].rearrange("p (t n) -> p t n", t=TPC)

        weights_in = sem("weights_in")
        tables_in = sem("tables_in")
        swapped = sem("swapped")
        x_in = [sem(f"x_in{u}") for u in range(2)]
        stats_ready = sem("stats_ready")
        var_ready = sem("var_ready")
        std_ready = sem("std_ready")
        rstd_ready = sem("rstd_ready")
        xn_ready = sem("xn_ready")
        xn_out = [sem(f"xn_out{u}") for u in range(2)]
        xnT_made = sem("xnT_made")
        xnT_ready = sem("xnT_ready")
        comb_made = sem("comb_made")
        comb_ready = sem("comb_ready")
        vl_made = sem("vl_made")
        vl_ready = sem("vl_ready")
        v_filled = sem("v_filled")
        zeros_ready = sem("zeros_ready")
        buf_blank = sem("buf_blank")
        v_out = [sem(f"v_out{u}") for u in range(2)]
        pair_made = sem("pair_made")
        pair_used = sem("pair_used")
        rot_ready = sem("rot_ready")
        high_ready = sem("high_ready")
        rest_ready = sem("rest_ready")
        mid_ready = sem("mid_ready")
        low_ready = sem("low_ready")
        parts_out = [sem(f"parts_out{k}") for k in range(3)]

        PAIRS = 3
        ROUNDS = NCH // 2
        x_rows = d["x"].rearrange("b (c t p) e -> (b c) p t e", t=TPC, p=P)
        xn_rows = d["xn"].rearrange("(c t p) e -> c p t e", t=TPC, p=P)

        def one(ap, c):
            return ap[bass.ds(c, 1)].rearrange("o p t e -> (o p) t e")

        def rounds(eng, chunk):
            with eng.Fori(0, ROUNDS - 2) as j:
                for u in range(2):
                    chunk(2 * j + u, u, 4)
            for c in range(NCH - 4, NCH):
                chunk(c, c % 2, NCH - 1 - c)

        def rows_of(k):
            return P if k < 2 else KVH * D

        block = ctx.enter_context(nc.Block())

        @block.sync
        def _(sp):
            for u in range(2):
                sp.dma_start(x[u][:], x_rows[u]).then_inc(x_in[u], 16)
            sp.dma_start(ident[:], d["c_ident"]).then_inc(weights_in, 16)
            for dst, src in (
                (wcomb[:, :, 0:QL], d["Wqa"].rearrange("(k p) n -> p k n", p=P)),
                (wcomb[:, :, QL:LAT], d["Wkva"].rearrange("(k p) n -> p k n", p=P)),
                (wcomb[:, :, LAT:COMB], d["Wg"].rearrange("(k p) n -> p k n", p=P)),
                (wqb[:], d["Wqb"]),
                (wkvb[QL:LAT], d["Wkvb"].rearrange("k (n two) -> k n two", two=2)),
            ):
                sp.dma_start(dst, src).then_inc(weights_in, 16)
            sp.dma_start(cos[:], d["c_cos"]).then_inc(tables_in, 16)
            sp.dma_start(sin[:], d["c_sin"]).then_inc(tables_in, 16)
            for u in range(2):
                sp.sem_inc(xn_out[u], 16)
                sp.sem_inc(v_out[u], 16)
            for k in range(PAIRS):
                sp.sem_inc(parts_out[k], 16)

            def xn_store(c, u, load):
                sp.wait_ge(xn_ready, 4 * c + 4)
                if load:
                    sp.dma_start(x[u][:], one(x_rows, c + 2)).then_inc(x_in[u], 16)
                sp.dma_start(one(xn_rows, c), xn[u][:]).then_inc(xn_out[u], 16)

            def chunk(c, u, behind):
                if behind >= 2:
                    xn_store(c + 2, u, behind == 4)
                sp.wait_ge(vl_ready, 2 * c + 4)
                sp.dma_start(d["v"][bass.ds(c, 1)].rearrange("o h p n -> p (o h) n"),
                             vtok[u][:].rearrange("p h t n -> p h (t n)")).then_inc(v_out[u], 16)
                for k in range(PAIRS):
                    sp.wait_ge(low_ready, PAIRS * c + k + 1)
                    dst = d["q_parts"][:, k * P:(k + 1) * P] if k < 2 else d["k_parts"]
                    sp.dma_start(dst[:, :, bass.ds(c * CH, CH)].rearrange("a p n -> p a n"),
                                 parts[k][0:rows_of(k)]).then_inc(parts_out[k], 16)

            for c in range(2):
                xn_store(c, c, True)
            rounds(sp, chunk)
            for u in range(2):
                sp.wait_ge(xn_out[u], 16 * (ROUNDS + 1))
                sp.wait_ge(v_out[u], 16 * (ROUNDS + 1))
            for k in range(PAIRS):
                sp.wait_ge(parts_out[k], 16 * (NCH + 1))

        @block.gpsimd
        def _(pool):
            pool.memset(zeros[:], 0.0).then_inc(zeros_ready, 1)
            pool.wait_ge(zeros_ready, 1)
            blank = d["buf"].rearrange("(a p r) e -> a p (r e)", p=P, r=8)
            for a in range(SLOTS // P // 8):
                pool.dma_start(blank[a], zeros[:]).then_inc(buf_blank, 16)

            def turned(c, k):
                pool.wait_ge(pair_used, 2 * (PAIRS * c + k) + 6)
                rows = rows_of(k)
                pool.tensor_tensor(rot[k][0:rows], by_cos[k][0:rows], by_sin[k][0:rows], ALU.add).then_inc(rot_ready, 1)

            def left(c, k):
                pool.wait_ge(high_ready, PAIRS * c + k + 1)
                rows = rows_of(k)
                pool.tensor_tensor(rest[k][0:rows], rot[k][0:rows], parts[k][0:rows, 0],
                                   ALU.subtract).then_inc(rest_ready, 1)

            def chunk(c, u, behind):
                turned(c, 0)
                for k in range(1, PAIRS):
                    turned(c, k)
                    left(c, k - 1)
                left(c, PAIRS - 1)

            rounds(pool, chunk)
            pool.wait_ge(buf_blank, 16 * (SLOTS // P // 8))

        @block.scalar
        def _(act):
            def std_of(c):
                act.wait_ge(var_ready, 5 * c + 5)
                act.activation(std[:], var_eps[:], ACT.Sqrt).then_inc(std_ready, 1)

            def xnT_copy(c, u):
                act.wait_ge(xnT_made, c + 1)
                act.copy(xnT[u][:, 0], pT[:, 0]).then_inc(xnT_ready, 1)
                act.copy(xnT[u][:, 1], pT[:, 1]).then_inc(xnT_ready, 1)

            def comb_copy(c, u):
                act.wait_ge(comb_made, c + 1)
                act.copy(comb[u][:], pC[:]).then_inc(comb_ready, 1)

            def high(c, k):
                act.wait_ge(rot_ready, PAIRS * c + k + 1)
                act.wait_ge(parts_out[k], 16 * (c + 1))
                act.copy(parts[k][0:rows_of(k), 0], rot[k][0:rows_of(k)]).then_inc(high_ready, 1)

            def mid(c, k):
                act.wait_ge(rest_ready, PAIRS * c + k + 1)
                act.copy(parts[k][0:rows_of(k), 1], rest[k][0:rows_of(k)]).then_inc(mid_ready, 1)

            def chunk(c, u, behind):
                high(c, 0)
                if behind:
                    xnT_copy(c + 1, 1 - u)
                high(c, 1)
                mid(c, 0)
                if behind:
                    comb_copy(c + 1, 1 - u)
                high(c, 2)
                mid(c, 1)
                if behind >= 2:
                    std_of(c + 2)
                mid(c, PAIRS - 1)

            std_of(0)
            act.wait_ge(weights_in, 16 * 6)
            q_pair = wqb[:].rearrange("k (n two) -> k n two", two=2)
            q_swap = wqb_swap[:].rearrange("k (n two) -> k n two", two=2)
            k_pair = wkvb[QL:LAT, :, 0].rearrange("k (n two) -> k n two", two=2)
            k_swap = wk_swap[QL:LAT].rearrange("k (n two) -> k n two", two=2)
            for dst, src in (
                (q_swap[:, :, 0], q_pair[:, :, 1]), (q_swap[:, :, 1], q_pair[:, :, 0]),
                (k_swap[:, :, 0], k_pair[:, :, 1]), (k_swap[:, :, 1], k_pair[:, :, 0]),
                (wk[QL:LAT], wkvb[QL:LAT, :, 0]), (wv[QL:LAT], wkvb[QL:LAT, :, 1]),
            ):
                act.copy(dst, src).then_inc(swapped, 1)
            std_of(1)
            xnT_copy(0, 0)
            comb_copy(0, 0)
            rounds(act, chunk)

        @block.tensor
        def _(pe):
            def turn(c, u):
                pe.wait_ge(xn_ready, 4 * c + 4)
                pe.wait_ge(xnT_ready, 2 * c + 2)
                if not isinstance(c, int) or c:
                    pe.wait_ge(vl_ready, 2 * c)
                for t in range(TPC):
                    for k in range(EC):
                        ins = pe.transpose(pT[:, k, t * P:(t + 1) * P], xn[u][:, t, k * P:(k + 1) * P], ident[:])
                ins.then_inc(xnT_made, 1)

            def combined(c, u):
                pe.wait_ge(xnT_ready, 2 * c + 4)
                pe.wait_ge(comb_ready, c + 1)
                for k in range(EC):
                    ins = pe.matmul(pC[:], wcomb[:, k, :], xnT[u][:, k, :], start=(k == 0), stop=(k == EC - 1))
                ins.then_inc(comb_made, 1)

            def pair(c, u, k):
                n, m = PAIRS * c + k, (PAIRS * u + k) % 2
                pe.wait_ge(pair_used, 2 * n + 2)
                for a in range(2):
                    w = (wqb, wqb_swap)[a][:, k * P:(k + 1) * P] if k < 2 else (wk, wk_swap)[a][QL:LAT]
                    rows = slice(0, QL) if k < 2 else slice(QL, LAT)
                    ins = pe.matmul(pR[m][0:rows_of(k), a], w, comb[u][rows, :], start=True, stop=True)
                ins.then_inc(pair_made, 1)

            def v_and_logits(c, u):
                pe.wait_ge(vl_ready, 2 * c + 2)
                for t in range(TPC):
                    pe.matmul(pV[:, t, :], comb[u][QL:LAT, t * P:(t + 1) * P], wv[QL:LAT, :], start=True, stop=True)
                for t in range(TPC):
                    cols = slice(t * P, (t + 1) * P)
                    ins = pe.transpose(pL[:, t, :], comb[u][LAT:COMB, cols], ident[LAT:COMB, LAT:COMB])
                ins.then_inc(vl_made, 1)

            def chunk(c, u, behind):
                pe.wait_ge(comb_ready, c + 2)
                pair(c, u, 0)
                pair(c, u, 1)
                if behind:
                    turn(c + 1, 1 - u)
                pair(c, u, 2)
                if behind:
                    combined(c + 1, 1 - u)
                v_and_logits(c, u)

            pe.sem_inc(xnT_ready, 2)
            pe.sem_inc(comb_ready, 1)
            pe.sem_inc(vl_ready, 2)
            pe.sem_inc(pair_used, 4)
            pe.wait_ge(weights_in, 16 * 6)
            turn(0, 0)
            combined(0, 0)
            pe.wait_ge(swapped, 6)
            rounds(pe, chunk)

        @block.vector
        def _(dve):
            def statistics(c, u, x_loads):
                dve.wait_ge(x_in[u], 16 * x_loads)
                for t in range(TPC):
                    dve.bn_stats(stats[:, t], x[u][:, t]).then_inc(stats_ready, 1)

            def variances(c):
                dve.wait_ge(stats_ready, 4 * c + 4)
                dve.memset(carrier[:], 0.0)
                for t in range(TPC):
                    dve.bn_aggr(mean_var[:, t], stats[:, t]).then_inc(var_ready, 1)
                dve.wait_ge(var_ready, 5 * c + 4)
                dve.tensor_scalar(var_eps[:], mean_var[:, :, 1], LN_EPS, None, ALU.add).then_inc(var_ready, 1)

            def normalise(c, u, x_loads):
                dve.wait_ge(std_ready, c + 1)
                dve.reciprocal(rstd[:], std[:]).then_inc(rstd_ready, 1)
                dve.wait_ge(rstd_ready, c + 1)
                dve.wait_ge(xn_out[u], 16 * x_loads)
                for t in range(TPC):
                    dve.tensor_scalar(xn[u][:, t], x[u][:, t], mean_var[:, t, 0:1], rstd[:, t:t + 1],
                                      ALU.subtract, ALU.mult).then_inc(xn_ready, 1)

            def products(c, u, k):
                n, m = PAIRS * c + k, (PAIRS * u + k) % 2
                rows = rows_of(k)
                at = bass.ds(c % NQ * CH, CH)
                dve.wait_ge(pair_made, n + 1)
                dve.tensor_tensor(by_cos[k][0:rows], pR[m][0:rows, 0], cos[0:rows, at], ALU.mult).then_inc(pair_used, 1)
                dve.tensor_tensor(by_sin[k][0:rows], pR[m][0:rows, 1], sin[0:rows, at], ALU.mult).then_inc(pair_used, 1)

            def low(c, k):
                dve.wait_ge(mid_ready, PAIRS * c + k + 1)
                dve.tensor_tensor(parts[k][0:rows_of(k), 2], rest[k][0:rows_of(k)], parts[k][0:rows_of(k), 1],
                                  ALU.subtract).then_inc(low_ready, 1)

            def chunk(c, u, behind):
                products(c, u, 0)
                products(c, u, 1)
                products(c, u, 2)
                ahead = behind >= 2
                if ahead:
                    statistics(c + 2, u, c // 2 + 2)
                low(c, 0)
                if ahead:
                    variances(c + 2)
                low(c, 1)
                if ahead:
                    normalise(c + 2, u, c // 2 + 2)
                low(c, 2)
                dve.wait_ge(vl_made, c + 1)
                dve.wait_ge(v_out[u], 16 * (c // 2) + 16)
                dve.tensor_copy(vtok[u][:, :, :, 0:D],
                                pV.rearrange("p t (h n) -> p h t n", h=KVH)).then_inc(vl_ready, 1)
                dve.tensor_copy(logits[:, bass.ds(c * TPC, TPC), :], pL).then_inc(vl_ready, 1)

            for u in range(2):
                dve.memset(vtok[u][:], 0.0).then_inc(v_filled, 1)
                dve.wait_ge(v_filled, 2 * u + 1)
                dve.memset(vtok[u][:, :, :, D:D + 1], 1.0).then_inc(v_filled, 1)
            dve.wait_ge(v_filled, 4)
            for c in range(2):
                statistics(c, c, 1)
                if c:
                    dve.wait_ge(xn_ready, 4 * c)
                variances(c)
                normalise(c, c, 1)
            dve.wait_ge(tables_in, 32)
            rounds(dve, chunk)


def routing(nc, d, s):
    with ExitStack() as ctx:
        def sb(name, shape, dt=F32):
            return ctx.enter_context(nc.sbuf_tensor("rt_" + name, shape, dt))

        def pb(name, shape, dt=F32):
            return ctx.enter_context(nc.psum_tensor("rt_" + name, shape, dt))

        def sem(name):
            return ctx.enter_context(nc.semaphore("rt_" + name))

        logits, gates = s["logits"], s["gates"]
        top = sb("top", [P, TILES, 8])
        top_at = sb("top_at", [P, TILES, 8], U32)
        expert = sb("expert", [P, TOPK, TILES])
        iota = sb("iota", [P, NX])
        below = sb("below", [P, P])
        ones = sb("ones", [P, P])
        chosen = sb("chosen", [P, TOPK, TILES, NX])
        shifted = sb("shifted", [P, TILES, NX])
        exps = sb("exps", [P, TILES, NX])
        total = sb("total", [P, TILES])
        inv = sb("inv", [P, TILES])
        top_shift = sb("top_shift", [P, TOPK, TILES])
        top_exp = sb("top_exp", [P, TOPK, TILES])
        prob = sb("prob", [P, TOPK, TILES])
        tile_count = sb("tile_count", [P, TOPK * TILES, NX])
        run_count = sb("run_count", [P, TOPK * TILES, NX])
        before = sb("before", [P, TOPK * TILES, NX])
        ahead = sb("ahead", [P, TOPK * TILES, NX])
        loc = sb("loc", [P, TOPK * TILES])
        keep = sb("keep", [P, TOPK * TILES])
        drop = sb("drop", [P, TOPK * TILES])
        slot = sb("slot", [P, TOPK * TILES])
        slot_low = sb("slot_low", [P, TOPK * TILES])
        slot_put = sb("slot_put", [P, TOPK * TILES])
        kept = sb("kept", [P, TOPK * TILES])
        denom = sb("denom", [P, TILES])
        denom_low = sb("denom_low", [P, TILES])
        inv_denom = sb("inv_denom", [P, TILES])
        pB = pb("p_before", [P, TOPK * TILES * NX])
        pN = pb("p_count", [P, TOPK * TILES * NX])

        consts_in = sem("consts_in")
        ones_ready = sem("ones_ready")
        dve_step = sem("dve_step")
        exp_ready = sem("exp_ready")
        counted = sem("counted")
        FAR = float(1 << 20)

        block = ctx.enter_context(nc.Block())
        after = {}

        def over_experts(ap):
            return ap.unsqueeze(len(ap.shape)).to_broadcast(list(ap.shape) + [NX])

        @block.sync
        def _(sp):
            sp.dma_start(iota[:], d["c_iota"]).then_inc(consts_in, 16)
            sp.dma_start(below[:], d["c_below"]).then_inc(consts_in, 16)

        @block.gpsimd
        def _(pool):
            pool.memset(ones[:], 1.0).then_inc(ones_ready, 1)

        @block.vector
        def _(dve):
            st = Steps(dve, dve_step)
            for t in range(TILES):
                st.did(dve.max(top[:, t], logits[:, t]))
            st.all_done()
            for t in range(TILES):
                st.did(dve.max_index(top_at[:, t], top[:, t], logits[:, t]))
            st.did(dve.tensor_tensor(shifted[:], logits[:], over_experts(top[:, :, 0]), ALU.subtract))
            for k in range(TOPK):
                st.did(dve.tensor_tensor(top_shift[:, k], top[:, :, k], top[:, :, 0], ALU.subtract))
            after["shifts"] = st.n
            st.all_done()
            for k in range(TOPK):
                st.did(dve.tensor_copy(expert[:, k], top_at[:, :, k]))
            st.all_done()
            dve.wait_ge(consts_in, 32)
            for k in range(TOPK):
                st.did(dve.tensor_tensor(chosen[:, k], iota[:].unsqueeze(1).to_broadcast([P, TILES, NX]),
                                         over_experts(expert[:, k]), ALU.is_equal))
            after["chosen"] = st.n
            dve.wait_ge(exp_ready, 2)
            st.did(dve.tensor_reduce(total[:], exps[:], AX.X, ALU.add))
            st.all_done()
            st.did(dve.reciprocal(inv[:], total[:]))
            st.all_done()
            for k in range(TOPK):
                st.did(dve.tensor_tensor(prob[:, k], top_exp[:, k], inv[:], ALU.mult))
            dve.wait_ge(counted, 2)
            st.did(dve.tensor_copy(tile_count[:].rearrange("p c e -> p (c e)"), pN[:]))
            st.all_done()
            for e in range(NX):
                st.did(dve.tensor_tensor_scan(run_count[:, :, e], ones[:, 0:TOPK * TILES], tile_count[:, :, e],
                                              0.0, ALU.mult, ALU.add))
            st.all_done()
            st.did(dve.tensor_tensor(before[:], run_count[:], tile_count[:], ALU.subtract))
            st.all_done()
            st.did(dve.tensor_tensor(ahead[:], before[:], pB[:].rearrange("p (c e) -> p c e", e=NX), ALU.add))
            st.all_done()
            st.did(dve.tensor_tensor(before[:], ahead[:], chosen[:].rearrange("p k t e -> p (k t) e"), ALU.mult))
            st.all_done()
            st.did(dve.tensor_reduce(loc[:], before[:], AX.X, ALU.add))
            st.all_done()
            experts_flat = expert[:].rearrange("p k t -> p (k t)")
            st.did(dve.tensor_scalar(keep[:], loc[:], float(CAP), None, ALU.is_lt))
            st.did(dve.tensor_scalar(drop[:], loc[:], float(CAP), FAR, ALU.is_ge, ALU.mult))
            st.did(dve.scalar_tensor_tensor(slot[:], experts_flat, float(CAP), loc[:], ALU.mult, ALU.add))
            st.all_done()
            st.did(dve.tensor_scalar(slot_low[:], slot[:], float(SLOTS - 1), None, ALU.min))
            st.did(dve.tensor_tensor(slot_put[:], slot[:], drop[:], ALU.add))
            st.did(dve.tensor_tensor(kept[:], prob[:].rearrange("p k t -> p (k t)"), keep[:], ALU.mult))
            st.all_done()
            st.did(dve.tensor_copy(s["slot_get"][:], slot_low[:]))
            st.did(dve.tensor_copy(s["slot_put"][:], slot_put[:]))
            st.did(dve.tensor_tensor(denom[:], kept[:, 0:TILES], kept[:, TILES:2 * TILES], ALU.add))
            st.all_done()
            st.did(dve.tensor_scalar(denom_low[:], denom[:], 1e-9, None, ALU.max))
            st.all_done()
            st.did(dve.reciprocal(inv_denom[:], denom_low[:]))
            st.all_done()
            for k in range(TOPK):
                st.did(dve.tensor_tensor(gates[:, k], kept[:, k * TILES:(k + 1) * TILES], inv_denom[:], ALU.mult))

        @block.scalar
        def _(act):
            act.wait_ge(dve_step, after["shifts"])
            act.activation(exps[:], shifted[:], ACT.Exp).then_inc(exp_ready, 1)
            act.activation(top_exp[:], top_shift[:], ACT.Exp).then_inc(exp_ready, 1)

        @block.tensor
        def _(pe):
            pe.wait_ge(consts_in, 32)
            pe.wait_ge(ones_ready, 1)
            pe.wait_ge(dve_step, after["chosen"])
            flat = chosen[:].rearrange("p k t e -> p (k t e)")
            pe.matmul(pB[:], below[:], flat, start=True, stop=True).then_inc(counted, 1)
            pe.matmul(pN[:], ones[:], flat, start=True, stop=True).then_inc(counted, 1)


def attention(nc, d, s):
    with ExitStack() as ctx:
        def sb(name, shape, dt=F32):
            return ctx.enter_context(nc.sbuf_tensor("at_" + name, shape, dt))

        def pb(name, shape, dt=F32):
            return ctx.enter_context(nc.psum_tensor("at_" + name, shape, dt))

        def sem(name):
            return ctx.enter_context(nc.semaphore("at_" + name))

        attn, ident = s["attn"], s["ident"]
        NA, NB, NE_ = 3, 3, 8
        MR = PARTS
        qa = [sb(f"qa{u}", [STACK, S], BF16) for u in range(2)]
        ka = [sb(f"ka{u}", [STACK, S], BF16) for u in range(2)]
        qb = [sb(f"qb{u}", [STACK + MR, S], BF16) for u in range(2)]
        kb = [sb(f"kb{u}", [STACK + MR, S], BF16) for u in range(2)]
        vs = [sb(f"v{u}", [P, NQ, TPC, VW]) for u in range(2)]
        v_first = [sb(f"v_first{u}", [P, P]) for u in range(2)]
        identb = sb("identb", [P, P], BF16)
        hide_f = sb("hide_f", [P, 2, P])
        hide = sb("hide", [P, 2, P], BF16)
        piece_max = sb("piece_max", [P, QT, NQ])
        neg_max = sb("neg_max", [P, QT])
        neg_rest = sb("neg_rest", [P, QT])
        max_parts = sb("max_parts", [P, 2, PARTS, QT // 2], BF16)
        max_rows = [sb(f"max_rows{i}", [PARTS * QT // 2, P], BF16) for i in range(2)]
        wt = [sb(f"wt{i}", [P, CH]) for i in range(NE_)]
        raw = [sb(f"raw{i}", [P, CH]) for i in range(2)]
        osum = sb("osum", [P, TPC, D + 1])
        oinv = sb("oinv", [P, TPC])
        xrow = [sb(f"xrow{i}", [P, E]) for i in range(2)]

        pA = [pb(f"A{i}", [P, CH]) for i in range(NA)]
        pB = [pb(f"B{i}", [P, CH]) for i in range(NB)]
        pO = [pb(f"O{i}", [P, CH]) for i in range(2)]

        def pX_of(j):
            return pO[j % 2][:].rearrange("p (t n) -> p t n", t=TPC)

        def pM_of(b):
            return pA[b][0:PARTS * QT // 2, 0:P // 2].bitcast(BF16)

        consts_in = sem("consts_in")
        consts_ready = sem("consts_ready")
        a_in = [sem(f"a_in{u}") for u in range(2)]
        b_in = [sem(f"b_in{u}") for u in range(2)]
        max_in = [sem(f"max_in{i}") for i in range(2)]
        a_made = sem("a_made")
        a_used = sem("a_used")
        max_step = sem("max_step")
        b_made = sem("b_made")
        wt_ready = sem("wt_ready")
        wt_used = sem("wt_used")
        o_ready = sem("o_ready")
        oT_made = sem("oT_made")
        o_step = sem("o_step")
        xrow_in = [sem(f"xrow_in{i}") for i in range(2)]
        put = [sem(f"put{i}") for i in range(2)]

        A = [(i, 512 * m, min(512, P * (i + 1) - 512 * m)) for i in range(QT) for m in range(i // 4 + 1)]
        Bp = [(j, kt, max(0, kt - 4 * j) * P) for j in range(NQ) for kt in range(4 * j + 4)]
        NPC = len(A)
        assert len(Bp) == NPC
        HALF = [sum(1 for a in A if a[0] < QT // 2), NPC]
        END = [sum(1 for p in Bp if p[0] <= j) for j in range(NQ)]
        LAG = 3
        M1_AT, M0_AT = 6, HALF[0] + 6
        PER_A = NPC + 2
        assert PER_A % NA == 0 and NPC % NE_ == 0

        def a_step(p):
            return p + (p > M1_AT) + (p > M0_AT)

        def wait(eng, sm, v):
            if not isinstance(v, int) or v > 0:
                eng.wait_ge(sm, v)

        def stack(dst, src, base, head, batch, q_side):
            for r, (g, n) in enumerate(RUNS):
                rows = dst[g * D:(g + n) * D, :]
                if q_side:
                    part = src[0:n, bass.ds(head * D, D), bass.ds(batch * S, S)].rearrange("a p n -> a p n")
                else:
                    part = src[r:r + 1, bass.ds(head * D, D), bass.ds(batch * S, S)].to_broadcast([n, D, S])
                yield rows, part

        def pB_of(p, u):
            return pB[(p + u) % NB]

        block = ctx.enter_context(nc.Block())

        @block.sync
        def _(sp):
            for dst, src in ((hide_f[:, 0], d["c_hide_q"]), (hide_f[:, 1], d["c_hide_k"])):
                sp.dma_start(dst, src).then_inc(consts_in, 16)

            def load_a(n, u):
                wait(sp, a_made, NPC * (n - 1))
                for dst, src in (*stack(qa[u], d["q_parts"], 0, n % H, n // H, True),
                                 *stack(ka[u], d["k_parts"], 0, n % H // 4, n // H, False)):
                    sp.dma_start(dst, src).then_inc(a_in[u], 16)

            def load_b(n, u):
                wait(sp, wt_used, NPC * (n - 1))
                for dst, src in (*stack(qb[u], d["q_parts"], 0, n % H, n // H, True),
                                 *stack(kb[u], d["k_parts"], 0, n % H // 4, n // H, False)):
                    sp.dma_start(dst, src).then_inc(b_in[u], 16)
                v = d["v"][bass.ds(n // H * NQ, NQ), bass.ds(n % H // 4, 1)].rearrange("c o p n -> p (c o) n")
                sp.dma_start(vs[u][:].rearrange("p c t n -> p c (t n)"), v).then_inc(b_in[u], 16)
                first = d["v"][bass.ds(n // H * NQ, 1), bass.ds(n % H // 4, 1), :, 0:VW].rearrange("c o p n -> (c o p) n")
                sp.dma_start(v_first[u][:, 0:VW], first).then_inc(b_in[u], 16)

            def max_store(n, u, half, copied):
                sp.wait_ge(a_used, copied)
                rows = qb[u][STACK:STACK + MR, half * S // 2:(half + 1) * S // 2]
                sp.dma_start(rows.rearrange("a (t n) -> a t n", n=P),
                             max_rows[half][:]).then_inc(max_in[half], 16)

            def round_(n, u):
                max_store(n, u, 1, PER_A * (n + 1) + M1_AT + 2)
                load_b(n + 1, 1 - u)
                load_a(n + 2, u)
                max_store(n + 1, 1 - u, 0, PER_A * (n + 1) + M0_AT + 3)

            load_a(0, 0)
            load_b(0, 0)
            load_a(1, 1)
            max_store(0, 0, 0, M0_AT + 3)
            for n in range(2):
                round_(n, n)
            with sp.Fori(1, HEADS // 2 - 1) as j:
                for u in range(2):
                    round_(2 * j + u, u)
            max_store(HEADS - 2, 0, 1, PER_A * (HEADS - 1) + M1_AT + 2)
            load_b(HEADS - 1, 1)
            max_store(HEADS - 1, 1, 0, PER_A * (HEADS - 1) + M0_AT + 3)
            max_store(HEADS - 1, 1, 1, PER_A * HEADS + 1)

        @block.gpsimd
        def _(pool):
            for u in range(2):
                pool.memset(kb[u][STACK:STACK + MR], 1.0).then_inc(consts_ready, 1)
            for t in range(TILES):
                i = t % 2
                if t >= 2:
                    pool.wait_ge(put[i], 16 * TOPK * (t // 2))
                pool.dma_start(xrow[i][:], d["xn"][t * P:(t + 1) * P]).then_inc(xrow_in[i], 16)
                pool.wait_ge(xrow_in[i], 16 * (t // 2 + 1))
                for k in range(TOPK):
                    c = k * TILES + t
                    pool.indirect_dma_start(
                        out=d["buf"], out_offset=bass.IndirectOffsetOnAxis(ap=s["slot_put"][:, c:c + 1], axis=0),
                        in_=xrow[i][:], in_offset=None, bounds_check=SLOTS - 1, oob_is_err=False,
                    ).then_inc(put[i], 16)
            for i in range(2):
                pool.wait_ge(put[i], 16 * TOPK * (TILES // 2))

        @block.scalar
        def _(act):
            act.wait_ge(consts_in, 32)
            act.copy(hide[:], hide_f[:]).then_inc(consts_ready, 1)
            act.copy(identb[:], ident[:]).then_inc(consts_ready, 1)

            def raw_copy(n, j):
                G = NQ * n + j
                act.wait_ge(wt_used, NPC * n + END[j])
                wait(act, oT_made, G - 1)
                act.copy(raw[j % 2][:], pO[j % 2][:]).then_inc(o_ready, 1)

            def round_(n, u, first):
                for p in range(NPC):
                    j, kt, q0 = Bp[p]
                    N = NPC * n + p
                    act.wait_ge(b_made, N + 1)
                    wait(act, wt_used, N - NE_ + 1)
                    act.activation(wt[p % NE_][:, q0:CH], pB_of(p, u)[:, q0:CH], ACT.Exp,
                                   scale=D ** -0.5).then_inc(wt_ready, 1)
                    for jj in range(NQ):
                        if p == (END[jj] + LAG - 1) % NPC:
                            if jj < NQ - 1:
                                raw_copy(n, jj)
                            elif not first:
                                raw_copy(n - 1, jj)

            for n in range(2):
                round_(n, n, n == 0)
            with act.Fori(1, HEADS // 2) as j:
                for u in range(2):
                    round_(2 * j + u, u, False)
            raw_copy(HEADS - 1, NQ - 1)

        @block.tensor
        def _(pe):
            pe.wait_ge(consts_ready, 7)

            def piece_a(n, u, p):
                i, k0, w = A[p]
                N = PER_A * n + a_step(p)
                b = a_step(p) % NA
                if p == 0:
                    pe.wait_ge(a_in[u], 6 * 16 * (n // 2 + 1))
                wait(pe, a_used, N - NA + 1)
                diag = k0 + w == P * (i + 1)
                ins = pe.matmul(pA[b][:, 0:w], qa[u][:, i * P:(i + 1) * P], ka[u][:, k0:k0 + w],
                                start=True, stop=not diag)
                if diag:
                    ins = pe.matmul(pA[b][:, w - P:w], identb[:], hide[:, 0], start=False, stop=True)
                ins.then_inc(a_made, 1)

            def max_turn(n, half, N, b):
                pe.wait_ge(max_step, 5 * (2 * n + half) + 5)
                wait(pe, a_used, N - NA + 1)
                pe.transpose(pM_of(b), max_parts[:, half].rearrange("p a t -> p (a t)"),
                             identb[:]).then_inc(a_made, 1)

            def piece_b(n, u, p):
                j, kt, q0 = Bp[p]
                N = NPC * n + p
                if p == 0:
                    pe.wait_ge(b_in[u], 8 * 16 * (n // 2 + 1))
                    pe.wait_ge(max_in[0], 16 * (n + 1))
                if p == END[1]:
                    pe.wait_ge(max_in[1], 16 * (n + 1))
                wait(pe, wt_ready, N - NB + 1 + (u == 0 and p < 2))
                diag = kt >= 4 * j
                ins = pe.matmul(pB_of(p, u)[:, q0:CH], kb[u][:, kt * P:(kt + 1) * P],
                                qb[u][:, j * CH + q0:(j + 1) * CH], start=True, stop=not diag)
                if diag:
                    ins = pe.matmul(pB_of(p, u)[:, q0:q0 + P], identb[:], hide[:, 1], start=False, stop=True)
                ins.then_inc(b_made, 1)

            def values(n, u, p4):
                pe.wait_ge(wt_ready, NPC * n + p4 + 4)
                for p in range(p4, p4 + 4):
                    j, kt, q0 = Bp[p]
                    g = kt % 4
                    if kt == 0:
                        wait(pe, o_step, 3 * (NQ * n + j - 2) + 1)
                    if p == 0:
                        pe.matmul(pO[0][:], v_first[u][:], wt[0][:], start=True, stop=False)
                        ins = pe.matmul(pO[0][0:VW, 0:1], v_first[u][:, VW:2 * VW], wt[0][:, 0:1],
                                        start=False, stop=True)
                    else:
                        ins = pe.matmul(pO[j % 2][VW * g:VW * (g + 1), q0:CH], vs[u][:, kt // TPC, kt % TPC, :],
                                        wt[p % NE_][:, q0:CH], start=kt < 4 and j > 0, stop=kt >= 4 * j)
                    ins.then_inc(wt_used, 1)

            def turn(n, j):
                G = NQ * n + j
                pe.wait_ge(o_ready, G + 1)
                for t in range(TPC):
                    ins = pe.transpose(pX_of(j)[:, t, :], raw[j % 2][:, t * P:(t + 1) * P], ident[:])
                ins.then_inc(oT_made, 1)

            def round_(n, u, first, ahead):
                for p in range(NPC):
                    if ahead:
                        piece_a(n + 1, 1 - u, p)
                    if p == M1_AT and ahead:
                        max_turn(n, 1, PER_A * (n + 1) + M1_AT + 1, (M1_AT + 1) % NA)
                    elif p == M1_AT:
                        max_turn(n, 1, PER_A * (n + 1) + NA - 1, 0)
                    if p == M0_AT and ahead:
                        max_turn(n + 1, 0, PER_A * (n + 1) + M0_AT + 2, (M0_AT + 2) % NA)
                    piece_b(n, u, p)
                    if p % 4 == (3 + LAG) % 4:
                        if p >= 3 + LAG:
                            values(n, u, p - 3 - LAG)
                        elif not first:
                            values(n - 1, 1 - u, NPC - 3 - LAG + p)
                    for j in range(NQ):
                        if p == (END[j] + LAG + 2) % NPC:
                            if j < NQ - 1:
                                turn(n, j)
                            elif not first:
                                turn(n - 1, j)

            for p in range(NPC):
                piece_a(0, 0, p)
                if p == M1_AT:
                    pe.wait_ge(a_made, M1_AT + 1)
                    pe.sem_inc(a_made, 1)
                if p == M0_AT:
                    max_turn(0, 0, M0_AT + 2, (M0_AT + 2) % NA)
            for n in range(2):
                round_(n, n, n == 0, True)
            with pe.Fori(1, HEADS // 2 - 1) as j:
                for u in range(2):
                    round_(2 * j + u, u, False, True)
            round_(HEADS - 2, 0, False, True)
            round_(HEADS - 1, 1, False, False)
            values(HEADS - 1, 1, NPC - 4)
            turn(HEADS - 1, NQ - 1)

        @block.vector
        def _(dve):
            dve.memset(piece_max[:], NEG).then_inc(consts_ready, 1)
            for u in range(2):
                dve.memset(v_first[u][:, VW:P], 0.0).then_inc(consts_ready, 1)
            dve.wait_ge(consts_ready, 7)

            def maximum(n, p):
                i, k0, w = A[p]
                dve.wait_ge(a_made, PER_A * n + a_step(p) + 1)
                dve.tensor_reduce(piece_max[:, i, k0 // CH:k0 // CH + 1], pA[a_step(p) % NA][:, 0:w], AX.X,
                                  ALU.max).then_inc(a_used, 1)

            def max_copy(n, half, N, b):
                dve.wait_ge(a_made, N + 1)
                wait(dve, max_in[half], 16 * n)
                dve.tensor_copy(max_rows[half][:], pM_of(b)).then_inc(a_used, 1)

            def cut_max(n, half, step):
                t = slice(half * QT // 2, (half + 1) * QT // 2)
                base = 5 * (2 * n + half)
                if step:
                    dve.wait_ge(max_step, base + step)
                if step == 0:
                    dve.wait_ge(a_used, PER_A * n + a_step(HALF[half] - 1) + 1)
                    ins = dve.tensor_reduce(neg_max[:, t], piece_max[:, t], AX.X, ALU.max, negate=True)
                elif step == 1:
                    ins = dve.tensor_copy(max_parts[:, half, 0], neg_max[:, t])
                elif step == 2:
                    ins = dve.tensor_tensor(neg_rest[:, t], neg_max[:, t], max_parts[:, half, 0], ALU.subtract)
                elif step == 3:
                    ins = dve.tensor_copy(max_parts[:, half, 1], neg_rest[:, t])
                else:
                    ins = dve.tensor_tensor(max_parts[:, half, 2], neg_rest[:, t], max_parts[:, half, 1], ALU.subtract)
                ins.then_inc(max_step, 1)

            def result(n, j, step):
                G = NQ * n + j
                if step == 0:
                    dve.wait_ge(oT_made, G + 1)
                    wait(dve, o_step, 3 * G)
                    src = pX_of(j).rearrange("p t (g n) -> p t n g", g=4)[:, :, 0:D + 1, :]
                    dve.tensor_reduce(osum[:], src, AX.X, ALU.add).then_inc(o_step, 1)
                elif step == 1:
                    dve.wait_ge(o_step, 3 * G + 1)
                    dve.reciprocal(oinv[:], osum[:, :, D]).then_inc(o_step, 1)
                else:
                    dve.wait_ge(o_step, 3 * G + 2)
                    tile0 = n // H * QT + j * TPC
                    dst = attn[:, bass.ds(tile0, TPC), bass.ds(n % H * D, D)]
                    dve.tensor_tensor(dst, osum[:, :, 0:D], oinv[:].unsqueeze(2).to_broadcast([P, TPC, D]),
                                      ALU.mult).then_inc(o_step, 1)

            CUT_1 = {0: (0,), 1: (1, 2), 2: (3, 4)}
            CUT_0 = {HALF[0] + k: (k,) for k in range(5)}

            def round_(n, first, ahead):
                for p in range(NPC):
                    if ahead:
                        maximum(n + 1, p)
                    for step in CUT_1.get(p, ()):
                        cut_max(n, 1, step)
                    if p == M1_AT and ahead:
                        max_copy(n, 1, PER_A * (n + 1) + M1_AT + 1, (M1_AT + 1) % NA)
                    elif p == M1_AT:
                        max_copy(n, 1, PER_A * (n + 1), 0)
                    if ahead:
                        for step in CUT_0.get(p, ()):
                            cut_max(n + 1, 0, step)
                        if p == M0_AT:
                            max_copy(n + 1, 0, PER_A * (n + 1) + M0_AT + 2, (M0_AT + 2) % NA)
                    for j in range(NQ):
                        step = (p - END[j] - LAG - 3) % NPC
                        if step < 3:
                            if j < NQ - 1:
                                result(n, j, step)
                            elif not first:
                                result(n - 1, j, step)

            for p in range(NPC):
                maximum(0, p)
                if p == M1_AT:
                    dve.wait_ge(a_used, M1_AT + 1)
                    dve.sem_inc(a_used, 1)
                for step in CUT_0.get(p, ()):
                    cut_max(0, 0, step)
                if p == M0_AT:
                    max_copy(0, 0, M0_AT + 2, (M0_AT + 2) % NA)
            for n in range(2):
                round_(n, n == 0, True)
            with dve.Fori(1, HEADS // 2 - 1) as j:
                for u in range(2):
                    round_(2 * j + u, False, True)
            round_(HEADS - 2, False, True)
            round_(HEADS - 1, False, False)
            for step in range(3):
                result(HEADS - 1, NQ - 1, step)


def layer1_weights(nc, d, s):
    with ExitStack() as ctx:
        def sb(name, shape, dt=F32):
            return ctx.enter_context(nc.sbuf_tensor("lw_" + name, shape, dt))

        def pb(name, shape, dt=F32):
            return ctx.enter_context(nc.psum_tensor("lw_" + name, shape, dt))

        def sem(name):
            return ctx.enter_context(nc.semaphore("lw_" + name))

        ident = s["ident"]
        NW = 4
        gate_n = [sb(f"gate_n{i}", [P, E]) for i in range(NW)]
        up_n = [sb(f"up_n{i}", [P, E]) for i in range(NW)]
        down_n = [sb(f"down_n{i}", [P, EC, I1]) for i in range(NW)]
        down_full = sb("down_full", [P, NX + SI // I1, E])
        route_n = sb("route_n", [NX, E])
        pats = sb("pats", [NPAT, E])
        wq = sb("wq", [P, EC, E])
        wk = sb("wk", [P, EC, E])
        wv = sb("wv", [P, EC, E])
        bq = sb("bq", [P, EC])
        bk = sb("bk", [P, EC])
        bv = sb("bv", [P, E])
        diag = sb("diag", [P, 8, NPAT])
        diag_q = sb("diag_q", [P, 8, NPAT])
        diag_v = sb("diag_v", [P, 4, D])
        bq_wide = sb("bq_wide", [P, EC, P])
        zeros = sb("zeros", [P, P])
        patsT = sb("patsT", [P, EC, NPAT])
        wqT = sb("wqT", [P, EC, E])
        keysT = sb("keysT", [P, EC, NPAT])
        keysT4 = sb("keysT4", [P, EC, 4, NPAT])
        values4 = sb("values4", [P, E])
        key_blocks = sb("key_blocks", [P, EC, 8 * NPAT])

        pG = [pb(f"G{i}", [P, 2 * EC, I1]) for i in range(2)]
        pD = [pb(f"D{i}", [P, EC, P]) for i in range(2)]
        pS = pb("S", [P, EC, NPAT])
        pQ = pb("Q", [P, EC, E])
        pZ = pb("Z", [P, 512])

        mlp_in = [sem(f"mlp_in{i}") for i in range(NW)]
        small_in = sem("small_in")
        turned = sem("turned")
        kept = sem("kept")
        low_kept = sem("low_kept")
        pe_step = sem("pe_step")
        dve_step = sem("dve_step")
        MLPS = NX + SI // I1
        at_dve = {}
        order = [("zeros", 1), ("diag_q", 1), ("bq_wide", 2), ("patsT", 1), ("wqT", 1), ("keysT", 2),
                 ("keysT4", 2), ("key_blocks", 2), ("values4", 1), ("values", 1), (("fold", 0), 1), (("fold", 1), 1),
                 ("bias", 1), ("route", 1)]
        n = 0
        for name, count in order:
            n += count
            at_dve[name] = n

        def halves(ap):
            return ap.rearrange("(k p) n -> p k n", p=P)

        block = ctx.enter_context(nc.Block())

        @block.sync
        def _(sp):
            for dst, src in (
                (pats[:], d["key_param"].rearrange("o s e -> (o s) e")), (route_n[:], d["gate_w"]),
                (wq[:], halves(d["Wq"])), (wk[:], halves(d["Wk"])), (wv[:], halves(d["Wv"])), 
                (bq[:], d["bq"].rearrange("(k p) -> p k", p=P)), (bk[:], d["bk"].rearrange("(k p) -> p k", p=P)),
                (bv[:], d["bv"].rearrange("(o n) -> o n", o=1).to_broadcast([P, E])), (diag[:], d["c_diag"]),
                (diag_v[:], d["c_diag_v"]),
            ):
                sp.dma_start(dst, src, allow_slow_non_contiguous=True).then_inc(small_in, 16)
            for e in range(MLPS):
                i = e % NW
                if e >= NW:
                    sp.wait_ge(turned, 2 * (e - NW + 1))
                if e < NX:
                    gate, up, down = d["expert_gate_w"][e], d["expert_up_w"][e], d["expert_down_w"][e]
                else:
                    part = slice((e - NX) * I1, (e - NX + 1) * I1)
                    gate, up, down = d["shared_gate_w"][part], d["shared_up_w"][part], d["shared_down_w"][:, part]
                sp.dma_start(gate_n[i][:], gate).then_inc(mlp_in[i], 16)
                sp.dma_start(up_n[i][:], up).then_inc(mlp_in[i], 16)
                sp.dma_start(down_n[i][:], halves(down)).then_inc(mlp_in[i], 16)

        @block.tensor
        def _(pe):
            st = Steps(pe, pe_step)

            def mlp(e):
                i, b = e % NW, e % 2
                pe.wait_ge(mlp_in[i], 3 * 16 * (e // NW + 1))
                if e >= 2:
                    pe.wait_ge(kept, 3 * (e - 1))
                for k in range(EC):
                    cols = slice(k * P, (k + 1) * P)
                    pe.transpose(pG[b][:, k, :], gate_n[i][:, cols], ident[:])
                    ins = pe.transpose(pG[b][:, EC + k, :], up_n[i][:, cols], ident[:])
                ins.then_inc(turned, 1)
                for k in range(EC):
                    ins = pe.transpose(pD[b][:, k, :], down_n[i][:, k, :], ident[:])
                ins.then_inc(turned, 1)

            pe.wait_ge(small_in, 16 * 10)
            for k in range(EC):
                ins = pe.transpose(pS[:, k, :], pats[:, k * P:(k + 1) * P], ident[0:NPAT, 0:NPAT])
            st.did(ins)
            mlp(0)
            for c in range(EC):
                for k in range(EC):
                    ins = pe.transpose(pQ[:, c, k * P:(k + 1) * P], wq[:, k, c * P:(c + 1) * P], ident[:])
            st.did(ins)
            mlp(1)
            pe.wait_ge(dve_step, at_dve["patsT"])
            for c in range(EC):
                for k in range(EC):
                    ins = pe.matmul(pS[:, c, :], wk[:, k, c * P:(c + 1) * P], patsT[:, k, :], start=(k == 0),
                                    stop=(k == EC - 1))
            st.did(ins)
            mlp(2)
            pe.wait_ge(dve_step, at_dve["keysT4"])
            for k in range(EC):
                ins = pe.matmul(pZ[:, 0:E], keysT4[:, k].rearrange("p a n -> p (a n)"), wv[:, k, :], start=(k == 0),
                                stop=(k == EC - 1))
            st.did(ins)
            mlp(3)
            pe.wait_ge(dve_step, at_dve["values4"])
            for k in range(EC):
                for c in range(EC):
                    ins = pe.matmul(pQ[:, c, :], wqT[:, c, k * P:(k + 1) * P], key_blocks[:, c, :], start=True, stop=True)
                st.did(ins)
                mlp(4 + k)
                pe.wait_ge(dve_step, at_dve["fold", k])
            for c in range(EC):
                ins = pe.matmul(pZ[:, c * E:(c + 1) * E], bq_wide[:, c, :], key_blocks[:, c, :], start=True, stop=True)
            st.did(ins)
            mlp(6)
            pe.wait_ge(dve_step, at_dve["bias"])
            for k in range(EC):
                ins = pe.transpose(pQ[:, 0, k * NX:(k + 1) * NX], route_n[:, k * P:(k + 1) * P], ident[0:NX, 0:NX])
            st.did(ins)
            mlp(7)
            for e in range(8, MLPS):
                mlp(e)

        @block.scalar
        def _(act):
            for e in range(MLPS):
                act.wait_ge(turned, 2 * e + 2)
                act.copy(s["gate_up"][:, e], pG[e % 2][:]).then_inc(kept, 1)
                down = pD[e % 2][:].rearrange("p k n -> p (k n)")
                act.copy(s["down0"][:, e], down).then_inc(kept, 1)
                act.copy(down_full[:, e], down).then_inc(kept, 1)

        @block.gpsimd
        def _(pool):
            for e in range(MLPS):
                pool.wait_ge(kept, 3 * e + 3)
                if e:
                    pool.wait_ge(low_kept, e)
                pool.tensor_tensor(s["down1"][:, e], down_full[:, e], s["down0"][:, e].bitcast(F32),
                                   ALU.subtract).then_inc(low_kept, 1)

        @block.vector
        def _(dve):
            st = Steps(dve, dve_step)
            st.did(dve.memset(zeros[:], 0.0))
            dve.wait_ge(small_in, 16 * 10)
            st.did(dve.tensor_scalar(diag_q[:], diag[:], D ** -0.5, None, ALU.mult))
            st.all_done()
            for c in range(EC):
                st.did(dve.tensor_scalar(bq_wide[:, c, :], zeros[:], bq[:, c:c + 1], None, ALU.add))
            dve.wait_ge(pe_step, 1)
            st.did(dve.tensor_copy(patsT[:], pS[:]))
            dve.wait_ge(pe_step, 2)
            st.did(dve.tensor_copy(wqT[:], pQ[:]))
            dve.wait_ge(pe_step, 3)
            for c in range(EC):
                st.did(dve.tensor_scalar(keysT[:, c, :], pS[:, c, :], bk[:, c:c + 1], None, ALU.add))
            st.all_done()
            for c in range(EC):
                st.did(dve.tensor_copy(keysT4[:, c], keysT[:, c, :].unsqueeze(1).to_broadcast([P, 4, NPAT])))
            for c in range(EC):
                st.did(dve.tensor_tensor(key_blocks[:, c, :].rearrange("p (h n) -> p h n", n=NPAT), diag_q[:],
                                         keysT[:, c, :].unsqueeze(1).to_broadcast([P, 8, NPAT]), ALU.mult))
            dve.wait_ge(pe_step, 4)
            st.did(dve.tensor_tensor(values4[:], pZ[:, 0:E], bv[:], ALU.add))
            st.all_done()
            st.did(dve.tensor_tensor(s["values"][:], values4[:].rearrange("p (g n) -> p g n", g=4),
                                     diag_v[:].rearrange("p a n -> p (a n)").unsqueeze(1).to_broadcast([P, 4, 4 * D]),
                                     ALU.mult))
            for k in range(EC):
                dve.wait_ge(pe_step, 5 + k)
                st.did(dve.tensor_copy(s["to_scores"][:, k, :], pQ[:].rearrange("p c n -> p (c n)")))
            dve.wait_ge(pe_step, 7)
            st.did(dve.tensor_copy(s["score_bias"][:], pZ[:]))
            dve.wait_ge(pe_step, 8)
            st.did(dve.tensor_copy(s["route"][:].rearrange("p k n -> p (k n)"), pQ[:, 0, 0:EC * NX]))
            assert st.n == at_dve["route"]


def experts(nc, d, s):
    with ExitStack() as ctx:
        def sb(name, shape, dt=F32):
            return ctx.enter_context(nc.sbuf_tensor("ex_" + name, shape, dt))

        def pb(name, shape, dt=F32):
            return ctx.enter_context(nc.psum_tensor("ex_" + name, shape, dt))

        def sem(name):
            return ctx.enter_context(nc.semaphore("ex_" + name))

        RT = 2
        R = RT * P
        PER = CAP // R
        FC = F // P
        assert PER * R == CAP and FC % 4 == 0
        ident = s["ident"]
        raw_in = sb("raw_in", [P, EC, 2 * F])
        raw_out = sb("raw_out", [P, FC, E])
        w_in = [[sb(f"w_in{i}{a}", [P, EC, 2 * F], F32R) for a in range(2)] for i in range(2)]
        w_out = [[sb(f"w_out{i}{a}", [P, FC, E], F32R) for a in range(2)] for i in range(2)]
        x = [sb(f"x{i}", [P, RT, E]) for i in range(2)]
        xT = [[sb(f"xT{i}{a}", [P, EC, R], F32R) for a in range(2)] for i in range(2)]
        act_a = [sb(f"act_a{i}", [P, R]) for i in range(4)]
        h = [sb(f"h{i}", [P, FC, R]) for i in range(2)]
        hT = [[sb(f"hT{i}{a}", [P, FC, R], F32R) for a in range(2)] for i in range(2)]
        y = [sb(f"y{i}", [P, RT, E]) for i in range(2)]
        pXT = pb("XT", [P, EC, R])
        pH = [pb(f"H{i}", [P, 2, R]) for i in range(4)]
        pY = [pb(f"Y{i}", [P, RT, E]) for i in range(2)]

        w_loaded = sem("w_loaded")
        w_high = sem("w_high")
        w_low = sem("w_low")
        x_loaded = [sem(f"x_loaded{i}") for i in range(2)]
        xT_made = sem("xT_made")
        xT_high = sem("xT_high")
        xT_low = sem("xT_low")
        h_made = sem("h_made")
        act_ready = sem("act_ready")
        h_ready = sem("h_ready")
        h_high = sem("h_high")
        h_low = sem("h_low")
        y_made = sem("y_made")
        y_ready = sem("y_ready")
        y_stored = [sem(f"y_stored{i}") for i in range(2)]

        rows_in = d["buf"].rearrange("(m t p) e -> m p t e", t=RT, p=P)
        rows_out = d["expert_out"].rearrange("(m t p) e -> m p t e", t=RT, p=P)
        win = d["W_in"].rearrange("x (k p) f -> x p k f", p=P)
        wout = d["W_out"].rearrange("x (k p) e -> x p k e", p=P)

        def one(ap, m):
            return ap[bass.ds(m, 1)].rearrange("o p t e -> (o p) t e")

        def wait(eng, sm, v):
            if not isinstance(v, int) or v > 0:
                eng.wait_ge(sm, v)

        def pieces(w):
            flat = "p a b -> p (a b)"
            found = []
            for raw, parts in ((raw_in, w_in[w]), (raw_out, w_out[w])):
                views = [t[:].rearrange(flat) for t in (raw, *parts)]
                found += [tuple(v[:, c:c + 512] for v in views) for c in range(0, views[0].shape[1], 512)]
            return found

        CUTS = len(pieces(0))
        CUT_IN = {2: (0, 1), 3: (2, 3), 4: (4, 5)}
        CUTS_IN = 4
        assert CUTS == 6 and PER == 5

        PAIR = 2 * PER
        ROUNDS = NX // 2
        assert PAIR % 2 == 0

        def cuts(cut, j, i, last):
            e = 2 * j + i // PER
            if not (last and i >= PER):
                for q in CUT_IN.get(i % PER, ()):
                    cut(e + 1, 1 - i // PER, q)

        block = ctx.enter_context(nc.Block())

        @block.sync
        def _(sp):
            def weights(e):
                wait(sp, w_low, CUTS * e)
                sp.dma_start(raw_in[:], one(win, e)).then_inc(w_loaded, 16)
                sp.dma_start(raw_out[:], one(wout, e)).then_inc(w_loaded, 16)

            def rows(m, i):
                wait(sp, xT_made, m - 1)
                sp.dma_start(x[i][:], one(rows_in, m)).then_inc(x_loaded[i], 16)

            def round_(j, more):
                for i in range(PAIR):
                    m = PAIR * j + i
                    if i < PAIR - 2 or more:
                        rows(m + 2, i % 2)
                    if i % PER == 0 and (i < PER or more):
                        weights(2 * j + i // PER + 1)

            weights(0)
            rows(0, 0)
            rows(1, 1)
            with sp.Fori(0, ROUNDS - 1) as j:
                round_(j, True)
            round_(ROUNDS - 1, False)

        @block.tensor
        def _(pe):
            def turn(m, i):
                pe.wait_ge(x_loaded[i], 16 * (m // 2 + 1))
                wait(pe, xT_low, m)
                for t in range(RT):
                    for k in range(EC):
                        ins = pe.transpose(pXT[:, k, t * P:(t + 1) * P], x[i][:, t, k * P:(k + 1) * P], ident[:])
                ins.then_inc(xT_made, 1)

            def hidden(m, i, w, f):
                wait(pe, h_ready, FC * m + f - 3)
                for a in range(2):
                    terms = [(k, *q) for k in range(EC) for q in TERMS]
                    for n, (k, wq, xq) in enumerate(terms):
                        cols = slice(a * F + f * P, a * F + (f + 1) * P)
                        ins = pe.matmul(pH[f][:, a, :], w_in[w][wq][:, k, cols], xT[i][xq][:, k, :],
                                        start=(n == 0), stop=(n == len(terms) - 1))
                ins.then_inc(h_made, 1)

            def output(m, i, w):
                pe.wait_ge(h_low, FC * m + FC)
                wait(pe, y_ready, m - 1)
                for t in range(RT):
                    terms = [(f, *q) for f in range(FC) for q in TERMS]
                    for n, (f, hq, wq) in enumerate(terms):
                        ins = pe.matmul(pY[i][:, t, :], hT[i][hq][:, f, t * P:(t + 1) * P], w_out[w][wq][:, f, :],
                                        start=(n == 0), stop=(n == len(terms) - 1))
                ins.then_inc(y_made, 1)

            def round_(j, first, last):
                for i in range(PAIR):
                    m, w, b = PAIR * j + i, i // PER, i % 2
                    if i % PER == 0:
                        pe.wait_ge(w_low, CUTS * (2 * j + w) + CUTS_IN)
                    pe.wait_ge(xT_low, m + 1)
                    for f in range(FC):
                        hidden(m, b, w, f)
                        if f == 0 and not (last and i == PAIR - 1):
                            turn(m + 1, 1 - b)
                        if f == 1 and not (first and i == 0):
                            if i % PER == 1:
                                pe.wait_ge(w_low, CUTS * (2 * j + w + 1))
                            output(m - 1, 1 - b, (i - 1) % PAIR // PER)

            turn(0, 0)
            round_(0, True, False)
            with pe.Fori(1, ROUNDS - 1) as j:
                round_(j, False, False)
            round_(ROUNDS - 1, False, True)
            output(PAIR * ROUNDS - 1, 1, 1)

        @block.gpsimd
        def _(pool):
            with pool.Fori(0, ROUNDS) as j:
                for i in range(PAIR):
                    for f in range(FC):
                        pool.wait_ge(h_high, FC * (PAIR * j + i) + f + 1)
                        pool.tensor_tensor(hT[i % 2][1][:, f, :], h[i % 2][:, f, :],
                                           hT[i % 2][0][:, f, :].bitcast(F32), ALU.subtract).then_inc(h_low, 1)

        @block.scalar
        def _(act):
            def gelus(m, f):
                act.wait_ge(h_made, FC * m + f + 1)
                act.activation(act_a[f][:], pH[f][:, 0, :], ACT.Gelu).then_inc(act_ready, 1)

            def high(m, i, f):
                act.wait_ge(h_ready, FC * m + f + 1)
                act.copy(hT[i][0][:, f, :], h[i][:, f, :]).then_inc(h_high, 1)

            def keep(m, i):
                act.wait_ge(y_made, m + 1)
                wait(act, y_stored[i], 16 * (m // 2))
                act.copy(y[i][:], pY[i][:]).then_inc(y_ready, 1)

            def store(m, i):
                act.wait_ge(y_ready, m + 1)
                act.dma_start(one(rows_out, m), y[i][:]).then_inc(y_stored[i], 16)

            def xT_copy(m, i):
                act.wait_ge(xT_made, m + 1)
                wait(act, h_made, FC * (m - 1))
                act.copy(xT[i][0][:], pXT[:]).then_inc(xT_high, 1)

            def cut(e, w, q):
                raw, parts = pieces(w)[q][0], pieces(w)[q][1:]
                act.wait_ge(w_loaded, 32 * (e + 1))
                act.copy(parts[0], raw).then_inc(w_high, 1)

            def round_(j, first, last):
                for i in range(PAIR):
                    m, b = PAIR * j + i, i % 2
                    for f in range(FC):
                        gelus(m, f)
                        if f == 0 and not (last and i == PAIR - 1):
                            xT_copy(m + 1, 1 - b)
                        if f:
                            high(m, b, f - 1)
                        if f == 1 and not (first and i == 0):
                            keep(m - 1, 1 - b)
                        if f == 2 and not (first and i == 0):
                            store(m - 1, 1 - b)
                        if f == 2:
                            cuts(cut, j, i, last)
                    high(m, b, FC - 1)

            for q in range(CUTS):
                cut(0, 0, q)
            xT_copy(0, 0)
            round_(0, True, False)
            with act.Fori(1, ROUNDS - 1) as j:
                round_(j, False, False)
            round_(ROUNDS - 1, False, True)
            keep(PAIR * ROUNDS - 1, 1)
            store(PAIR * ROUNDS - 1, 1)
            for i in range(2):
                act.wait_ge(y_stored[i], 16 * (PAIR // 2 * ROUNDS))

        @block.vector
        def _(dve):
            def xT_rest(m, i):
                dve.wait_ge(xT_high, m + 1)
                dve.tensor_tensor(xT[i][1][:], pXT[:], xT[i][0][:].bitcast(F32), ALU.subtract).then_inc(xT_low, 1)

            def cut(e, w, q):
                raw, high, low = pieces(w)[q]
                dve.wait_ge(w_high, CUTS * e + q + 1)
                dve.tensor_tensor(low, raw, high.bitcast(F32), ALU.subtract).then_inc(w_low, 1)

            def round_(j, first, last):
                for i in range(PAIR):
                    m, b = PAIR * j + i, i % 2
                    for f in range(FC):
                        dve.wait_ge(act_ready, FC * m + f + 1)
                        if f == 0:
                            wait(dve, y_made, m - 1)
                        dve.tensor_tensor(h[b][:, f, :], act_a[f][:], pH[f][:, 1, :], ALU.mult).then_inc(h_ready, 1)
                        if f == 0 and not (last and i == PAIR - 1):
                            xT_rest(m + 1, 1 - b)
                        if f == 2:
                            cuts(cut, j, i, last)

            for q in range(CUTS):
                cut(0, 0, q)
            xT_rest(0, 0)
            round_(0, True, False)
            with dve.Fori(1, ROUNDS - 1) as j:
                round_(j, False, False)
            round_(ROUNDS - 1, False, True)


def mixing(nc, d, s):
    with ExitStack() as ctx:
        def sb(name, shape, dt=F32):
            return ctx.enter_context(nc.sbuf_tensor("mx_" + name, shape, dt))

        def pb(name, shape, dt=F32):
            return ctx.enter_context(nc.psum_tensor("mx_" + name, shape, dt))

        def sem(name):
            return ctx.enter_context(nc.semaphore("mx_" + name))

        ident = s["ident"]
        w_out = sb("w_out", [P, EC, E])
        bout = sb("bout", [P, E])
        bo = sb("bo", [P, E])
        x = [sb(f"x{u}", [P, 2, E]) for u in range(2)]
        at = [sb(f"at{u}", [P, 2, E]) for u in range(2)]
        at_slot = [sb(f"at_slot{u}", [P, TOPK, 2], U32) for u in range(2)]
        gate = [sb(f"gate{u}", [P, TOPK, 2]) for u in range(2)]
        ye = [[sb(f"ye{k}{u}", [P, 2, E]) for u in range(2)] for k in range(TOPK)]
        aT = [sb(f"aT{u}", [P, EC, 2 * P]) for u in range(2)]
        part = [sb(f"part{u}", [P, 3, 2, E]) for u in range(2)]
        x1 = [sb(f"x1{u}", [P, 2, E]) for u in range(2)]
        xb = [sb(f"xb{u}", [P, 2, E]) for u in range(2)]
        stats = sb("stats", [P, 2, 6])
        carrier = sb("carrier", [P, 1])
        mean_var = sb("mean_var", [P, 2, 2])
        var_eps = sb("var_eps", [P, 2])
        std = sb("std", [P, 2])
        rstd = sb("rstd", [P, 2])
        xn = [sb(f"xn{u}", [P, 2, E]) for u in range(2)]
        xnT = [sb(f"xnT{u}", [P, EC, 2 * P]) for u in range(2)]
        pA = [pb(f"A{u}", [P, EC, 2 * P]) for u in range(2)]
        pW = [pb(f"W{u}", [P, 2, E]) for u in range(2)]
        pT = [pb(f"T{u}", [P, EC, 2 * P]) for u in range(2)]
        pL = [pb(f"L{u}", [P, 2, NX]) for u in range(2)]

        consts_in = sem("consts_in")
        x_in = [sem(f"x_in{u}") for u in range(2)]
        picked = sem("picked")
        rows_in = [sem(f"rows_in{u}") for u in range(2)]
        aT_made = sem("aT_made")
        aT_ready = sem("aT_ready")
        w_made = sem("w_made")
        sums = sem("sums")
        norm = sem("norm")
        std_ready = sem("std_ready")
        xb_ready = sem("xb_ready")
        xb_out = [sem(f"xb_out{u}") for u in range(2)]
        xnT_made = sem("xnT_made")
        xnT_ready = sem("xnT_ready")
        xnT_out = [sem(f"xnT_out{u}") for u in range(2)]
        logits_made = sem("logits_made")
        logits_ready = sem("logits_ready")
        STEPS = TILES // 2
        ROUNDS = STEPS // 2
        x_rows = d["x"].rearrange("b (t w p) e -> (b t) p w e", p=P, w=2)
        xb_rows = d["x1b"].rearrange("(t w p) e -> t p w e", p=P, w=2)

        def wait(eng, sm, v):
            if not isinstance(v, int) or v > 0:
                eng.wait_ge(sm, v)

        def one(ap, t):
            return ap[bass.ds(t, 1)].rearrange("o p w e -> (o p) w e")

        def rounds(eng, tile):
            for t in range(2):
                tile(t, t)
            with eng.Fori(1, ROUNDS) as j:
                for u in range(2):
                    tile(2 * j + u, u)

        block = ctx.enter_context(nc.Block())

        @block.sync
        def _(sp):
            sp.dma_start(w_out[:], d["Wout"].rearrange("(k p) n -> p k n", p=P)).then_inc(consts_in, 16)
            sp.dma_start(bout[:], d["bout"].rearrange("(o n) -> o n", o=1).to_broadcast([P, E])).then_inc(consts_in, 16)
            sp.dma_start(bo[:], d["bo"].rearrange("(o n) -> o n", o=1).to_broadcast([P, E])).then_inc(consts_in, 16)

            def tile(t, u):
                wait(sp, sums, 6 * (t - 1))
                wait(sp, aT_made, t - 1)
                sp.dma_start(x[u][:], one(x_rows, t)).then_inc(x_in[u], 16)
                sp.dma_start(at[u][:], s["attn"][:, bass.ds(2 * t, 2), :]).then_inc(x_in[u], 16)

            rounds(sp, tile)

        @block.gpsimd
        def _(pool):
            def tile(t, u):
                wait(pool, sums, 6 * (t - 1))
                slots = s["slot_get"][:].rearrange("p (k t) -> p k t", k=TOPK)
                pool.tensor_copy(at_slot[u][:], slots[:, :, bass.ds(2 * t, 2)]).then_inc(picked, 1)
                pool.wait_ge(picked, 2 * t + 1)
                pool.tensor_copy(gate[u][:], s["gates"][:, :, bass.ds(2 * t, 2)]).then_inc(picked, 1)
                for k in range(TOPK):
                    for w in range(2):
                        pool.indirect_dma_start(
                            out=ye[k][u][:, w, :], out_offset=None, in_=d["expert_out"],
                            in_offset=bass.IndirectOffsetOnAxis(ap=at_slot[u][:, k, w:w + 1], axis=0),
                        ).then_inc(rows_in[u], 16)

            rounds(pool, tile)

        @block.tensor
        def _(pe):
            pe.wait_ge(consts_in, 48)

            def project(t, u):
                pe.wait_ge(x_in[u], 32 * (t // 2 + 1))
                wait(pe, aT_ready, t - 1)
                for k in range(EC):
                    for w in range(2):
                        ins = pe.transpose(pA[u][:, k, w * P:(w + 1) * P], at[u][:, w, k * P:(k + 1) * P], ident[:])
                ins.then_inc(aT_made, 1)
                pe.wait_ge(aT_ready, t + 1)
                wait(pe, sums, 6 * (t - 1))
                for w in range(2):
                    for k in range(EC):
                        ins = pe.matmul(pW[u][:, w, :], aT[u][:, k, w * P:(w + 1) * P], w_out[:, k, :],
                                        start=(k == 0), stop=(k == EC - 1))
                ins.then_inc(w_made, 1)

            def route(t, u):
                pe.wait_ge(norm, 8 * t + 8)
                wait(pe, xnT_ready, t - 1)
                for k in range(EC):
                    for w in range(2):
                        ins = pe.transpose(pT[u][:, k, w * P:(w + 1) * P], xn[u][:, w, k * P:(k + 1) * P], ident[:])
                ins.then_inc(xnT_made, 1)
                pe.wait_ge(xnT_ready, t + 1)
                wait(pe, logits_ready, t - 1)
                for w in range(2):
                    for k in range(EC):
                        ins = pe.matmul(pL[u][:, w, :], xnT[u][:, k, w * P:(w + 1) * P], s["route"][:, k, :],
                                        start=(k == 0), stop=(k == EC - 1))
                ins.then_inc(logits_made, 1)

            project(0, 0)
            project(1, 1)
            for t in range(2, 4):
                project(t, t % 2)
                route(t - 2, t % 2)
            with pe.Fori(2, ROUNDS) as j:
                for u in range(2):
                    project(2 * j + u, u)
                    route(2 * j + u - 2, u)
            route(STEPS - 2, 0)
            route(STEPS - 1, 1)

        @block.scalar
        def _(act):
            def turned(t, u):
                act.wait_ge(aT_made, t + 1)
                wait(act, w_made, t - 1)
                act.copy(aT[u][:], pA[u][:]).then_inc(aT_ready, 1)

            def rest(t, u):
                act.wait_ge(norm, 8 * t + 5)
                act.activation(std[:], var_eps[:], ACT.Sqrt).then_inc(std_ready, 1)
                act.wait_ge(xnT_made, t + 1)
                wait(act, logits_made, t - 1)
                wait(act, xnT_out[u], 16 * (t // 2))
                act.copy(xnT[u][:], pT[u][:]).then_inc(xnT_ready, 1)
                act.wait_ge(xnT_ready, t + 1)
                dst = d["x1nT"][:, :, bass.ds(t * 2 * P, 2 * P)].rearrange("k p n -> p k n")
                act.dma_start(dst, xnT[u][:]).then_inc(xnT_out[u], 16)
                act.wait_ge(xb_ready, t + 1)
                act.dma_start(one(xb_rows, t), xb[u][:]).then_inc(xb_out[u], 16)

            turned(0, 0)
            turned(1, 1)
            for t in range(2, 4):
                turned(t, t % 2)
                rest(t - 2, t % 2)
            with act.Fori(2, ROUNDS) as j:
                for u in range(2):
                    turned(2 * j + u, u)
                    rest(2 * j + u - 2, u)
            rest(STEPS - 2, 0)
            rest(STEPS - 1, 1)
            for u in range(2):
                act.wait_ge(xnT_out[u], 16 * ROUNDS)
                act.wait_ge(xb_out[u], 16 * ROUNDS)

        @block.vector
        def _(dve):
            dve.wait_ge(consts_in, 48)

            def total(t, u, k):
                if k == 0:
                    dve.wait_ge(x_in[u], 32 * (t // 2 + 1))
                    both = bout[:].unsqueeze(1).to_broadcast([P, 2, E])
                    dve.tensor_tensor(part[u][:, 0], x[u][:], both, ALU.add).then_inc(sums, 1)
                elif k == 1:
                    dve.wait_ge(w_made, t + 1)
                    dve.wait_ge(sums, 6 * t + 1)
                    dve.tensor_tensor(part[u][:, 1], pW[u][:], part[u][:, 0], ALU.add).then_inc(sums, 1)
                elif k == 2:
                    dve.wait_ge(sums, 6 * t + 2)
                    dve.wait_ge(rows_in[u], 64 * (t // 2 + 1))
                    dve.wait_ge(picked, 2 * t + 2)
                    for w in range(2):
                        dve.scalar_tensor_tensor(part[u][:, 2, w], ye[0][u][:, w], gate[u][:, 0, w:w + 1],
                                                 part[u][:, 1, w], ALU.mult, ALU.add).then_inc(sums, 1)
                elif k == 3:
                    dve.wait_ge(sums, 6 * t + 4)
                    wait(dve, xb_ready, t - 1)
                    for w in range(2):
                        dve.scalar_tensor_tensor(x1[u][:, w], ye[1][u][:, w], gate[u][:, 1, w:w + 1],
                                                 part[u][:, 2, w], ALU.mult, ALU.add).then_inc(sums, 1)
                else:
                    dve.wait_ge(sums, 6 * t + 6)
                    wait(dve, xb_out[u], 16 * (t // 2))
                    both = bo[:].unsqueeze(1).to_broadcast([P, 2, E])
                    dve.tensor_tensor(xb[u][:], x1[u][:], both, ALU.add).then_inc(xb_ready, 1)

            def normal(t, u, k):
                if k == 0:
                    dve.wait_ge(sums, 6 * t + 6)
                    for w in range(2):
                        dve.bn_stats(stats[:, w], x1[u][:, w]).then_inc(norm, 1)
                elif k == 1:
                    dve.wait_ge(norm, 8 * t + 2)
                    dve.memset(carrier[:], 0.0)
                    for w in range(2):
                        dve.bn_aggr(mean_var[:, w], stats[:, w]).then_inc(norm, 1)
                elif k == 2:
                    dve.wait_ge(norm, 8 * t + 4)
                    dve.tensor_scalar(var_eps[:], mean_var[:, :, 1], LN_EPS, None, ALU.add).then_inc(norm, 1)
                elif k == 3:
                    dve.wait_ge(std_ready, t + 1)
                    dve.reciprocal(rstd[:], std[:]).then_inc(norm, 1)
                else:
                    dve.wait_ge(norm, 8 * t + 6)
                    wait(dve, xnT_made, t - 1)
                    for w in range(2):
                        dve.tensor_scalar(xn[u][:, w], x1[u][:, w], mean_var[:, w, 0:1], rstd[:, w:w + 1],
                                          ALU.subtract, ALU.mult).then_inc(norm, 1)

            def logits(t, u):
                dve.wait_ge(logits_made, t + 1)
                dve.tensor_copy(s["logits"][:, bass.ds(2 * t, 2), :], pL[u][:]).then_inc(logits_ready, 1)

            def both(t, u):
                for k in range(5):
                    total(t, u, k)
                    normal(t - 1, 1 - u, k)

            for k in range(5):
                total(0, 0, k)
            both(1, 1)
            for t in range(2, 4):
                both(t, t % 2)
                logits(t - 2, t % 2)
            with dve.Fori(2, ROUNDS) as j:
                for u in range(2):
                    both(2 * j + u, u)
                    logits(2 * j + u - 2, u)
            for k in range(5):
                normal(STEPS - 1, 1, k)
            logits(STEPS - 2, 0)
            logits(STEPS - 1, 1)


def weighting(nc, d, s):
    with ExitStack() as ctx:
        def sb(name, shape, dt=F32):
            return ctx.enter_context(nc.sbuf_tensor("wg_" + name, shape, dt))

        def sem(name):
            return ctx.enter_context(nc.semaphore("wg_" + name))

        biased = sb("biased", [P, TILES, NX])
        bias = sb("bias", [P, NX])
        iota = sb("iota", [P, NX])
        ones = sb("ones", [P, P])
        top = sb("top", [P, TILES, 8])
        top_at = sb("top_at", [P, TILES, 8], U32)
        expert = sb("expert", [P, TOPK, TILES])
        chosen = sb("chosen", [P, TOPK, TILES, NX])
        score = sb("score", [P, TOPK, TILES])
        both = sb("both", [P, TILES])
        both_eps = sb("both_eps", [P, TILES])
        inv = sb("inv", [P, TILES])
        share = sb("share", [P, TOPK, TILES])
        picked = sb("picked", [P, TILES, NX])
        shares = sb("shares", [P, TOPK, TILES, NX])
        shared_sum = sb("shared_sum", [P, TILES, NX])
        sums = sb("sums", [P, 2, NX])
        count = sb("count", [P, NX])
        inv_count = sb("inv_count", [P, NX])
        mean = sb("mean", [P, NX])
        pS = ctx.enter_context(nc.psum_tensor("wg_pS", [P, 2 * NX], F32))

        consts_in = sem("consts_in")
        ones_ready = sem("ones_ready")
        dve_step = sem("dve_step")
        scored = sem("scored")
        summed = sem("summed")
        after = {}
        block = ctx.enter_context(nc.Block())

        def over_experts(ap):
            return ap.unsqueeze(len(ap.shape)).to_broadcast(list(ap.shape) + [NX])

        def over_tiles(ap):
            return ap.unsqueeze(1).to_broadcast([P, TILES, NX])

        @block.sync
        def _(sp):
            sp.dma_start(iota[:], d["c_iota"]).then_inc(consts_in, 16)
            sp.dma_start(bias[:], d["lb_bias"].rearrange("(o n) -> o n", o=1).to_broadcast([P, NX])).then_inc(consts_in, 16)
            xT = s["attn"][:].rearrange("p t e -> p (t e)").rearrange("p (k n) -> p k n", k=EC)
            for b in range(B):
                cols = slice(b * S, (b + 1) * S)
                sp.dma_start(xT[:, :, cols], d["x1nT"][:, :, cols].rearrange("k p n -> p k n")).then_inc(s["xT_in"][b], 16)

        @block.gpsimd
        def _(pool):
            pool.memset(ones[:], 1.0).then_inc(ones_ready, 1)

        @block.vector
        def _(dve):
            st = Steps(dve, dve_step)
            dve.wait_ge(consts_in, 32)
            st.did(dve.tensor_tensor(biased[:], s["logits"][:], over_tiles(bias[:]), ALU.add))
            st.all_done()
            for t in range(TILES):
                st.did(dve.max(top[:, t], biased[:, t]))
            st.all_done()
            after["top"] = st.n
            for t in range(TILES):
                st.did(dve.max_index(top_at[:, t], top[:, t], biased[:, t]))
            st.all_done()
            for k in range(TOPK):
                st.did(dve.tensor_copy(expert[:, k], top_at[:, :, k]))
            st.all_done()
            for k in range(TOPK):
                st.did(dve.tensor_tensor(chosen[:, k], over_tiles(iota[:]), over_experts(expert[:, k]), ALU.is_equal))
            dve.wait_ge(scored, TOPK)
            st.did(dve.tensor_tensor(both[:], score[:, 0], score[:, 1], ALU.add))
            st.all_done()
            st.did(dve.tensor_scalar(both_eps[:], both[:], 1e-8, None, ALU.add))
            st.all_done()
            st.did(dve.reciprocal(inv[:], both_eps[:]))
            st.all_done()
            for k in range(TOPK):
                st.did(dve.tensor_tensor(share[:, k], score[:, k], inv[:], ALU.mult))
            st.did(dve.tensor_tensor(picked[:], chosen[:, 0], chosen[:, 1], ALU.add))
            st.all_done()
            for k in range(TOPK):
                st.did(dve.tensor_tensor(shares[:, k], chosen[:, k], over_experts(share[:, k]), ALU.mult))
            st.did(dve.tensor_reduce(sums[:, 0], picked[:].rearrange("p t e -> p e t"), AX.X, ALU.add))
            st.all_done()
            st.did(dve.tensor_tensor(shared_sum[:], shares[:, 0], shares[:, 1], ALU.add))
            st.all_done()
            st.did(dve.tensor_reduce(sums[:, 1], shared_sum[:].rearrange("p t e -> p e t"), AX.X, ALU.add))
            after["sums"] = st.n
            dve.wait_ge(summed, 1)
            st.did(dve.tensor_scalar(count[:], pS[:, 0:NX], 1.0, None, ALU.max))
            st.all_done()
            st.did(dve.reciprocal(inv_count[:], count[:]))
            st.all_done()
            st.did(dve.tensor_tensor(mean[:], pS[:, NX:2 * NX], inv_count[:], ALU.mult))
            st.all_done()
            st.did(dve.tensor_tensor(s["weight"][:], picked[:], over_tiles(mean[:]), ALU.mult))

        @block.scalar
        def _(act):
            act.wait_ge(dve_step, after["top"])
            for k in range(TOPK):
                act.activation(score[:, k], top[:, :, k], ACT.Sigmoid).then_inc(scored, 1)

        @block.tensor
        def _(pe):
            pe.wait_ge(ones_ready, 1)
            pe.wait_ge(dve_step, after["sums"])
            pe.matmul(pS[:], ones[:], sums[:].rearrange("p a e -> p (a e)"), start=True, stop=True).then_inc(summed, 1)


def layer1(nc, d, s):
    with ExitStack() as ctx:
        def sb(name, shape, dt=F32):
            return ctx.enter_context(nc.sbuf_tensor("l1_" + name, shape, dt))

        def pb(name, shape, dt=F32):
            return ctx.enter_context(nc.psum_tensor("l1_" + name, shape, dt))

        def sem(name):
            return ctx.enter_context(nc.semaphore("l1_" + name))

        ident = s["ident"]
        MLPS = NX + SI // I1
        ORDER = list(range(NX, MLPS)) + list(range(NX))
        ADDS = MLPS - 1
        PD = TPC // 2
        ZW = H * NPAT
        MIX, SCORE = 1, 6
        SORTED = 9
        seg = sb("seg", [P, TPC * ZW])
        inv_k = sb("inv_k", [P, NPAT])
        xT = s["attn"][:].rearrange("p t e -> p (t e)").rearrange("p (k n) -> p k n", k=EC)
        xT_score = sb("xT_score", [P, EC, TPC, P])
        weight = [sb(f"weight{u}", [P, TPC, NX]) for u in range(2)]
        act_g = [sb(f"act_g{i}", [P, CH]) for i in range(2)]
        h = [sb(f"h{i}", [P, CH]) for i in range(2)]
        hT = [[sb(f"hT{i}{a}", [P, CH], F32R) for a in range(2)] for i in range(2)]
        scaled = [sb(f"scaled{i}", [P, TPC, E]) for i in range(2)]
        sumy = [sb(f"sumy{u}", [P, TPC, E]) for u in range(2)]
        z = [sb(f"z{u}", [P, TPC, ZW]) for u in range(2)]
        order = [sb(f"order{i}", [P, TPC * ZW]) for i in range(2)]
        tau = sb("tau", [P, TPC * H])
        over = sb("over", [P, TPC, ZW])
        wT = [sb(f"wT{i}", [P, 4, P]) for i in range(2)]

        pG = [pb(f"G{i}", [P, CH]) for i in range(2)]
        pU = [pb(f"U{i}", [P, CH]) for i in range(2)]
        pD = [pb(f"D{i}", [P, 2, E]) for i in range(PD)]
        pZ = pb("Z", [P, ZW])
        pO = pb("O", [P, E])

        consts_in = sem("consts_in")
        xT_in = s["xT_in"]
        score_cols = sem("score_cols")
        base_in = [sem(f"base_in{u}") for u in range(2)]
        weight_ready = sem("weight_ready")
        gate_made = sem("gate_made")
        up_made = sem("up_made")
        act_ready = sem("act_ready")
        h_ready = sem("h_ready")
        h_high = sem("h_high")
        h_low = sem("h_low")
        down_made = sem("down_made")
        scale_step = sem("scale_step")
        sum_step = sem("sum_step")
        z_made = sem("z_made")
        z_ready = sem("z_ready")
        sort_step = sem("sort_step")
        over_ready = sem("over_ready")
        wts_ready = sem("wts_ready")
        wT_made = sem("wT_made")
        wT_ready = sem("wT_ready")
        ao_made = sem("ao_made")
        ao_ready = sem("ao_ready")
        stored = [sem(f"stored{u}") for u in range(2)]

        STAGES = []
        size = 2
        while size <= NPAT:
            STAGES.append((size, 0))
            dist = size // 4
            while dist:
                STAGES.append((2 * dist, dist))
                dist //= 2
            size *= 2
        SORTS = 2 * len(STAGES)
        SORT_STEPS = SORTS + 3
        ITEMS = len(STAGES) + 3
        partial = d["partial"].rearrange("(c t p) e -> c p t e", t=TPC, p=P)
        xb_rows = d["x1b"].rearrange("(c t p) e -> c p t e", t=TPC, p=P)

        def wait(eng, sm, v):
            if not isinstance(v, int) or v > 0:
                eng.wait_ge(sm, v)

        def one(ap, c):
            return ap[bass.ds(c, 1)].rearrange("o p t e -> (o p) t e")

        def rounds(eng, chunk):
            for c in range(2):
                chunk(c, c, 2)
            with eng.Fori(1, NCH // 2 - 1) as j:
                for u in range(2):
                    chunk(2 * j + u, u, 2)
            chunk(NCH - 2, 0, 1)
            chunk(NCH - 1, 1, 0)

        def first(c):
            return isinstance(c, int) and c == 0

        def buffer(u, i):
            return scaled[(ADDS * u + i - 1) % 2]

        block = ctx.enter_context(nc.Block())

        @block.sync
        def _(sp):
            sp.dma_start(seg[:], d["c_seg"]).then_inc(consts_in, 16)
            sp.dma_start(inv_k[:], d["c_inv_k"]).then_inc(consts_in, 16)

            def load(c, u):
                wait(sp, stored[u], 16 * (c // 2))
                sp.dma_start(sumy[u][:], one(xb_rows, c)).then_inc(base_in[u], 16)

            def chunk(c, u, behind):
                if behind:
                    load(c + 1, 1 - u)
                sp.wait_ge(sum_step, ADDS * (c + 1))
                sp.dma_start(one(partial, c), sumy[u][:]).then_inc(stored[u], 16)

            load(0, 0)
            rounds(sp, chunk)
            for u in range(2):
                sp.wait_ge(stored[u], 16 * (NCH // 2))

        @block.gpsimd
        def _(pool):
            def above(c, u):
                pool.wait_ge(sort_step, SORT_STEPS * (c + 1))
                wait(pool, wT_made, TPC * c)
                zv = z[u][:].rearrange("p t (h n) -> p (t h) n", n=NPAT)
                ov = over[:].rearrange("p t (h n) -> p (t h) n", n=NPAT)
                pool.tensor_tensor(ov, zv, tau[:].unsqueeze(2).to_broadcast([P, TPC * H, NPAT]),
                                   ALU.subtract).then_inc(over_ready, 1)

            def columns(c, k):
                wait(pool, z_made, TPC * c)
                cols = xT[:, :, bass.ds(c // NQ * S, S)].rearrange("p k (r j) -> p k j r", j=QT)
                pool.tensor_copy(xT_score[:, k], cols[:, k, bass.ds(c % NQ * TPC, TPC), :]).then_inc(score_cols, 1)

            def low(c, i):
                pool.wait_ge(h_high, MLPS * c + i + 1)
                pool.tensor_tensor(hT[i % 2][1][:], h[i % 2][:], hT[i % 2][0][:].bitcast(F32),
                                   ALU.subtract).then_inc(h_low, 1)

            def add(c, u, i):
                n = ADDS * c + i - 1
                if i == 1:
                    pool.wait_ge(base_in[u], 16 * (c // 2 + 1))
                pool.wait_ge(scale_step, 2 * PD * (n + 1))
                wait(pool, sum_step, n)
                pool.tensor_tensor(sumy[u][:], sumy[u][:], buffer(u, i)[:], ALU.add).then_inc(sum_step, 1)

            def chunk(c, u, behind):
                wait(pool, sum_step, ADDS * (c - 1))
                pool.tensor_copy(weight[u][:], s["weight"][:, bass.ds(c * TPC, TPC), :]).then_inc(weight_ready, 1)
                for i in range(MLPS):
                    low(c, i)
                    if 1 <= i <= EC and behind:
                        columns(c + 1, i - 1)
                    if i == SORTED:
                        above(c, u)
                    if i > 1:
                        add(c, u, i - 1)
                add(c, u, MLPS - 1)

            pool.wait_ge(xT_in[0], 16)
            for k in range(EC):
                columns(0, k)
            pool.wait_ge(xT_in[1], 16)
            rounds(pool, chunk)

        @block.tensor
        def _(pe):
            def scores(c, t):
                if t == 0:
                    pe.wait_ge(score_cols, EC * (c + 1))
                    wait(pe, wT_ready, TPC * (c - 1))
                wait(pe, z_ready, TPC * c + t)
                for k in range(EC):
                    ins = pe.matmul(pZ[:], xT_score[:, k, t, :], s["to_scores"][:, k, :],
                                    start=(k == 0), stop=(k == EC - 1))
                ins.then_inc(z_made, 1)

            def turn(c, t):
                if t == 0:
                    pe.wait_ge(wts_ready, c + 1)
                    last = isinstance(c, int) and c == NCH - 1
                    pe.wait_ge(z_ready, TPC * (NCH if last else c + 2))
                n = TPC * c + t
                wait(pe, wT_ready, n)
                for g in range(4):
                    ins = pe.transpose(pZ[:, g * P:(g + 1) * P], over[:, t, g * P:(g + 1) * P], ident[:])
                ins.then_inc(wT_made, 1)

            def mix(c, t):
                n = TPC * c + t
                pe.wait_ge(wT_ready, n + 1)
                wait(pe, ao_ready, n)
                for g in range(4):
                    ins = pe.matmul(pO[:, g * 4 * D:(g + 1) * 4 * D], wT[t % 2][:, g, :], s["values"][:, g, :],
                                    start=True, stop=True)
                ins.then_inc(ao_made, 1)

            def up(c, u, i):
                n, e = MLPS * c + i, ORDER[i]
                wait(pe, act_ready, n - 1)
                for k in range(EC):
                    ins = pe.matmul(pG[i % 2][:], s["gate_up"][:, e, k, :], xT[:, k, bass.ds(c * CH, CH)], start=(k == 0),
                                    stop=(k == EC - 1))
                ins.then_inc(gate_made, 1)
                wait(pe, h_ready, n - 1)
                for k in range(EC):
                    ins = pe.matmul(pU[i % 2][:], s["gate_up"][:, e, EC + k, :], xT[:, k, bass.ds(c * CH, CH)], start=(k == 0),
                                    stop=(k == EC - 1))
                ins.then_inc(up_made, 1)

            def down(c, i):
                if i == 0:
                    return
                halves = (0, 1) if i == 1 else (i,)
                pe.wait_ge(h_low, MLPS * c + i + 1)
                for q in range(PD):
                    n = PD * (ADDS * c + i - 1) + q
                    wait(pe, scale_step, 2 * (n - PD + 1))
                    for t in range(2):
                        cols = slice((2 * q + t) * P, (2 * q + t + 1) * P)
                        terms = [(m, *q2) for m in halves for q2 in TERMS]
                        for n2, (m, hq, wq) in enumerate(terms):
                            ins = pe.matmul(pD[q][:, t, :], hT[m % 2][hq][:, cols], s[f"down{wq}"][:, ORDER[m], :],
                                            start=(n2 == 0), stop=(n2 == len(terms) - 1))
                    ins.then_inc(down_made, 1)

            def chunk(c, u, behind):
                for i in range(MLPS):
                    mixes = MIX <= i < MIX + TPC and not first(c)
                    if mixes:
                        turn(c - 1, i - MIX)
                    up(c, u, i)
                    if mixes:
                        mix(c - 1, i - MIX)
                    if behind and SCORE <= i < SCORE + TPC:
                        scores(c + 1, i - SCORE)
                    if i:
                        down(c, i - 1)
                down(c, MLPS - 1)

            pe.wait_ge(xT_in[0], 16)
            for t in range(TPC):
                scores(0, t)
            pe.wait_ge(xT_in[1], 16)
            rounds(pe, chunk)
            for t in range(TPC):
                turn(NCH - 1, t)
                mix(NCH - 1, t)

        @block.scalar
        def _(act):
            def turned(c, t):
                n = TPC * c + t
                act.wait_ge(wT_made, n + 1)
                wait(act, ao_made, n - 1)
                act.copy(wT[t % 2][:].rearrange("p g n -> p (g n)"), pZ[:]).then_inc(wT_ready, 1)

            def mixed(c, t):
                n = TPC * c + t
                act.wait_ge(ao_made, n + 1)
                dst = s["mixed"][:, bass.ds(n, 1), :].rearrange("p o n -> p (o n)")
                act.copy(dst, pO[:]).then_inc(ao_ready, 1)

            def high(c, i):
                n = MLPS * c + i
                act.wait_ge(h_ready, n + 1)
                used = ADDS * c + (max(1, i - 2) if i >= 2 else i - 1)
                wait(act, down_made, PD * used)
                act.copy(hT[i % 2][0][:], h[i % 2][:]).then_inc(h_high, 1)

            def relu(c):
                act.wait_ge(over_ready, c + 1)
                wait(act, wT_made, TPC * c)
                act.activation(over[:], over[:], ACT.Relu).then_inc(wts_ready, 1)

            def scale(c, u, i):
                for q in range(PD):
                    n = ADDS * c + i - 1
                    act.wait_ge(down_made, PD * n + q + 1)
                    if q == 0:
                        wait(act, sum_step, n - 1)
                    if i == 1:
                        act.copy(buffer(u, i)[:, 2 * q:2 * q + 2, :], pD[q][:]).then_inc(scale_step, 2)
                        continue
                    if i == 2 and q == 0:
                        act.wait_ge(weight_ready, c + 1)
                    for t in range(2):
                        tt = 2 * q + t
                        act.activation(buffer(u, i)[:, tt, :], pD[q][:, t, :], ACT.Copy,
                                       scale=weight[u][:, tt, ORDER[i]:ORDER[i] + 1]).then_inc(scale_step, 1)

            def chunk(c, u, behind):
                for i in range(MLPS):
                    n = MLPS * c + i
                    if MIX <= i < MIX + TPC and not first(c):
                        turned(c - 1, i - MIX)
                    act.wait_ge(gate_made, n + 1)
                    wait(act, h_ready, n - 1)
                    act.activation(act_g[i % 2][:], pG[i % 2][:], ACT.Silu).then_inc(act_ready, 1)
                    if MIX <= i < MIX + TPC and not first(c):
                        mixed(c - 1, i - MIX)
                    high(c, i)
                    if i > 1:
                        scale(c, u, i - 1)
                scale(c, u, MLPS - 1)
                relu(c)

            rounds(act, chunk)
            for t in range(TPC):
                turned(NCH - 1, t)
                mixed(NCH - 1, t)

        @block.vector
        def _(dve):
            dve.wait_ge(consts_in, 32)

            def keep_scores(c, u, t):
                dve.wait_ge(z_made, TPC * c + t + 1)
                if t == 0:
                    wait(dve, over_ready, c - 1)
                dve.tensor_tensor(z[u][:, t, :], pZ[:], s["score_bias"][:], ALU.add).then_inc(z_ready, 1)

            def sort(c, u, k):
                size, dist = STAGES[k]
                first = SORT_STEPS * c + 2 * k
                src = z[u][:].rearrange("p t n -> p (t n)") if k == 0 else order[(k - 1) % 2][:]
                sv = src.rearrange("p (b n) -> p b n", n=size)
                dv = order[k % 2][:].rearrange("p (b n) -> p b n", n=size)
                half = size // 2
                low, high = sv[:, :, 0:half], sv[:, :, half:size]
                if dist or half == 1:
                    low_m, high_m = low, high
                else:
                    low_m, high_m = sv[:, :, half - 1::-1], sv[:, :, size - 1:half - 1:-1]
                if k == 0:
                    dve.wait_ge(z_ready, TPC * c + TPC)
                wait(dve, sort_step, first)
                dve.tensor_tensor(dv[:, :, 0:half], low, high_m, ALU.max).then_inc(sort_step, 1)
                dve.tensor_tensor(dv[:, :, half:size], high, low_m, ALU.min).then_inc(sort_step, 1)

            def threshold(c, step):
                done = SORT_STEPS * c + SORTS
                top = order[(len(STAGES) - 1) % 2]
                run = order[len(STAGES) % 2]
                run_v, top_v = (a[:].rearrange("p (b n) -> p b n", n=NPAT) for a in (run, top))
                dve.wait_ge(sort_step, done + step)
                if step == 0:
                    dve.tensor_tensor_scan(run[:], seg[:], top[:], 0.0, ALU.mult, ALU.add).then_inc(sort_step, 1)
                elif step == 1:
                    over_k = inv_k[:].unsqueeze(1).to_broadcast([P, TPC * H, NPAT])
                    dve.scalar_tensor_tensor(top_v, run_v, -1.0, over_k, ALU.add, ALU.mult).then_inc(sort_step, 1)
                else:
                    wait(dve, over_ready, c)
                    dve.tensor_reduce(tau[:], top_v, AX.X, ALU.max).then_inc(sort_step, 1)

            def hidden(c, i):
                n = MLPS * c + i
                dve.wait_ge(act_ready, n + 1)
                dve.wait_ge(up_made, n + 1)
                wait(dve, h_low, n - 1)
                dve.tensor_tensor(h[i % 2][:], act_g[i % 2][:], pU[i % 2][:], ALU.mult).then_inc(h_ready, 1)

            def chunk(c, u, behind):
                for i in range(MLPS):
                    hidden(c, i)
                    for k in range(min(ITEMS, ITEMS * i // SORTED), min(ITEMS, ITEMS * (i + 1) // SORTED)):
                        if k < len(STAGES):
                            sort(c, u, k)
                        else:
                            threshold(c, k - len(STAGES))
                    if behind and SCORE <= i < SCORE + TPC:
                        keep_scores(c + 1, 1 - u, i - SCORE)

            for t in range(TPC):
                keep_scores(0, 0, t)
            rounds(dve, chunk)


def finish(nc, d, s):
    with ExitStack() as ctx:
        def sb(name, shape, dt=F32):
            return ctx.enter_context(nc.sbuf_tensor("fi_" + name, shape, dt))

        def pb(name, shape, dt=F32):
            return ctx.enter_context(nc.psum_tensor("fi_" + name, shape, dt))

        def sem(name):
            return ctx.enter_context(nc.semaphore("fi_" + name))

        ident = s["ident"]
        wo = sb("wo", [P, EC, E])
        head = [sb(f"head{u}", [P, 2, E]) for u in range(2)]
        part = [sb(f"part{u}", [P, 2, E]) for u in range(2)]
        hT = [sb(f"hT{u}", [P, EC, 2 * P]) for u in range(2)]
        res = [sb(f"res{u}", [P, 2, E]) for u in range(2)]
        pT = [pb(f"T{u}", [P, EC, 2 * P]) for u in range(2)]
        pO = [pb(f"O{u}", [P, 2, E]) for u in range(2)]
        wo_in = sem("wo_in")
        part_in = [sem(f"part_in{u}") for u in range(2)]
        head_ready = sem("head_ready")
        hT_made = sem("hT_made")
        hT_ready = sem("hT_ready")
        o_made = sem("o_made")
        res_ready = sem("res_ready")
        stored = [sem(f"stored{u}") for u in range(2)]
        STEPS = TILES // 2
        ROUNDS = STEPS // 2
        part_rows = d["partial"].rearrange("(t w p) e -> t p w e", p=P, w=2)
        out_rows = d["out"].rearrange("b (t w p) e -> (b t) p w e", p=P, w=2)

        def wait(eng, sm, v):
            if not isinstance(v, int) or v > 0:
                eng.wait_ge(sm, v)

        def one(ap, t):
            return ap[bass.ds(t, 1)].rearrange("o p w e -> (o p) w e")

        block = ctx.enter_context(nc.Block())

        @block.sync
        def _(sp):
            sp.dma_start(wo[:], d["Wo"].rearrange("(k p) n -> p k n", p=P)).then_inc(wo_in, 16)

            def store(t, u):
                sp.wait_ge(res_ready, t + 1)
                sp.dma_start(one(out_rows, t), res[u][:]).then_inc(stored[u], 16)

            for t in range(2):
                sp.dma_start(part[t][:], one(part_rows, t)).then_inc(part_in[t], 16)
            with sp.Fori(1, ROUNDS) as j:
                for u in range(2):
                    store(2 * j + u - 2, u)
                    sp.dma_start(part[u][:], one(part_rows, 2 * j + u)).then_inc(part_in[u], 16)
            for u in range(2):
                store(STEPS - 2 + u, u)
            for u in range(2):
                sp.wait_ge(stored[u], 16 * ROUNDS)

        @block.tensor
        def _(pe):
            pe.wait_ge(wo_in, 16)

            def turn(t, u):
                pe.wait_ge(head_ready, t + 1)
                wait(pe, hT_ready, t - 1)
                for k in range(EC):
                    for w in range(2):
                        ins = pe.transpose(pT[u][:, k, w * P:(w + 1) * P], head[u][:, w, k * P:(k + 1) * P], ident[:])
                ins.then_inc(hT_made, 1)

            def project(t, u):
                pe.wait_ge(hT_ready, t + 1)
                wait(pe, res_ready, t - 1)
                for w in range(2):
                    for k in range(EC):
                        ins = pe.matmul(pO[u][:, w, :], hT[u][:, k, w * P:(w + 1) * P], wo[:, k, :],
                                        start=(k == 0), stop=(k == EC - 1))
                ins.then_inc(o_made, 1)

            turn(0, 0)
            for t in range(1, 4):
                turn(t, t % 2)
                project(t - 1, (t - 1) % 2)
            with pe.Fori(2, ROUNDS) as j:
                for u in range(2):
                    turn(2 * j + u, u)
                    project(2 * j + u - 1, 1 - u)
            project(STEPS - 1, 1)

        @block.scalar
        def _(act):
            def copy(t, u):
                act.wait_ge(hT_made, t + 1)
                wait(act, o_made, t - 1)
                act.copy(hT[u][:], pT[u][:]).then_inc(hT_ready, 1)

            for t in range(2):
                copy(t, t)
            with act.Fori(1, ROUNDS) as j:
                for u in range(2):
                    copy(2 * j + u, u)

        @block.vector
        def _(dve):
            def gather(t, u):
                wait(dve, hT_made, t - 1)
                src = s["mixed"][:, bass.ds(2 * t // H * QT, QT), bass.ds(2 * t % H * D, 2 * D)]
                dve.tensor_copy(head[u][:].rearrange("p w (j n) -> p w j n", n=D),
                                src.rearrange("p j (w n) -> p w j n", w=2)).then_inc(head_ready, 1)

            def add(t, u):
                dve.wait_ge(o_made, t + 1)
                dve.wait_ge(part_in[u], 16 * (t // 2 + 1))
                wait(dve, stored[u], 16 * (t // 2))
                dve.tensor_tensor(res[u][:], pO[u][:], part[u][:], ALU.add).then_inc(res_ready, 1)

            gather(0, 0)
            gather(1, 1)
            for t in range(2):
                gather(t + 2, t)
                add(t, t)
            with dve.Fori(1, ROUNDS - 1) as j:
                for u in range(2):
                    gather(2 * j + u + 2, u)
                    add(2 * j + u, u)
            for u in range(2):
                add(STEPS - 2 + u, u)


def build(nc, d):
    with ExitStack() as ctx:
        for name, shape, dt in (
            ("xn", [NT, E], F32), ("v", [NCH, KVH, P, TPC * VW], F32),
            ("q_parts", [PARTS, H * D, NT], BF16), ("k_parts", [PARTS, KVH * D, NT], BF16),
            ("buf", [SLOTS, E], F32), ("expert_out", [SLOTS, E], F32),
            ("x1b", [NT, E], F32), ("x1nT", [EC, P, NT], F32),
            ("partial", [NT, E], F32),
        ):
            d[name] = nc.dram_tensor(name, shape, dt, kind="Internal").ap()
        s = {}

        def keep(name, shape, dt=F32):
            s[name] = ctx.enter_context(nc.sbuf_tensor("s_" + name, shape, dt))

        keep("ident", [P, P])
        keep("logits", [P, TILES, NX])
        keep("gates", [P, TOPK, TILES])
        keep("slot_get", [P, TOPK * TILES], U32)
        keep("slot_put", [P, TOPK * TILES], U32)
        keep("attn", [P, TILES, E])
        keep("gate_up", [P, NX + SI // I1, 2 * EC, I1])
        for a in range(2):
            keep(f"down{a}", [P, NX + SI // I1, E], F32R)
        keep("route", [P, EC, NX])
        keep("to_scores", [P, EC, H * NPAT])
        keep("score_bias", [P, H * NPAT])
        keep("values", [P, 4, 4 * D])
        keep("weight", [P, TILES, NX])
        s["xT_in"] = [ctx.enter_context(nc.semaphore(f"xT_in{b}")) for b in range(B)]
        latents(nc, d, s)
        routing(nc, d, s)
        attention(nc, d, s)
        layer1_weights(nc, d, s)
        experts(nc, d, s)
        mixing(nc, d, s)
        weighting(nc, d, s)
        keep("mixed", [P, TILES, E])
        layer1(nc, d, s)
        finish(nc, d, s)


_NAMES = {
    "x": "L0_attn_x", "Wqa": "L0_attn_Wqa", "Wqb": "L0_attn_Wqb", "Wkva": "L0_attn_Wkva", "Wkvb": "L0_attn_Wkvb",
    "Wout": "L0_attn_Wout", "bout": "L0_attn_bout", "Wg": "L0_ffn_Wg", "W_in": "L0_ffn_W_in", "W_out": "L0_ffn_W_out",
    "key_param": "L1_attn_key_param", "Wq": "L1_attn_Wq", "bq": "L1_attn_bq", "Wk": "L1_attn_Wk", "bk": "L1_attn_bk",
    "Wv": "L1_attn_Wv", "bv": "L1_attn_bv", "Wo": "L1_attn_Wo", "bo": "L1_attn_bo", "gate_w": "L1_ffn_gate_w",
    "lb_bias": "L1_ffn_lb_bias", "expert_gate_w": "L1_ffn_expert_gate_w", "expert_up_w": "L1_ffn_expert_up_w",
    "expert_down_w": "L1_ffn_expert_down_w", "shared_gate_w": "L1_ffn_shared_gate_w",
    "shared_up_w": "L1_ffn_shared_up_w", "shared_down_w": "L1_ffn_shared_down_w",
}


def constants():
    import numpy as np

    f = np.float32
    at = np.arange(P)
    freq = (f(1.0) / f(10000.0) ** (np.arange(0, D, 2, dtype=f) / f(D))).astype(f)
    angle = np.outer(np.arange(S, dtype=f), freq).astype(f)[:, at % D // 2].T
    sign = np.where(at % 2 == 0, f(-1), f(1))[:, None]
    hide = np.where(at[None, :] > at[:, None], f(NEG), f(0))
    diag = (at[:, None] // D == np.arange(8)[None, :]).astype(f)
    return {
        "c_cos": np.ascontiguousarray(np.cos(angle).astype(f)),
        "c_sin": np.ascontiguousarray((np.sin(angle) * sign).astype(f)),
        "c_ident": np.eye(P, dtype=f),
        "c_iota": np.tile(np.arange(NX, dtype=f), (P, 1)),
        "c_below": (at[:, None] < at[None, :]).astype(f),
        "c_hide_q": hide,
        "c_hide_k": np.ascontiguousarray(hide.T),
        "c_diag": np.repeat(diag[:, :, None], NPAT, axis=2),
        "c_diag_v": np.repeat((at[:, None] // NPAT == np.arange(4)[None, :]).astype(f)[:, :, None], D, axis=2),
        "c_seg": np.tile((np.arange(TPC * H * NPAT) % NPAT != 0).astype(f), (P, 1)),
        "c_inv_k": np.tile((f(1) / np.arange(1, NPAT + 1, dtype=f)).astype(f), (P, 1)),
    }


def kernel(**inputs):
    import numpy as np
    import concourse.bacc as bacc
    from concourse.bass_utils import run_bass_kernel_spmd

    nc = bacc.Bacc("TRN2", target_bir_lowering=False, num_devices=1)
    arrays, d = {}, {}
    for name, a in [(n, np.ascontiguousarray(inputs[full])) for n, full in _NAMES.items()] + list(constants().items()):
        arrays["in_" + name] = a
        d[name] = nc.dram_tensor("in_" + name, a.shape, mybir.dt.from_np(a.dtype), kind="ExternalInput").ap()
    d["out"] = nc.dram_tensor("out_0", (B, S, E), F32, kind="ExternalOutput").ap()
    build(nc, d)
    r = run_bass_kernel_spmd(nc, [arrays], core_ids=[0])
    return r.results[0]["out_0"]
```
